# Optimizing a Trainium2 kernel written in Bass

```python
import numpy as np
import jax
import jax.numpy as jnp

def _softmax(x, axis=-1):
    return jax.nn.softmax(x, axis=axis)

def _gelu(x):
    return jax.nn.gelu(x, approximate=True)

def _silu(x):
    return jax.nn.silu(x)

def _sigmoid(x):
    return jax.nn.sigmoid(x)

def _layernorm(x, axis=-1, eps=1e-05):
    m = jnp.mean(x, axis=axis, keepdims=True)
    v = jnp.var(x, axis=axis, keepdims=True)
    return (x - m) / jnp.sqrt(v + eps)

def _scatter_add(tgt, idx, src, axis=0):
    return tgt.at[idx].add(src)

def _segment_sum(src, seg, n):
    return jax.ops.segment_sum(src, seg, n)
kernel_name = 'mk_decoder_preln_d2_seqx_r8_c7dfa6'

def setup_inputs(seed: int=0):
    np.random.seed(seed)
    _w = jnp.asarray

    def _rec_inputs():
        import jax
        import jax.numpy as jnp
        _rk = jax.random.key(seed)
        x = -0.0002928 + 1 * jax.random.normal(jax.random.fold_in(_rk, 1), (32, 64, 128), jnp.float32)
        _lenS = 64 - jax.random.randint(jax.random.fold_in(_rk, 7), (32,), 0, max(1, 64 // 4) + 1, jnp.int32)
        _lenS2 = 64 - jax.random.randint(jax.random.fold_in(_rk, 8), (32,), 0, max(1, 64 // 4) + 1, jnp.int32)
        _ctx_1024P = jax.random.normal(jax.random.fold_in(_rk, 11), (32, 16, 128), jnp.float32)
        _ctx_1024c = jax.random.dirichlet(jax.random.fold_in(_rk, 511), 0.3 * jnp.ones((16,), jnp.float32), (32, 64))
        _ctx_1024t = jnp.einsum('bsk,bkd->bsd', _ctx_1024c, _ctx_1024P)
        _ctx_1024t = _ctx_1024t * jax.lax.rsqrt(jnp.mean(jnp.square(_ctx_1024t)) + 1e-12) * 0.953939
        ctx_1024 = -1.39393e-06 + 0.999914 * (_ctx_1024t + 0.3 * jax.random.normal(jax.random.fold_in(_rk, 611), (32, 64, 128), jnp.float32))
        return (x, ctx_1024)
    x, ctx_1024 = _rec_inputs()

    def _L0_attn_setup():
        import jax, jax.numpy as jnp
        import numpy as np
        D_MODEL = 128
        NHEAD = 16
        HEAD_DIM = D_MODEL // NHEAD
        LN_EPS = 1e-05

        def _layer_norm(x, gamma, beta):
            mu = jnp.mean(x, axis=-1, keepdims=True)
            var = jnp.mean(jnp.square(x - mu), axis=-1, keepdims=True)
            return (x - mu) * jax.lax.rsqrt(var + LN_EPS) * gamma + beta
        key = jax.random.key(seed)
        k1, k2, k3 = jax.random.split(key, 3)
        x = jax.random.normal(k1, (2, 256, D_MODEL), dtype=jnp.float32)
        w_qkv = jax.random.normal(k2, (3 * D_MODEL, D_MODEL), dtype=jnp.float32) * (1.0 / np.sqrt(D_MODEL))
        b_qkv = jax.random.normal(k3, (3 * D_MODEL,), dtype=jnp.float32) * 0.01
        ln_gamma = jnp.ones((D_MODEL,), dtype=jnp.float32)
        ln_beta = jnp.zeros((D_MODEL,), dtype=jnp.float32)
        return {'x': x, 'w_qkv': w_qkv, 'b_qkv': b_qkv, 'ln_gamma': ln_gamma, 'ln_beta': ln_beta}
    _L0_attn_all = _L0_attn_setup()
    _L0_attn_in = {k: v for k, v in _L0_attn_all.items() if k in ('w_qkv', 'b_qkv', 'ln_gamma', 'ln_beta')}
    del _L0_attn_all

    def _L0_xattn_setup():
        import jax, jax.numpy as jnp
        import numpy as np
        D_MODEL = 128
        NUM_HEADS = 16
        NUM_KV_HEADS = 4
        D_K = D_MODEL // NUM_HEADS
        GROUP = NUM_HEADS // NUM_KV_HEADS
        D_KV = D_MODEL // GROUP
        key = jax.random.key(seed)
        ks = jax.random.split(key, 12)
        B, S = (2, 256)
        sc = 0.02
        return {'query': jax.random.normal(ks[0], (B, S, D_MODEL), jnp.float32), 'key': jax.random.normal(ks[1], (B, S, D_MODEL), jnp.float32), 'value': jax.random.normal(ks[2], (B, S, D_MODEL), jnp.float32), 'w_q': jax.random.normal(ks[3], (D_MODEL, D_MODEL), jnp.float32) * sc, 'b_q': jnp.zeros((D_MODEL,), jnp.float32), 'w_k': jax.random.normal(ks[4], (D_KV, D_MODEL), jnp.float32) * sc, 'b_k': jnp.zeros((D_KV,), jnp.float32), 'w_v': jax.random.normal(ks[5], (D_KV, D_MODEL), jnp.float32) * sc, 'b_v': jnp.zeros((D_KV,), jnp.float32), 'w_o': jax.random.normal(ks[6], (D_MODEL, D_MODEL), jnp.float32) * sc, 'b_o': jnp.zeros((D_MODEL,), jnp.float32)}
    _L0_xattn_all = _L0_xattn_setup()
    _L0_xattn_in = {k: v for k, v in _L0_xattn_all.items() if k in ('w_q', 'b_q', 'w_k', 'b_k', 'w_v', 'b_v', 'w_o', 'b_o')}
    del _L0_xattn_all

    def _L0_ffn_setup():
        import jax, jax.numpy as jnp
        import numpy as np
        H = 128
        I = 64
        E = 8
        K = 2
        SI = I * 2
        B, S = (2, 128)

        def _mlp(x, gw, uw, dw):
            return jax.nn.silu(x @ gw.T) * (x @ uw.T) @ dw.T
        key = jax.random.key(seed)
        ks = jax.random.split(key, 9)
        s = 0.02
        return {'x': jax.random.normal(ks[0], (B, S, H), jnp.float32), 'gate_w': jax.random.normal(ks[1], (E, H), jnp.float32) * s, 'lb_bias': jnp.zeros((E,), jnp.float32), 'expert_gate_w': jax.random.normal(ks[2], (E, I, H), jnp.float32) * s, 'expert_up_w': jax.random.normal(ks[3], (E, I, H), jnp.float32) * s, 'expert_down_w': jax.random.normal(ks[4], (E, H, I), jnp.float32) * s, 'shared_gate_w': jax.random.normal(ks[5], (SI, H), jnp.float32) * s, 'shared_up_w': jax.random.normal(ks[6], (SI, H), jnp.float32) * s, 'shared_down_w': jax.random.normal(ks[7], (H, SI), jnp.float32) * s}
    _L0_ffn_all = _L0_ffn_setup()
    _L0_ffn_in = {k: v for k, v in _L0_ffn_all.items() if k in ('gate_w', 'lb_bias', 'expert_gate_w', 'expert_up_w', 'expert_down_w', 'shared_gate_w', 'shared_up_w', 'shared_down_w')}
    del _L0_ffn_all

    def _L1_attn_setup():
        import jax, jax.numpy as jnp
        import numpy as np
        D = 128
        H = 16
        DH = D // H
        B, N = (4, 128)
        key = jax.random.key(seed)
        k0, k1, k2 = jax.random.split(key, 3)
        x = jax.random.normal(k0, (B, N, D), jnp.float32)
        Wkqv = jax.random.normal(k1, (H, D, 2 * D + DH), jnp.float32) * 0.02
        bkqv = jnp.zeros((H, 2 * D + DH), jnp.float32)
        Wp = jax.random.normal(k2, (D, D), jnp.float32) * 0.02
        bp = jnp.zeros((D,), jnp.float32)
        return {'x': x, 'Wkqv': Wkqv, 'bkqv': bkqv, 'Wp': Wp, 'bp': bp}
    _L1_attn_all = _L1_attn_setup()
    _L1_attn_in = {k: v for k, v in _L1_attn_all.items() if k in ('Wkqv', 'bkqv', 'Wp', 'bp')}
    del _L1_attn_all

    def _L1_xattn_setup():
        import jax, jax.numpy as jnp
        import numpy as np
        import math
        B, S, D, H = (1, 256, 128, 16)
        DK = D // H
        DH = 64
        LOG_T_MIN = math.log(0.1)
        LOG_T_MAX = math.log(10.0)

        def _linear(x, W, b):
            return x @ W.T + b
        key = jax.random.key(seed)
        ks = jax.random.split(key, 20)
        p = 0.02
        return {'query': jax.random.normal(ks[0], (B, S, D), jnp.float32), 'key': jax.random.normal(ks[1], (B, S, D), jnp.float32), 'value': jax.random.normal(ks[2], (B, S, D), jnp.float32), 'Wq': jax.random.normal(ks[3], (D, D), jnp.float32) * p, 'bq': jax.random.normal(ks[4], (D,), jnp.float32) * p, 'Wk': jax.random.normal(ks[5], (D, D), jnp.float32) * p, 'bk': jax.random.normal(ks[6], (D,), jnp.float32) * p, 'Wv': jax.random.normal(ks[7], (D, D), jnp.float32) * p, 'bv': jax.random.normal(ks[8], (D,), jnp.float32) * p, 'Wo': jax.random.normal(ks[9], (D, D), jnp.float32) * p, 'bo': jax.random.normal(ks[10], (D,), jnp.float32) * p, 'w1': jax.random.normal(ks[11], (DH, 3), jnp.float32) * 0.3, 'b1': jax.random.normal(ks[12], (DH,), jnp.float32) * 0.1, 'w2': jax.random.normal(ks[13], (DH, DH), jnp.float32) * 0.1, 'b2': jax.random.normal(ks[14], (DH,), jnp.float32) * 0.1, 'w3': jax.random.normal(ks[15], (1, DH), jnp.float32) * 0.1, 'b3': jnp.full((1,), (LOG_T_MIN + LOG_T_MAX) / 2, jnp.float32)}
    _L1_xattn_all = _L1_xattn_setup()
    _L1_xattn_in = {k: v for k, v in _L1_xattn_all.items() if k in ('Wq', 'bq', 'Wk', 'bk', 'Wv', 'bv', 'Wo', 'bo', 'w1', 'b1', 'w2', 'b2', 'w3', 'b3')}
    del _L1_xattn_all

    def _L1_ffn_setup():
        import jax, jax.numpy as jnp
        import numpy as np
        B, S, D_MODEL, D_HIDDEN = (4, 256, 128, 512)

        def act_quant(x):
            scale = 127.0 / jnp.clip(jnp.max(jnp.abs(x), axis=-1, keepdims=True), 1e-05)
            return jnp.clip(jnp.round(x * scale), -128, 127) / scale

        def weight_quant(w):
            scale = 1.0 / jnp.clip(jnp.mean(jnp.abs(w)), 1e-05)
            return jnp.clip(jnp.round(w * scale), -1, 1) / scale

        def bit_linear(x, w):
            xq = x + jax.lax.stop_gradient(act_quant(x) - x)
            wq = w + jax.lax.stop_gradient(weight_quant(w) - w)
            return jnp.einsum('bsd,hd->bsh', xq, wq)

        def depthwise_conv1d(x_bcl, w, b):
            y = jax.lax.conv_general_dilated(x_bcl, w, window_strides=(1,), padding=[(1, 1)], dimension_numbers=('NCH', 'OIH', 'NCH'), feature_group_count=x_bcl.shape[1])
            return y + b[None, :, None]
        key = jax.random.key(seed)
        ks = jax.random.split(key, 5)
        lim1 = 1.0 / np.sqrt(D_MODEL)
        lim2 = 1.0 / np.sqrt(D_HIDDEN)
        limc = 1.0 / np.sqrt(3.0)
        return {'x': jax.random.normal(ks[0], (B, S, D_MODEL), dtype=jnp.float32), 'w1': jax.random.uniform(ks[1], (D_HIDDEN, D_MODEL), jnp.float32, -lim1, lim1), 'conv_w': jax.random.uniform(ks[2], (D_HIDDEN, 1, 3), jnp.float32, -limc, limc), 'conv_b': jax.random.uniform(ks[3], (D_HIDDEN,), jnp.float32, -limc, limc), 'w2': jax.random.uniform(ks[4], (D_MODEL, D_HIDDEN), jnp.float32, -lim2, lim2)}
    _L1_ffn_all = _L1_ffn_setup()
    _L1_ffn_in = {k: v for k, v in _L1_ffn_all.items() if k in ('w1', 'conv_w', 'conv_b', 'w2')}
    del _L1_ffn_all
    return {'x': x, 'ctx_1024': ctx_1024, 'L0_attn_w_qkv': _L0_attn_in['w_qkv'], 'L0_attn_b_qkv': _L0_attn_in['b_qkv'], 'L0_attn_ln_gamma': _L0_attn_in['ln_gamma'], 'L0_attn_ln_beta': _L0_attn_in['ln_beta'], 'L0_xattn_w_q': _L0_xattn_in['w_q'], 'L0_xattn_b_q': _L0_xattn_in['b_q'], 'L0_xattn_w_k': _L0_xattn_in['w_k'], 'L0_xattn_b_k': _L0_xattn_in['b_k'], 'L0_xattn_w_v': _L0_xattn_in['w_v'], 'L0_xattn_b_v': _L0_xattn_in['b_v'], 'L0_xattn_w_o': _L0_xattn_in['w_o'], 'L0_xattn_b_o': _L0_xattn_in['b_o'], 'L0_ffn_gate_w': _L0_ffn_in['gate_w'], 'L0_ffn_lb_bias': _L0_ffn_in['lb_bias'], 'L0_ffn_expert_gate_w': _L0_ffn_in['expert_gate_w'], 'L0_ffn_expert_up_w': _L0_ffn_in['expert_up_w'], 'L0_ffn_expert_down_w': _L0_ffn_in['expert_down_w'], 'L0_ffn_shared_gate_w': _L0_ffn_in['shared_gate_w'], 'L0_ffn_shared_up_w': _L0_ffn_in['shared_up_w'], 'L0_ffn_shared_down_w': _L0_ffn_in['shared_down_w'], 'L1_attn_Wkqv': _L1_attn_in['Wkqv'], 'L1_attn_bkqv': _L1_attn_in['bkqv'], 'L1_attn_Wp': _L1_attn_in['Wp'], 'L1_attn_bp': _L1_attn_in['bp'], 'L1_xattn_Wq': _L1_xattn_in['Wq'], 'L1_xattn_bq': _L1_xattn_in['bq'], 'L1_xattn_Wk': _L1_xattn_in['Wk'], 'L1_xattn_bk': _L1_xattn_in['bk'], 'L1_xattn_Wv': _L1_xattn_in['Wv'], 'L1_xattn_bv': _L1_xattn_in['bv'], 'L1_xattn_Wo': _L1_xattn_in['Wo'], 'L1_xattn_bo': _L1_xattn_in['bo'], 'L1_xattn_w1': _L1_xattn_in['w1'], 'L1_xattn_b1': _L1_xattn_in['b1'], 'L1_xattn_w2': _L1_xattn_in['w2'], 'L1_xattn_b2': _L1_xattn_in['b2'], 'L1_xattn_w3': _L1_xattn_in['w3'], 'L1_xattn_b3': _L1_xattn_in['b3'], 'L1_ffn_w1': _L1_ffn_in['w1'], 'L1_ffn_conv_w': _L1_ffn_in['conv_w'], 'L1_ffn_conv_b': _L1_ffn_in['conv_b'], 'L1_ffn_w2': _L1_ffn_in['w2']}

def reference(x, ctx_1024, L0_attn_w_qkv, L0_attn_b_qkv, L0_attn_ln_gamma, L0_attn_ln_beta, L0_xattn_w_q, L0_xattn_b_q, L0_xattn_w_k, L0_xattn_b_k, L0_xattn_w_v, L0_xattn_b_v, L0_xattn_w_o, L0_xattn_b_o, L0_ffn_gate_w, L0_ffn_lb_bias, L0_ffn_expert_gate_w, L0_ffn_expert_up_w, L0_ffn_expert_down_w, L0_ffn_shared_gate_w, L0_ffn_shared_up_w, L0_ffn_shared_down_w, L1_attn_Wkqv, L1_attn_bkqv, L1_attn_Wp, L1_attn_bp, L1_xattn_Wq, L1_xattn_bq, L1_xattn_Wk, L1_xattn_bk, L1_xattn_Wv, L1_xattn_bv, L1_xattn_Wo, L1_xattn_bo, L1_xattn_w1, L1_xattn_b1, L1_xattn_w2, L1_xattn_b2, L1_xattn_w3, L1_xattn_b3, L1_ffn_w1, L1_ffn_conv_w, L1_ffn_conv_b, L1_ffn_w2):
    import jax
    import jax.numpy as jnp

    def _L0_attn_ref(x, w_qkv, b_qkv, ln_gamma, ln_beta):
        import jax, jax.numpy as jnp
        import numpy as np
        D_MODEL = 128
        NHEAD = 16
        HEAD_DIM = D_MODEL // NHEAD
        LN_EPS = 1e-05

        def _layer_norm(x, gamma, beta):
            mu = jnp.mean(x, axis=-1, keepdims=True)
            var = jnp.mean(jnp.square(x - mu), axis=-1, keepdims=True)
            return (x - mu) * jax.lax.rsqrt(var + LN_EPS) * gamma + beta
        B, L, _ = x.shape
        x_norm = _layer_norm(x, ln_gamma, ln_beta)
        qkv = x_norm @ w_qkv.T + b_qkv
        qkv = qkv.reshape(B, L, 3, NHEAD, HEAD_DIM)
        qkv = jnp.transpose(qkv, (2, 0, 3, 1, 4))
        q, k, v = (qkv[0], qkv[1], qkv[2])
        scale = 1.0 / np.sqrt(HEAD_DIM).astype(np.float32)
        scores = jnp.einsum('bhqd,bhkd->bhqk', q, k) * scale
        attn = jax.nn.softmax(scores, axis=-1)
        out = jnp.einsum('bhqk,bhkd->bhqd', attn, v)
        out = jnp.transpose(out, (0, 2, 1, 3)).reshape(B, L, D_MODEL)
        return out

    def _L0_xattn_ref(query, key, value, w_q, b_q, w_k, b_k, w_v, b_v, w_o, b_o):
        import jax, jax.numpy as jnp
        import numpy as np
        D_MODEL = 128
        NUM_HEADS = 16
        NUM_KV_HEADS = 4
        D_K = D_MODEL // NUM_HEADS
        GROUP = NUM_HEADS // NUM_KV_HEADS
        D_KV = D_MODEL // GROUP
        B, S, _ = query.shape
        Q = query @ w_q.T + b_q
        K = key @ w_k.T + b_k
        V = value @ w_v.T + b_v
        Q = Q.reshape(B, S, NUM_KV_HEADS, GROUP, D_K).transpose(0, 2, 3, 1, 4)
        K = K.reshape(B, S, NUM_KV_HEADS, D_K).transpose(0, 2, 1, 3)
        V = V.reshape(B, S, NUM_KV_HEADS, D_K).transpose(0, 2, 1, 3)
        scale = 1.0 / jnp.sqrt(jnp.asarray(D_K, Q.dtype))
        scores = jnp.einsum('bhgsd,bhtd->bhgst', Q, K) * scale
        attn = jax.nn.softmax(scores, axis=-1)
        out = jnp.einsum('bhgst,bhtd->bhgsd', attn, V)
        out = out.transpose(0, 3, 1, 2, 4).reshape(B, S, D_MODEL)
        return out @ w_o.T + b_o

    def _L0_ffn_ref(x, gate_w, lb_bias, expert_gate_w, expert_up_w, expert_down_w, shared_gate_w, shared_up_w, shared_down_w):
        import jax, jax.numpy as jnp
        import numpy as np
        H = 128
        I = 64
        E = 8
        K = 2
        SI = I * 2
        B, S = (2, 128)

        def _mlp(x, gw, uw, dw):
            return jax.nn.silu(x @ gw.T) * (x @ uw.T) @ dw.T
        b, s, h = x.shape
        xf = x.reshape(-1, h)
        logits = xf @ gate_w.T + lb_bias
        scores = jax.nn.sigmoid(logits.astype(jnp.float32))
        topw, topi = jax.lax.top_k(scores, K)
        topw = (topw / (topw.sum(-1, keepdims=True) + 1e-08)).astype(x.dtype)
        out = jnp.zeros_like(xf)
        for e in range(E):
            m = topi == e
            sel = m.any(axis=-1)
            cnt = m.sum()
            wmean = (topw * m).sum() / jnp.maximum(cnt, 1).astype(topw.dtype)
            y = _mlp(xf, expert_gate_w[e], expert_up_w[e], expert_down_w[e])
            out = out + jnp.where(sel[:, None], y * wmean, jnp.zeros((), x.dtype))
        out = out.reshape(b, s, h)
        out = out + _mlp(x, shared_gate_w, shared_up_w, shared_down_w)
        return out

    def _L1_attn_ref(x, Wkqv, bkqv, Wp, bp):
        import jax, jax.numpy as jnp
        import numpy as np
        D = 128
        H = 16
        DH = D // H
        B, N = (4, 128)
        Bm, Nm, Dm = x.shape
        y = jnp.einsum('bnd,hde->bhne', x, Wkqv) + bkqv[None, :, None, :]
        k = y[..., :Dm]
        q = y[..., Dm:2 * Dm]
        v = y[..., 2 * Dm:]
        A = jnp.einsum('bhnd,bhmd->bhnm', q, k) / jnp.sqrt(jnp.float32(Dm))
        mask = jnp.tril(jnp.ones((Nm, Nm), dtype=bool))
        A = jnp.where(mask[None, None], A, -jnp.inf)
        A = jax.nn.softmax(A, axis=-1)
        sa = jnp.einsum('bhnm,bhmd->bnhd', A, v).reshape(Bm, Nm, Dm)
        return sa @ Wp + bp

    def _L1_xattn_ref(query, key, value, Wq, bq, Wk, bk, Wv, bv, Wo, bo, w1, b1, w2, b2, w3, b3):
        import jax, jax.numpy as jnp
        import numpy as np
        import math
        B, S, D, H = (1, 256, 128, 16)
        DK = D // H
        DH = 64
        LOG_T_MIN = math.log(0.1)
        LOG_T_MAX = math.log(10.0)

        def _linear(x, W, b):
            return x @ W.T + b
        b, sq, d = query.shape
        sk = key.shape[1]
        h, dk = (H, DK)
        Q = _linear(query, Wq, bq).reshape(b, sq, h, dk).transpose(0, 2, 1, 3)
        K = _linear(key, Wk, bk).reshape(b, sk, h, dk).transpose(0, 2, 1, 3)
        V = _linear(value, Wv, bv).reshape(b, sk, h, dk).transpose(0, 2, 1, 3)
        qk = jnp.einsum('bhqd,bhkd->bhqk', Q, K)
        scores = qk / math.sqrt(dk)
        mean_sim = scores.mean(axis=(-2, -1))
        max_sim = scores.max(axis=-1).mean(axis=-1)
        probs = jax.nn.softmax(scores, axis=-1)
        entropy_proxy = jnp.var(probs, axis=-1, ddof=1).mean(axis=-1)
        feats = jnp.stack([mean_sim, max_sim, entropy_proxy], axis=-1)
        hidden = jax.nn.gelu(_linear(feats, w1, b1), approximate=False)
        hidden = jax.nn.gelu(_linear(hidden, w2, b2), approximate=False)
        log_t = jnp.clip(_linear(hidden, w3, b3), LOG_T_MIN, LOG_T_MAX)
        t = jnp.exp(log_t)[..., None]
        attn_scores = qk / (2.0 * t)
        attn = jax.nn.softmax(attn_scores, axis=-1)
        attn = jnp.nan_to_num(attn, nan=0.0)
        out = jnp.einsum('bhqk,bhkd->bhqd', attn, V)
        out = out.transpose(0, 2, 1, 3).reshape(b, sq, d)
        return _linear(out, Wo, bo)

    def _L1_ffn_ref(x, w1, conv_w, conv_b, w2):
        import jax, jax.numpy as jnp
        import numpy as np
        B, S, D_MODEL, D_HIDDEN = (4, 256, 128, 512)

        def act_quant(x):
            scale = 127.0 / jnp.clip(jnp.max(jnp.abs(x), axis=-1, keepdims=True), 1e-05)
            return jnp.clip(jnp.round(x * scale), -128, 127) / scale

        def weight_quant(w):
            scale = 1.0 / jnp.clip(jnp.mean(jnp.abs(w)), 1e-05)
            return jnp.clip(jnp.round(w * scale), -1, 1) / scale

        def bit_linear(x, w):
            xq = x + jax.lax.stop_gradient(act_quant(x) - x)
            wq = w + jax.lax.stop_gradient(weight_quant(w) - w)
            return jnp.einsum('bsd,hd->bsh', xq, wq)

        def depthwise_conv1d(x_bcl, w, b):
            y = jax.lax.conv_general_dilated(x_bcl, w, window_strides=(1,), padding=[(1, 1)], dimension_numbers=('NCH', 'OIH', 'NCH'), feature_group_count=x_bcl.shape[1])
            return y + b[None, :, None]
        h = bit_linear(x, w1)
        h = depthwise_conv1d(h.transpose(0, 2, 1), conv_w, conv_b)
        h = h.transpose(0, 2, 1)
        h = jax.nn.silu(h)
        return bit_linear(h, w2)
    x = x + _L0_attn_ref(_layernorm(x, axis=-1), L0_attn_w_qkv, L0_attn_b_qkv, L0_attn_ln_gamma, L0_attn_ln_beta)
    x = x + _L0_xattn_ref(_layernorm(x, axis=-1), ctx_1024, ctx_1024, L0_xattn_w_q, L0_xattn_b_q, L0_xattn_w_k, L0_xattn_b_k, L0_xattn_w_v, L0_xattn_b_v, L0_xattn_w_o, L0_xattn_b_o)
    x = x + _L0_ffn_ref(_layernorm(x, axis=-1), L0_ffn_gate_w, L0_ffn_lb_bias, L0_ffn_expert_gate_w, L0_ffn_expert_up_w, L0_ffn_expert_down_w, L0_ffn_shared_gate_w, L0_ffn_shared_up_w, L0_ffn_shared_down_w)
    x = x + _L1_attn_ref(_layernorm(x, axis=-1), L1_attn_Wkqv, L1_attn_bkqv, L1_attn_Wp, L1_attn_bp)
    x = x + _L1_xattn_ref(_layernorm(x, axis=-1), ctx_1024, ctx_1024, L1_xattn_Wq, L1_xattn_bq, L1_xattn_Wk, L1_xattn_bk, L1_xattn_Wv, L1_xattn_bv, L1_xattn_Wo, L1_xattn_bo, L1_xattn_w1, L1_xattn_b1, L1_xattn_w2, L1_xattn_b2, L1_xattn_w3, L1_xattn_b3)
    x = x + _L1_ffn_ref(_layernorm(x, axis=-1), L1_ffn_w1, L1_ffn_conv_w, L1_ffn_conv_b, L1_ffn_w2)
    return x

_drawn_inputs = setup_inputs


def setup_inputs(seed=0):
    import zlib

    import numpy as np

    out = dict(_drawn_inputs(seed))
    spreads = {'L0_attn_ln_gamma': (1.0, 0.2),
     'L0_attn_ln_beta': (0.0, 0.1),
     'L0_xattn_b_q': (0.0, 0.8),
     'L0_xattn_b_k': (0.0, 2.0),
     'L0_xattn_b_v': (0.0, 0.426),
     'L0_xattn_b_o': (0.0, 0.1),
     'L0_ffn_lb_bias': (0.0, 0.8),
     'L1_attn_bkqv': (0.0, 1.73),
     'L1_attn_bp': (0.0, 0.34)}
    factors = {'L0_attn_b_qkv': 5.312,
     'L0_xattn_w_q': 8.0,
     'L0_xattn_w_k': 8.0,
     'L0_ffn_gate_w': 8.0,
     'L0_ffn_expert_gate_w': 8.0,
     'L0_ffn_expert_up_w': 8.0,
     'L0_ffn_expert_down_w': 8.0,
     'L0_ffn_shared_gate_w': 8.0,
     'L0_ffn_shared_up_w': 8.0,
     'L0_ffn_shared_down_w': 8.0,
     'L1_attn_Wkqv': 14.597,
     'L1_xattn_Wq': 40.588,
     'L1_xattn_bq': 64.0,
     'L1_xattn_Wk': 39.77,
     'L1_xattn_bk': 64.0,
     'L1_xattn_bv': 49.131,
     'L1_xattn_w1': 64.0,
     'L1_xattn_b1': 8.0,
     'L1_xattn_w2': 8.0,
     'L1_xattn_b2': 8.0,
     'L1_xattn_w3': 8.0,
     'L1_xattn_Wv': 4.359,
     'L1_xattn_Wo': 3.653,
     'L1_xattn_bo': 8.0,
     'L1_ffn_w1': 4.49,
     'L1_ffn_conv_w': 4.325,
     'L1_ffn_conv_b': 3.458,
     'L1_ffn_w2': 2.793}
    for name, (base, spread) in spreads.items():
        noise = np.random.default_rng([zlib.crc32(name.encode()), seed]).standard_normal(out[name].shape)
        drawn = base * np.exp(spread * noise) if base else spread * noise
        out[name] = jnp.asarray(drawn.astype(out[name].dtype))
    for name, factor in factors.items():
        out[name] = (out[name] * factor).astype(out[name].dtype)
    return out
```

```python
from collections import namedtuple
from contextlib import ExitStack

import numpy as np

import concourse.bass as bass
from concourse import mybir

F32 = mybir.dt.float32
BF16 = mybir.dt.bfloat16
I32 = mybir.dt.int32
ALU = mybir.AluOpType
ACT = mybir.ActivationFunctionType
AX = mybir.AxisListType

B, S, D = 32, 64, 128
H, DH = 16, 8
P = 128
TILES = B * S // P
PAIRS = TILES // 2
TOK = 2 * P
PB = TOK // S
G = 4
HG = H // G
UNIT = 2 * HG * S
VW = DH + 1
E8, FI = 8, 64
FC = 5
EPS = 1e-5
HID = 512
HC = HID // P
MLP = 64
ROUND = 1.5 * 2.0 ** 23

PACKS = {
    "A": [("ident", P), ("headmask", HG), ("A_wq", D), ("A_wk", D), ("A_wv", D),
          ("A_bq", 1), ("A_bk", 1), ("A_bv", D), ("gamma", 1), ("beta", 1)],
    "B": [("B_wq", D), ("B_wk", D), ("B_wv", D), ("B_bq", 1), ("B_bk", 1), ("B_bv", D), ("B_wo", D), ("B_bo", D)],
    "C": [("C_gate", E8), ("C_lb", E8), ("C_wg", FC * P), ("C_wu", FC * P), ("C_wd", FC * D),
          ("C_first", E8), ("C_sel", 4 * P)],
    "D": [("D_wq", H * D), ("D_wk", H * D), ("D_wv", D), ("D_bq", H), ("D_bk", H), ("D_bv", D),
          ("D_wo", D), ("D_bo", D), ("D_causal", S)],
    "E": [("E_wq", D), ("E_wk", D), ("E_wv", D), ("E_bq", 1), ("E_bk", 1), ("E_bv", D), ("E_wo", D), ("E_bo", D),
          ("E_w1", MLP), ("E_b1", 1), ("E_w2", MLP), ("E_b2", 1), ("E_w3", 64), ("E_b3", 1),
          ("E_headblk", H), ("E_featsel", 18)],
    "F": [("F_w1", HID), ("F_cw", 3 * HID), ("F_cb", HID), ("F_w2", HC * D)],
}


def named(things):
    return namedtuple("Named", list(things))(*things.values())


class Signal:

    def __init__(self, sem, base=0):
        self.sem, self.base = sem, base

    def at(self, n):
        return self.base + (max(n, 0) if isinstance(n, int) else n)


def offsets():
    at, width = {}, {}
    for pack, parts in PACKS.items():
        n = 0
        for name, w in parts:
            at[name] = (pack, n, w)
            n += w
        width[pack] = n
    return at, width


STAGES = "ABCDEF"


def build(nc, x_in, ctx_in, packs_in, out):
    at, width = offsets()
    with ExitStack() as ctx:
        def sb(name, shape, dt=F32):
            return ctx.enter_context(nc.sbuf_tensor(name, shape, dt))

        def sems(stage, names):
            return named({n: Signal(ctx.enter_context(nc.semaphore(f"{stage}_{n}"))) for n in names.split()})

        shared, counted = {}, {}

        def signals(per_pair, prefix=""):
            out = {}
            for item in per_pair.split():
                name, n = item.split(":")
                name = prefix + name
                if name not in shared:
                    shared[name], counted[name] = ctx.enter_context(nc.semaphore(name)), 0
                out[name] = Signal(shared[name], counted[name])
                counted[name] += int(n) * PAIRS
            return named({name[len(prefix):]: signal for name, signal in out.items()})

        def bc(ap, axis, n):
            a = ap.unsqueeze(axis)
            shape = list(a.shape)
            shape[axis] = n
            return a.broadcast_to(shape)

        wt = {p: sb(f"w_{p}", [P, n]) for p, n in width.items() if p in STAGES}

        def w(name, rows=P):
            pack, o, n = at[name]
            return wt[pack][0:rows, o:o + n]

        x = sb("x", [P, TILES, D])
        ones = sb("ones", [P, P])
        xm = sb("xm", [P, 2, D])
        xn = sb("xn", [P, 2, D])
        stats = sb("stats", [P, 2, 6])
        carrier = sb("carrier", [P, 1])
        mv = sb("mv", [P, 2, 2])
        vareps = sb("vareps", [P, 2, 1])
        rstd = sb("rstd", [P, 2, 1])
        minus_half = sb("minus_half", [P, 2, 1])
        xT = sb("xT", [P, TOK])
        cT = sb("cT", [P, TOK])
        qT = sb("qT", [P, TOK])
        kx = sb("kx", [P, HG, TOK])
        vbd = sb("vbd", [P, PB, H // 2, 2, VW])
        rowmax = sb("rowmax", [P, G, 2, HG])
        shifted = sb("shifted", [P, G, UNIT])
        probs = sb("probs", [P, G, UNIT])
        probsT = sb("probsT", [P, 2, 4, P])
        rsum = sb("rsum", [P, 2, H])
        heads = sb("heads", [P, 2, D])
        headsT = sb("headsT", [P, TOK])

        zeros = sb("zeros", [P, 2, D])
        isnan = sb("isnan", [P, 2, D], I32)
        qh = sb("qh", [P, 2, TOK])
        kh = sb("kh", [P, 2, TOK])
        big = sb("big", [P, TILES * H * S])
        kept = big[:].rearrange("p (t c) -> p t c", t=TILES)
        hidden = big[:, 0:FC * B * S].rearrange("p (k n) -> p k n", k=FC)
        ksum = sb("ksum", [P, PB])
        bk64 = sb("bk64", [P, 1])
        ksb = sb("ksb", [P, PB, H])
        squares = sb("squares", [P, G, UNIT])
        fpair = sb("fpair", [P, 3, 2, H])
        feat = sb("feat", [P, 4, TILES, H])
        fwork = sb("fwork", [P, TILES, H])
        over_t = sb("over_t", [P, TILES, H])
        feats = sb("feats", [3, 512])
        hid1 = sb("hid1", [MLP, 512])
        hid2 = sb("hid2", [MLP, 512])
        silu = sb("silu", [P, 2, TOK])
        logits = sb("logits", [P, TILES, E8])
        key = sb("key", [P, TILES, E8])
        eq = sb("eq", [P, TILES, E8])
        hot1 = sb("hot1", [P, TILES, E8])
        hot2 = sb("hot2", [P, TILES, E8])
        score = sb("score", [P, TILES, E8])
        sel = sb("sel", [P, TILES, E8])
        tok1 = sb("tok1", [P, TILES])
        tally = sb("tally", [P, 2 * E8])
        total = sb("total", [P, 2 * E8])
        selp = sb("selp", [P, 2, E8])
        selT = sb("selT", [E8, TOK], BF16)
        selmat = sb("selmat", [E8, 4 * P], BF16)
        hm = sb("hm", [P, FC, TOK])
        wsum = sb("wsum", [P, 2])
        wmean = sb("wmean", [P, 2])
        wscale = sb("wscale", [P, 2])
        taps = big[:, 0:3 * HID].rearrange("p (k f) -> p k f", k=3)
        w2q = sb("w2q", [P, HC * D], BF16)
        identb = sb("identb", [P, P], BF16)
        amax = sb("amax", [P, 2])
        ainv = sb("ainv", [P, 2])
        xi = sb("xi", [P, 2, D])
        xs = sb("xs", [P, 3, TOK])
        hb = shifted[:, 0:2, :]
        hs = shifted[:, 2:4, :]
        hr = probs[:, 0:2, :]
        hi8 = squares[:, 0, :].bitcast(BF16).rearrange("p (t f) -> p t f", t=2)
        hT = squares[:, 1, :].bitcast(BF16).rearrange("p (t f) -> p t f", t=2)
        hmax = sb("hmax", [P, 2])
        hinv = sb("hinv", [P, 2])
        outstep = sb("outstep", [P, 2])

        psS = [ctx.enter_context(nc.psum_tensor(f"psS{i}", [P, 512], F32)) for i in range(2)]
        psT = [ctx.enter_context(nc.psum_tensor(f"psT{i}", [P, 512], F32)) for i in range(2)]
        psO = ctx.enter_context(nc.psum_tensor("psO", [P, 512], F32))
        psV = ctx.enter_context(nc.psum_tensor("psV", [P, 512], F32))
        psK = ctx.enter_context(nc.psum_tensor("psK", [P, 512], F32))
        psQ = ctx.enter_context(nc.psum_tensor("psQ", [P, 512], F32))
        psTb = [t[:, :].bitcast(BF16) for t in psT]
        O = psO[:, 0:2 * H * VW].rearrange("p (a h v) -> p a h v", a=2, h=H)

        load = sems("load", "x A B C D E F out")
        loads = {"A": load.A, "B": load.B, "C": load.C, "D": load.D, "E": load.E, "F": load.F}
        init = sems("init", "pool")
        ident = w("ident")

        def pair(t, j):
            return t[:, bass.ds(2 * j, 2), :]

        def tile_of(t, j):
            if isinstance(j, int):
                return lambda a: t[:, 2 * j + a, :]
            return lambda a: t[:, bass.ds(2 * j + a, 1), :].rearrange("p o d -> p (o d)")

        def norm_stats(dve, n, j, src, freed, count):
            for a in range(2):
                nc.vector.bn_stats(stats[:, a, :], src(a)).then_inc(n.stats.sem, 1)
            dve.wait_ge(n.stats.sem, n.stats.at(2 * j + 2))
            nc.vector.memset(carrier[:], 0.0)
            for a in range(2):
                nc.vector.bn_aggr(mv[:, a, :], stats[:, a, :]).then_inc(n.aggr.sem, 1)
            dve.wait_ge(n.aggr.sem, n.aggr.at(2 * j + 2))
            dve.wait_ge(freed.sem, freed.at(count))
            nc.vector.tensor_scalar(vareps[:], mv[:, :, 1:2], EPS, None, ALU.add).then_inc(n.vareps.sem, 1)

        def norm_rstd(pool, n, j, freed, count):
            pool.wait_ge(n.vareps.sem, n.vareps.at(j + 1))
            pool.wait_ge(freed.sem, freed.at(count))
            nc.gpsimd.tensor_tensor(rstd[:], vareps[:], minus_half[:], ALU.pow).then_inc(n.rstd.sem, 1)

        def norm_apply(dve, n, j, src, dst, freed, count):
            dve.wait_ge(n.rstd.sem, n.rstd.at(j + 1))
            dve.wait_ge(freed.sem, freed.at(count))
            for a in range(2):
                nc.vector.tensor_scalar(dst[:, a, :], src(a), mv[:, a, 0:1], rstd[:, a, :],
                                        ALU.subtract, ALU.mult).then_inc(n.normed.sem, 1)

        def norm_signals(prefix=""):
            return signals("stats:2 aggr:2 vareps:1 rstd:1 normed:2 xT_ps:1", prefix)

        def attention(st, wst=None, affine=False, cross=False, wide=False, out_proj=True, scale=DH ** -0.5,
                      queries=True, values=True, guard=False):
            n = norm_signals() if queries else None
            n0 = norm_signals("first_") if affine else None
            s = signals(f"shift:{G} exp:{G} "
                          + ("xT:1 rowmax:4 " + ("q_ps:16 k_ps:16 q:16 k:16 scores:16 " if wide else
                                                 "q_ps:1 k_ps:1 q:1 k:1 scores:4 ")) * queries
                          + f"v_ps:1 v:2 tr:{G} pT:{G} pv:{G} recip:1 heads:1 res:1 " * values
                          + "headsT_ps:1 headsT:1 out_ps:1 " * out_proj + "ctx:16 " * cross
                          + f"masked:{G} " * wide + "nans:2 " * guard)
            projected = (s.v_ps, 1) if values and not wide else (s.k_ps, H if wide else 1)
            return named(dict(st=st, w=wst or st, affine=affine, cross=cross, wide=wide, out_proj=out_proj, scale=scale,
                              queries=queries, values=values, guard=guard, n=n, n0=n0, s=s, projected=projected))

        def pe_front(pe, a, j):
            n, s = a.n, a.s
            if a.queries:
                pe.wait_ge(n.normed.sem, n.normed.at(2 * j + 2))
                if a.wide:
                    pe.wait_ge(s.q.sem, s.q.at(H * j))
                else:
                    pe.wait_ge(s.k.sem, s.k.at(j))
                for t in range(2):
                    last = nc.tensor.transpose(psK[:, t * P:(t + 1) * P], xn[:, t, :], ident)
                last.then_inc(n.xT_ps.sem, 1)
                pe.wait_ge(s.xT.sem, s.xT.at(j + 1))
            if a.cross:
                pe.wait_ge(s.ctx.sem, s.ctx.at(16 * j + 16))
            if a.out_proj:
                pe.wait_ge(s.res.sem, s.res.at(j - 1))
            src = cT if a.cross else xT
            if a.queries and not a.wide:
                pe.wait_ge(s.q.sem, s.q.at(j))
                nc.tensor.matmul(psQ[:, 0:TOK], w(a.w + "_wq"), xT[:], start=True, stop=True).then_inc(s.q_ps.sem, 1)
                nc.tensor.matmul(psK[:, TOK:2 * TOK], w(a.w + "_wk"), src[:], start=True, stop=True).then_inc(s.k_ps.sem, 1)
            if a.values:
                pe.wait_ge(s.v.sem, s.v.at(2 * j))
                for b in range(PB):
                    for e in range(2):
                        last = nc.tensor.matmul(psV[64 * e:64 * e + 64, b * 64:b * 64 + 64], src[:, b * S:(b + 1) * S],
                                                w(a.w + "_wv")[:, 64 * e:64 * e + 64], start=True, stop=True)
                last.then_inc(s.v_ps.sem, 1)

        def act_tokens(act, a, j):
            n, s = a.n, a.s
            act.wait_ge(n.xT_ps.sem, n.xT_ps.at(j + 1))
            act.wait_ge(a.projected[0].sem, a.projected[0].at(a.projected[1] * j))
            if a.affine:
                nc.scalar.activation(xT[:], psK[:, 0:TOK], ACT.Identity, bias=w("beta"), scale=w("gamma")).then_inc(s.xT.sem, 1)
            else:
                nc.scalar.activation(xT[:], psK[:, 0:TOK], ACT.Copy).then_inc(s.xT.sem, 1)

        def act_queries(act, a, j):
            s = a.s
            act.wait_ge(s.q_ps.sem, s.q_ps.at(j + 1))
            act.wait_ge(s.scores.sem, s.scores.at(G * j))
            nc.scalar.activation(qT[:], psQ[:, 0:TOK], ACT.Identity, bias=w(a.w + "_bq")).then_inc(s.q.sem, 1)

        def dve_keys(dve, a, j):
            s = a.s
            dve.wait_ge(s.k_ps.sem, s.k_ps.at(j + 1))
            dve.wait_ge(s.scores.sem, s.scores.at(G * j))
            nc.vector.scalar_tensor_tensor(out=kx[:], in0=bc(psK[:, TOK:2 * TOK], 1, HG), scalar=w(a.w + "_bk"),
                                           in1=bc(w("headmask"), 2, TOK), op0=ALU.add, op1=ALU.mult).then_inc(s.k.sem, 1)

        def dve_values(dve, a, j):
            s = a.s
            dve.wait_ge(s.v_ps.sem, s.v_ps.at(j + 1))
            dve.wait_ge(s.pv.sem, s.pv.at(G * j))
            v = psV[:, 0:PB * 64].rearrange("p (b q d) -> p b q d", b=PB, d=DH)
            bias = w(a.w + "_bv").rearrange("p (e q d) -> p e q d", e=2, d=DH)
            for e in range(2):
                r = slice(64 * e, 64 * e + 64)
                nc.vector.tensor_tensor(vbd[r, :, :, e, 0:DH], v[r, :, :, :], bc(bias[r, e, :, :], 1, PB),
                                        ALU.add).then_inc(s.v.sem, 1)

        def pe_scores(pe, a, j, g):
            s = a.s
            if g == 0:
                pe.wait_ge(s.q.sem, s.q.at(j + 1))
                pe.wait_ge(s.k.sem, s.k.at(j + 1))
            pe.wait_ge(s.shift.sem, s.shift.at(G * j + g - 1))
            r = slice(32 * g, 32 * g + 32)
            for b in range(PB):
                o = 64 * (b % 2)
                last = nc.tensor.matmul(psS[g % 2][o:o + 64, (b // 2) * 256:(b // 2) * 256 + 256],
                                        qT[r, b * S:(b + 1) * S], kx[r, :, b * S:(b + 1) * S], start=True, stop=True)
            last.then_inc(s.scores.sem, 1)

        def dve_softmax(dve, a, j, g):
            s = a.s
            dve.wait_ge(s.scores.sem, s.scores.at(G * j + g + 1))
            sc = psS[g % 2][:, :].rearrange("p (r m) -> p r m", m=S)
            mx = rowmax[:, g, :, :].rearrange("p t h -> p (t h)")
            nc.vector.tensor_reduce(mx, sc, AX.X, ALU.max).then_inc(s.rowmax.sem, 1)
            dve.wait_ge(s.rowmax.sem, s.rowmax.at(G * j + g + 1))
            dve.wait_ge(s.exp.sem, s.exp.at(G * j + g - 3))
            if a is E1:
                dve.wait_ge(e_stored[g].sem, e_stored[g].at(16 * j))
            nc.vector.tensor_tensor(shifted[:, g, :].rearrange("p (r m) -> p r m", m=S), sc, bc(mx, 2, S),
                                    ALU.subtract).then_inc(s.shift.sem, 1)

        def act_exp(act, a, j, g):
            s = a.s
            act.wait_ge(s.shift.sem, s.shift.at(G * j + g + 1))
            if a is E1:
                act.wait_ge(e.z.sem, e.z.at(G * j + g - 3))
                act.wait_ge(e.sq.sem, e.sq.at(G * j + g - 3))
            else:
                act.wait_ge(s.tr.sem, s.tr.at(G * j + g - 3))
            nc.scalar.activation(probs[:, g, :], shifted[:, g, :], ACT.Exp, scale=a.scale).then_inc(s.exp.sem, 1)

        def pe_transpose(pe, a, j, g):
            s = a.s
            pe.wait_ge(s.exp.sem, s.exp.at(G * j + g + 1))
            for k in range(4):
                last = nc.tensor.transpose(psT[g % 2][:, k * P:(k + 1) * P], probs[:, g, k * P:(k + 1) * P], ident)
            last.then_inc(s.tr.sem, 1)

        def act_probsT(act, a, j, g):
            s = a.s
            act.wait_ge(s.tr.sem, s.tr.at(G * j + g + 1))
            nc.scalar.activation(probsT[:, g % 2, :, :].rearrange("p k n -> p (k n)"), psT[g % 2][:, :],
                                 ACT.Copy).then_inc(s.pT.sem, 1)

        def pe_values(pe, a, j, g):
            s = a.s
            if g == 0:
                pe.wait_ge(s.v.sem, s.v.at(2 * j + 2))
                pe.wait_ge(s.heads.sem, s.heads.at(j))
            pe.wait_ge(s.pT.sem, s.pT.at(G * j + g + 1))
            for t in range(2):
                for q in range(2):
                    hp = 2 * g + q
                    for b in range(2):
                        last = nc.tensor.matmul(O[64 * b:64 * b + 64, t, 2 * hp:2 * hp + 2, :],
                                                probsT[:, g % 2, 2 * t + q, 64 * b:64 * b + 64],
                                                vbd[:, 2 * t + b, hp, :, :], start=True, stop=True)
            last.then_inc(s.pv.sem, 1)

        def dve_heads(dve, a, j):
            s = a.s
            dve.wait_ge(s.pv.sem, s.pv.at(G * j + G))
            nc.vector.reciprocal(rsum[:, :, :], O[:, :, :, DH]).then_inc(s.recip.sem, 1)
            dve.wait_ge(s.recip.sem, s.recip.at(j + 1))
            if a.out_proj:
                dve.wait_ge(s.headsT_ps.sem, s.headsT_ps.at(j))
            for t in range(2):
                ins = nc.vector.tensor_tensor(heads[:, t, :].rearrange("p (h d) -> p h d", h=H), O[:, t, :, 0:DH],
                                              bc(rsum[:, t, :], 2, DH), ALU.mult)
            if not a.guard:
                ins.then_inc(s.heads.sem, 1)
                return
            ins.then_inc(s.nans.sem, 1)
            dve.wait_ge(s.nans.sem, s.nans.at(2 * j + 1))
            nc.vector.tensor_tensor(isnan[:], heads[:], heads[:], ALU.not_equal).then_inc(s.nans.sem, 1)
            dve.wait_ge(s.nans.sem, s.nans.at(2 * j + 2))
            nc.vector.memset(carrier[:], 0.0)
            nc.vector.copy_predicated(heads[:], isnan[:], zeros[:]).then_inc(s.heads.sem, 1)

        def pe_out(pe, a, j):
            s = a.s
            pe.wait_ge(s.heads.sem, s.heads.at(j + 1))
            for t in range(2):
                last = nc.tensor.transpose(psQ[:, t * P:(t + 1) * P], heads[:, t, :], ident)
            last.then_inc(s.headsT_ps.sem, 1)
            pe.wait_ge(s.headsT.sem, s.headsT.at(j + 1))
            for t in range(2):
                o = psQ[:, TOK + t * D:TOK + (t + 1) * D]
                nc.tensor.matmul(o, headsT[:, t * P:(t + 1) * P], w(a.w + "_wo"), start=True, stop=False)
                last = nc.tensor.matmul(o, ones[0:1, 0:P], w(a.w + "_bo")[0:1, :], start=False, stop=True)
            last.then_inc(s.out_ps.sem, 1)

        def act_headsT(act, a, j):
            s = a.s
            act.wait_ge(s.headsT_ps.sem, s.headsT_ps.at(j + 1))
            act.wait_ge(s.out_ps.sem, s.out_ps.at(j))
            nc.scalar.activation(headsT[:], psQ[:, 0:TOK], ACT.Copy).then_inc(s.headsT.sem, 1)

        def dve_residual(dve, a, j):
            s = a.s
            if a.out_proj:
                dve.wait_ge(s.out_ps.sem, s.out_ps.at(j + 1))
                add = psQ[:, TOK:2 * TOK].rearrange("p (t d) -> p t d", t=2)
            else:
                dve.wait_ge(s.heads.sem, s.heads.at(j + 1))
                add = heads[:]
            nc.vector.tensor_tensor(pair(x, j), add, pair(x, j), ALU.add).then_inc(s.res.sem, 1)

        def pe_wide_scores(pe, a, j, g):
            s = a.s

            def project(h):
                pe.wait_ge(s.q.sem, s.q.at(H * j + h))
                nc.tensor.matmul(psK[:, 0:TOK], w("D_wq")[:, h * D:(h + 1) * D], xT[:], start=True, stop=True).then_inc(s.q_ps.sem, 1)
                pe.wait_ge(s.k.sem, s.k.at(H * j + h))
                nc.tensor.matmul(psQ[:, 0:TOK], w("D_wk")[:, h * D:(h + 1) * D], xT[:], start=True, stop=True).then_inc(s.k_ps.sem, 1)

            def score(h):
                pe.wait_ge(s.q.sem, s.q.at(H * j + h + 1))
                pe.wait_ge(s.k.sem, s.k.at(H * j + h + 1))
                if h == HG * g:
                    pe.wait_ge(s.masked.sem, s.masked.at(G * j + g - 1))
                for b in range(PB):
                    o, c = 64 * (b % 2), (b // 2) * 256 + (h % HG) * S
                    last = nc.tensor.matmul(psS[g % 2][o:o + 64, c:c + S], qh[:, h % 2, b * S:(b + 1) * S],
                                            kh[:, h % 2, b * S:(b + 1) * S], start=True, stop=True)
                last.then_inc(s.scores.sem, 1)

            project(HG * g)
            for h in range(HG * g + 1, HG * g + HG):
                project(h)
                score(h - 1)
            score(HG * g + HG - 1)

        def act_wide_queries(act, a, j, g):
            s = a.s
            for h in range(HG * g, HG * g + HG):
                act.wait_ge(s.q_ps.sem, s.q_ps.at(H * j + h + 1))
                act.wait_ge(s.scores.sem, s.scores.at(H * j + h - 1))
                nc.scalar.activation(qh[:, h % 2, :], psK[:, 0:TOK], ACT.Identity, bias=w("D_bq")[:, h:h + 1]).then_inc(s.q.sem, 1)

        def dve_wide_keys(dve, a, j, g):
            s = a.s
            for h in range(HG * g, HG * g + HG):
                dve.wait_ge(s.k_ps.sem, s.k_ps.at(H * j + h + 1))
                dve.wait_ge(s.scores.sem, s.scores.at(H * j + h - 1))
                nc.vector.tensor_scalar(kh[:, h % 2, :], psQ[:, 0:TOK], w("D_bk")[:, h:h + 1], None, ALU.add).then_inc(s.k.sem, 1)

        def dve_wide_softmax(dve, a, j, g):
            s = a.s
            sh = shifted[:, g, :].rearrange("p (r m) -> p r m", m=S)
            mx = rowmax[:, g, :, :].rearrange("p t h -> p (t h)")
            dve.wait_ge(s.scores.sem, s.scores.at(H * j + HG * g + HG))
            dve.wait_ge(s.exp.sem, s.exp.at(G * j + g - 3))
            nc.vector.tensor_tensor(sh, psS[g % 2][:, :].rearrange("p (r m) -> p r m", m=S), bc(w("D_causal"), 1, 2 * HG),
                                    ALU.add).then_inc(s.masked.sem, 1)
            dve.wait_ge(s.masked.sem, s.masked.at(G * j + g + 1))
            nc.vector.tensor_reduce(mx, sh, AX.X, ALU.max).then_inc(s.rowmax.sem, 1)
            dve.wait_ge(s.rowmax.sem, s.rowmax.at(G * j + g + 1))
            nc.vector.tensor_tensor(sh, sh, bc(mx, 2, S), ALU.subtract).then_inc(s.shift.sem, 1)

        def dve_keysum(dve, a, j):
            s = a.s
            dve.wait_ge(s.k_ps.sem, s.k_ps.at(j + 1))
            nc.vector.tensor_reduce(ksum[:], psK[:, TOK:2 * TOK].rearrange("p (b m) -> p b m", m=S), AX.X, ALU.add).then_inc(e.ksum.sem, 1)
            dve.wait_ge(e.ksum.sem, e.ksum.at(j + 1))
            dve.wait_ge(e.mean_ps.sem, e.mean_ps.at(j))
            nc.vector.scalar_tensor_tensor(out=ksb[:], in0=bc(ksum[:], 2, H), scalar=bk64[:], in1=bc(w("E_headblk"), 1, PB),
                                           op0=ALU.add, op1=ALU.mult).then_inc(e.ksb.sem, 1)

        def pe_means(pe, a, j):
            s = a.s
            pe.wait_ge(e.ksb.sem, e.ksb.at(j + 1))
            pe.wait_ge(s.q.sem, s.q.at(j + 1))
            pe.wait_ge(e.mean.sem, e.mean.at(j))
            for b in range(PB):
                o = 64 * (b % 2)
                last = nc.tensor.matmul(psO[o:o + 64, (b // 2) * H:(b // 2 + 1) * H], qT[:, b * S:(b + 1) * S], ksb[:, b, :],
                                        start=True, stop=True)
            last.then_inc(e.mean_ps.sem, 1)

        def dve_means(dve, a, j):
            dve.wait_ge(e.mean_ps.sem, e.mean_ps.at(j + 1))
            nc.vector.tensor_scalar(feat[:, 0, bass.ds(2 * j, 2), :], psO[:, 0:2 * H].rearrange("p (t h) -> p t h", h=H),
                                    1.0 / S, None, ALU.mult).then_inc(e.mean.sem, 1)

        def act_squares(act, a, j, g):
            s = a.s
            act.wait_ge(s.exp.sem, s.exp.at(G * j + g + 1))
            act.wait_ge(e.z2.sem, e.z2.at(G * j + g - 3))
            nc.scalar.activation(squares[:, g, :], probs[:, g, :], ACT.Square).then_inc(e.sq.sem, 1)

        def dve_sums(dve, a, j, g):
            s = a.s
            h4 = slice(HG * g, HG * g + HG)
            if g == 0:
                dve.wait_ge(e.kept.sem, e.kept.at(j))
            dve.wait_ge(s.exp.sem, s.exp.at(G * j + g + 1))
            nc.vector.tensor_reduce(fpair[:, 1, :, h4], probs[:, g, :].rearrange("p (t h m) -> p t h m", t=2, m=S), AX.X, ALU.add).then_inc(e.z.sem, 1)
            dve.wait_ge(e.sq.sem, e.sq.at(G * j + g + 1))
            nc.vector.tensor_reduce(fpair[:, 2, :, h4], squares[:, g, :].rearrange("p (t h m) -> p t h m", t=2, m=S), AX.X, ALU.add).then_inc(e.z2.sem, 1)

        def dve_keep(dve, a, j):
            dve.wait_ge(e.z2.sem, e.z2.at(G * j + G))
            dve.wait_ge(e.z.sem, e.z.at(G * j + G))
            nc.vector.tensor_scalar(feat[:, 2:4, bass.ds(2 * j, 2), :], fpair[:, 1:3, :, :], 1.0, None, ALU.mult).then_inc(e.kept2.sem, 1)
            nc.vector.tensor_scalar(feat[:, 1, bass.ds(2 * j, 2), :].rearrange("p t (g h) -> p t g h", h=HG),
                                    rowmax[:].rearrange("p g t h -> p t g h"), 1.0, None, ALU.mult).then_inc(e.kept.sem, 1)

        def dve_kept_softmax(dve, a, j, g):
            s = a.s
            dve.wait_ge(s.exp.sem, s.exp.at(G * j + g - 3))
            nc.vector.tensor_tensor(shifted[:, g, :].rearrange("p (t h m) -> p t h m", t=2, m=S),
                                    kept[:, bass.ds(2 * j, 2), g * 256:(g + 1) * 256].rearrange("p t (h m) -> p t h m", m=S),
                                    bc(over_t[:, bass.ds(2 * j, 2), HG * g:HG * g + HG], 3, S), ALU.mult).then_inc(s.shift.sem, 1)

        def temperature_dve(dve):
            z, p2, r = feat[:, 2, :, :], feat[:, 3, :, :], fwork[:]
            dve.wait_ge(e.kept.sem, e.kept.at(PAIRS))
            nc.vector.reciprocal(r, z).then_inc(e.v.sem, 1)
            dve.wait_ge(e.v.sem, e.v.at(1))
            nc.vector.tensor_tensor(p2, p2, r, ALU.mult).then_inc(e.v.sem, 1)
            dve.wait_ge(e.v.sem, e.v.at(2))
            nc.vector.tensor_tensor(p2, p2, r, ALU.mult).then_inc(e.v.sem, 1)
            dve.wait_ge(e.v.sem, e.v.at(3))
            nc.vector.tensor_scalar(z, p2, 1.0 / S, 1.0 / (S - 1), ALU.subtract, ALU.mult).then_inc(e.var.sem, 1)
            dve.wait_ge(e.feat_ps.sem, e.feat_ps.at(1))
            nc.vector.tensor_copy(feats[:], psS[0][0:3, :]).then_inc(e.feats.sem, 1)
            dve.wait_ge(e.logt_ps.sem, e.logt_ps.at(1))
            lt = psT[0][:, 0:TOK].rearrange("p (t h) -> p t h", h=H)
            nc.vector.tensor_scalar(fwork[:], lt, w("E_b3"), float(np.log(0.1)), ALU.add, ALU.max).then_inc(e.v.sem, 1)
            dve.wait_ge(e.v.sem, e.v.at(4))
            nc.vector.tensor_scalar(fwork[:], fwork[:], float(np.log(10.0)), None, ALU.min).then_inc(e.logt.sem, 1)
            dve.wait_ge(e.inv_t.sem, e.inv_t.at(1))
            nc.vector.tensor_scalar(over_t[:], over_t[:], 0.5, None, ALU.mult).then_inc(e.v.sem, 1)
            dve.wait_ge(e.v.sem, e.v.at(5))

        def temperature_pe(pe):
            pe.wait_ge(e.var.sem, e.var.at(1))
            for b in range(2):
                for f in range(3):
                    last = nc.tensor.matmul(psS[0][0:3, b * 256:(b + 1) * 256], w("E_featsel")[:, 9 * b + 3 * f:9 * b + 3 * f + 3],
                                            feat[:, f, :, :].rearrange("p t h -> p (t h)"), start=(f == 0), stop=(f == 2))
            last.then_inc(e.feat_ps.sem, 1)
            pe.wait_ge(e.feats.sem, e.feats.at(1))
            nc.tensor.matmul(psS[1][0:MLP, :], w("E_w1", 3), feats[:], start=True, stop=True).then_inc(e.h_ps.sem, 1)
            pe.wait_ge(e.h.sem, e.h.at(1))
            nc.tensor.matmul(psS[0][0:MLP, :], w("E_w2", MLP), hid1[:], start=True, stop=True).then_inc(e.h_ps.sem, 1)
            pe.wait_ge(e.h.sem, e.h.at(2))
            for b in range(2):
                last = nc.tensor.matmul(psT[0][64 * b:64 * b + 64, 0:TOK], w("E_w3", MLP), hid2[:, b * 256:(b + 1) * 256],
                                        start=True, stop=True)
            last.then_inc(e.logt_ps.sem, 1)

        def temperature_act(act):
            act.wait_ge(e.h_ps.sem, e.h_ps.at(1))
            nc.scalar.activation(hid1[:], psS[1][0:MLP, :], ACT.Gelu, bias=w("E_b1", MLP)).then_inc(e.h.sem, 1)
            act.wait_ge(e.h_ps.sem, e.h_ps.at(2))
            nc.scalar.activation(hid2[:], psS[0][0:MLP, :], ACT.Gelu, bias=w("E_b2", MLP)).then_inc(e.h.sem, 1)
            act.wait_ge(e.logt.sem, e.logt.at(1))
            nc.scalar.activation(over_t[:], fwork[:], ACT.Exp, scale=-1.0).then_inc(e.inv_t.sem, 1)

        def pe_hidden(pe, j):
            s = c
            pe.wait_ge(cn.normed.sem, cn.normed.at(2 * j + 2))
            pe.wait_ge(s.xT.sem, s.xT.at(j))
            for t in range(2):
                last = nc.tensor.transpose(psK[:, t * P:(t + 1) * P], xn[:, t, :], ident)
            last.then_inc(cn.xT_ps.sem, 1)
            pe.wait_ge(s.xT.sem, s.xT.at(j + 1))
            pe.wait_ge(s.logits.sem, s.logits.at(j))
            for t in range(2):
                last = nc.tensor.matmul(psO[:, t * E8:(t + 1) * E8], xT[:, t * P:(t + 1) * P], w("C_gate"), start=True, stop=True)
            last.then_inc(s.logits_ps.sem, 1)
            for k in range(FC):
                pe.wait_ge(s.hidden.sem, s.hidden.at(FC * j + max(k - 1, 0)))
                nc.tensor.matmul(psS[k % 2][:, 0:TOK], w("C_wg")[:, k * P:(k + 1) * P], xT[:], start=True, stop=True)
                nc.tensor.matmul(psS[k % 2][:, TOK:2 * TOK], w("C_wu")[:, k * P:(k + 1) * P], xT[:], start=True,
                                 stop=True).then_inc(s.gate_up.sem, 1)

        def act_hidden(act, j):
            s = c
            act.wait_ge(cn.xT_ps.sem, cn.xT_ps.at(j + 1))
            act.wait_ge(s.gate_up.sem, s.gate_up.at(FC * j))
            nc.scalar.activation(xT[:], psK[:, 0:TOK], ACT.Copy).then_inc(s.xT.sem, 1)
            for k in range(FC):
                act.wait_ge(s.gate_up.sem, s.gate_up.at(FC * j + k + 1))
                act.wait_ge(s.hidden.sem, s.hidden.at(FC * j + max(k - 1, 0)))
                nc.scalar.activation(silu[:, k % 2, :], psS[k % 2][:, 0:TOK], ACT.Silu).then_inc(s.silu.sem, 1)

        def dve_hidden(dve, j):
            s = c
            dve.wait_ge(s.logits_ps.sem, s.logits_ps.at(j + 1))
            nc.vector.tensor_tensor(logits[:, bass.ds(2 * j, 2), :], psO[:, 0:2 * E8].rearrange("p (t e) -> p t e", e=E8),
                                    bc(w("C_lb"), 1, 2), ALU.add).then_inc(s.logits.sem, 1)
            for k in range(FC):
                dve.wait_ge(s.silu.sem, s.silu.at(FC * j + k + 1))
                nc.vector.tensor_tensor(hidden[:, k, bass.ds(j * TOK, TOK)], silu[:, k % 2, :], psS[k % 2][:, TOK:2 * TOK],
                                        ALU.mult).then_inc(s.hidden.sem, 1)

        def route_dve(dve):
            seq = [0]

            def then(ins):
                seq[0] += 1
                ins.then_inc(c.route.sem, 1)
                dve.wait_ge(c.route.sem, c.route.at(seq[0]))

            def best(key, one):
                then(nc.vector.tensor_reduce(tok1[:], key, AX.X, ALU.max))
                then(nc.vector.tensor_tensor(eq[:], key, bc(tok1[:], 2, E8), ALU.is_equal))
                then(nc.vector.tensor_tensor(eq[:], eq[:], bc(w("C_first"), 1, TILES), ALU.mult))
                then(nc.vector.tensor_reduce(tok1[:], eq[:], AX.X, ALU.max))
                then(nc.vector.tensor_tensor(one, eq[:], bc(tok1[:], 2, E8), ALU.is_equal))

            dve.wait_ge(c.logits.sem, c.logits.at(PAIRS))
            then(nc.vector.tensor_scalar(key[:], logits[:], 17.0, None, ALU.min))
            best(key[:], hot1[:])
            then(nc.vector.scalar_tensor_tensor(out=key[:], in0=hot1[:], scalar=-1e30, in1=key[:], op0=ALU.mult, op1=ALU.add))
            best(key[:], hot2[:])
            dve.wait_ge(c.sig.sem, c.sig.at(1))
            then(nc.vector.tensor_tensor(eq[:], hot1[:], hot2[:], ALU.add))
            nc.vector.tensor_tensor(sel[:], hot1[:], hot2[:], ALU.add).then_inc(c.sel.sem, 1)
            then(nc.vector.tensor_tensor(key[:], eq[:], score[:], ALU.mult))
            then(nc.vector.tensor_reduce(tok1[:], key[:], AX.X, ALU.add))
            then(nc.vector.tensor_scalar(tok1[:], tok1[:], 1e-8, None, ALU.add))
            then(nc.vector.reciprocal(tok1[:], tok1[:]))
            then(nc.vector.tensor_tensor(key[:], key[:], bc(tok1[:], 2, E8), ALU.mult))
            then(nc.vector.tensor_reduce(tally[:, 0:E8], eq[:].rearrange("p t e -> p e t"), AX.X, ALU.add))
            then(nc.vector.tensor_reduce(tally[:, E8:2 * E8], key[:].rearrange("p t e -> p e t"), AX.X, ALU.add))
            nc.vector.memset(carrier[:], 0.0).then_inc(c.tally.sem, 1)
            dve.wait_ge(c.total_ps.sem, c.total_ps.at(1))
            then(nc.vector.tensor_scalar(total[:, 0:E8], psO[:, 0:E8], 1.0, None, ALU.max))
            then(nc.vector.reciprocal(total[:, 0:E8], total[:, 0:E8]))
            then(nc.vector.tensor_tensor(total[:, E8:2 * E8], total[:, 0:E8], psO[:, E8:2 * E8], ALU.mult))
            means = total[:, E8:2 * E8].rearrange("p (k e) -> p e k", e=2)
            wd = w("C_wd").rearrange("p (k d) -> p k d", k=FC)
            for half in range(2):
                r = slice(64 * half, 64 * half + 64)
                then(nc.vector.tensor_tensor(wd[r, 0:4, :], wd[r, 0:4, :], bc(means[r, half, :], 2, D), ALU.mult))
            nc.vector.memset(carrier[:], 0.0).then_inc(c.wd.sem, 1)

        def route_pe(pe):
            pe.wait_ge(c.tally.sem, c.tally.at(1))
            nc.tensor.matmul(psO[:, 0:2 * E8], ones[:], tally[:], start=True, stop=True).then_inc(c.total_ps.sem, 1)
            pe.wait_ge(c.wd.sem, c.wd.at(1))

        def dve_pick(dve, j):
            s = c
            dve.wait_ge(s.sel_ps.sem, s.sel_ps.at(j))
            nc.vector.tensor_scalar(selp[:], sel[:, bass.ds(2 * j, 2), :], 1.0, None, ALU.mult).then_inc(s.selp.sem, 1)
            dve.wait_ge(s.down_ps.sem, s.down_ps.at(j))
            nc.vector.tensor_scalar(hm[:, 4, :], hidden[:, 4, bass.ds(j * TOK, TOK)], 1.0, None, ALU.mult).then_inc(s.shared.sem, 1)

        def pe_down(pe, j):
            s = c
            pe.wait_ge(s.selp.sem, s.selp.at(j + 1))
            pe.wait_ge(s.selT.sem, s.selT.at(j))
            for t in range(2):
                last = nc.tensor.transpose(psK[0:E8, t * P:(t + 1) * P], selp[:, t, :], ident)
            last.then_inc(s.sel_ps.sem, 1)
            pe.wait_ge(s.selT.sem, s.selT.at(j + 1))
            for k in range(4):
                pe.wait_ge(s.masked.sem, s.masked.at(4 * j + k - 1))
                nc.tensor.matmul(psT[k % 2][:, 0:TOK], selmat[:, k * P:(k + 1) * P], selT[:], start=True, stop=True).then_inc(s.mask_ps.sem, 1)
            pe.wait_ge(s.masked.sem, s.masked.at(4 * j + 4))
            pe.wait_ge(s.shared.sem, s.shared.at(j + 1))
            pe.wait_ge(s.res.sem, s.res.at(j))
            for t in range(2):
                for k in range(FC):
                    last = nc.tensor.matmul(psV[:, t * D:(t + 1) * D], hm[:, k, t * P:(t + 1) * P], w("C_wd")[:, k * D:(k + 1) * D],
                                            start=(k == 0), stop=(k == FC - 1))
            last.then_inc(s.down_ps.sem, 1)

        def dve_down(dve, j):
            s = c
            for k in range(4):
                dve.wait_ge(s.mask_ps.sem, s.mask_ps.at(4 * j + k + 1))
                nc.vector.tensor_tensor(hm[:, k, :], psT[k % 2][:, 0:TOK], hidden[:, k, bass.ds(j * TOK, TOK)], ALU.mult).then_inc(s.masked.sem, 1)

        def dve_down_residual(dve, j):
            dve.wait_ge(c.down_ps.sem, c.down_ps.at(j + 1))
            nc.vector.tensor_tensor(pair(x, j), psV[:, 0:TOK].rearrange("p (t d) -> p t d", t=2), pair(x, j), ALU.add).then_inc(c.res.sem, 1)

        def weights_dve(dve):
            seq = [0]

            def then(ins):
                seq[0] += 1
                ins.then_inc(f.wstep.sem, 1)
                dve.wait_ge(f.wstep.sem, f.wstep.at(seq[0]))

            then(nc.vector.tensor_reduce(wsum[:, 0:1], w("F_w1"), AX.X, ALU.add, apply_absolute_value=True))
            then(nc.vector.tensor_reduce(wsum[:, 1:2], w("F_w2"), AX.X, ALU.add, apply_absolute_value=True))
            nc.vector.memset(carrier[:], 0.0).then_inc(f.wsum.sem, 1)
            dve.wait_ge(f.wsum_ps.sem, f.wsum_ps.at(1))
            then(nc.vector.tensor_scalar(wmean[:], psO[:, 0:2], 1.0 / (D * HID), 1e-5, ALU.mult, ALU.max))
            then(nc.vector.reciprocal(wscale[:], wmean[:]))
            for n, name in enumerate(("F_w1", "F_w2")):
                wq = w(name)
                then(nc.vector.tensor_scalar(wq, wq, wscale[:, n:n + 1], ROUND, ALU.mult, ALU.add))
                then(nc.vector.tensor_scalar(wq, wq, ROUND, 1.0, ALU.subtract, ALU.min))
                if n == 0:
                    then(nc.vector.tensor_scalar(wq, wq, -1.0, wmean[:, 0:1], ALU.max, ALU.mult))
                    then(nc.vector.tensor_tensor(taps[:], w("F_cw").rearrange("p (k f) -> p k f", k=3), bc(wq, 1, 3), ALU.mult))
                else:
                    then(nc.vector.tensor_scalar(w2q[:], wq, -1.0, None, ALU.max))
            then(nc.vector.tensor_copy(identb[:], ident))
            nc.vector.memset(carrier[:], 0.0).then_inc(f.weights.sem, 1)

        def weights_pe(pe):
            pe.wait_ge(f.wsum.sem, f.wsum.at(1))
            nc.tensor.matmul(psO[:, 0:2], ones[:], wsum[:], start=True, stop=True).then_inc(f.wsum_ps.sem, 1)
            pe.wait_ge(f.weights.sem, f.weights.at(1))

        def dve_quantise(dve, j):
            dve.wait_ge(fn.normed.sem, fn.normed.at(2 * j + 2))
            dve.wait_ge(fn.xT_ps.sem, fn.xT_ps.at(j))
            nc.vector.tensor_reduce(amax[:], xn[:], AX.X, ALU.max, apply_absolute_value=True).then_inc(f.amax.sem, 1)
            dve.wait_ge(f.amax.sem, f.amax.at(j + 1))
            nc.vector.tensor_scalar(amax[:], amax[:], 1e-5, 1.0 / 127.0, ALU.max, ALU.mult).then_inc(f.astep.sem, 1)
            dve.wait_ge(f.astep.sem, f.astep.at(j + 1))
            nc.vector.reciprocal(ainv[:], amax[:]).then_inc(f.ainv.sem, 1)
            dve.wait_ge(f.ainv.sem, f.ainv.at(j + 1))
            for t in range(2):
                nc.vector.tensor_scalar(xi[:, t, :], xn[:, t, :], ainv[:, t:t + 1], ROUND, ALU.mult, ALU.add).then_inc(f.xi.sem, 1)
            dve.wait_ge(f.xi.sem, f.xi.at(2 * j + 2))
            nc.vector.tensor_scalar(xi[:], xi[:], ROUND + 127.0, ROUND - 128.0, ALU.min, ALU.max).then_inc(f.clip.sem, 1)
            dve.wait_ge(f.clip.sem, f.clip.at(j + 1))
            for t in range(2):
                nc.vector.tensor_scalar(xi[:, t, :], xi[:, t, :], ROUND, amax[:, t:t + 1], ALU.subtract, ALU.mult).then_inc(f.xq.sem, 1)

        def pe_tokens(pe, j):
            pe.wait_ge(f.xq.sem, f.xq.at(2 * j + 2))
            pe.wait_ge(f.xs.sem, f.xs.at(3 * j))
            for t in range(2):
                last = nc.tensor.transpose(psK[:, t * P:(t + 1) * P], xi[:, t, :], ident)
            last.then_inc(fn.xT_ps.sem, 1)

        def act_shifts(act, j):
            act.wait_ge(fn.xT_ps.sem, fn.xT_ps.at(j + 1))
            act.wait_ge(f.h_ps.sem, f.h_ps.at(2 * j))
            src = psK[:, 0:TOK].rearrange("p (b m) -> p b m", m=S)
            for k in range(3):
                dst = xs[:, k, :].rearrange("p (b m) -> p b m", m=S)
                lo, hi = max(1 - k, 0), S - max(k - 1, 0)
                nc.scalar.activation(dst[:, :, lo:hi], src[:, :, lo + k - 1:hi + k - 1], ACT.Copy).then_inc(f.xs.sem, 1)

        def pe_conv(pe, j, t):
            pe.wait_ge(f.xs.sem, f.xs.at(3 * j + 3))
            pe.wait_ge(f.biased.sem, f.biased.at(2 * j + t - 1))
            for k in range(3):
                last = nc.tensor.matmul(psS[t][:, :], xs[:, k, t * P:(t + 1) * P], taps[:, k, :], start=(k == 0), stop=(k == 2))
            last.then_inc(f.h_ps.sem, 1)

        def dve_bias(dve, j, t):
            dve.wait_ge(f.h_ps.sem, f.h_ps.at(2 * j + t + 1))
            dve.wait_ge(f.hi.sem, f.hi.at(2 * j + t - 1))
            nc.vector.tensor_tensor(hb[:, t, :], psS[t][:, :], w("F_cb"), ALU.add).then_inc(f.biased.sem, 1)

        def act_silu(act, j, t):
            act.wait_ge(f.biased.sem, f.biased.at(2 * j + t + 1))
            act.wait_ge(f.hr.sem, f.hr.at(2 * j + t - 1))
            nc.scalar.activation(hs[:, t, :], hb[:, t, :], ACT.Silu).then_inc(f.silu.sem, 1)

        def dve_quantise_hidden(dve, j, t):
            n = 2 * j + t + 1
            m, r = hmax[:, t:t + 1], hinv[:, t:t + 1]
            dve.wait_ge(f.silu.sem, f.silu.at(n))
            nc.vector.tensor_reduce(m, hs[:, t, :], AX.X, ALU.max, apply_absolute_value=True).then_inc(f.hmax.sem, 1)
            dve.wait_ge(f.hmax.sem, f.hmax.at(n))
            dve.wait_ge(f.res.sem, f.res.at(n - 2))
            nc.vector.tensor_scalar(m, m, 1e-5, 1.0 / 127.0, ALU.max, ALU.mult).then_inc(f.hstep.sem, 1)
            dve.wait_ge(f.hstep.sem, f.hstep.at(n))
            nc.vector.reciprocal(r, m).then_inc(f.hinv.sem, 1)
            nc.vector.tensor_scalar(outstep[:, t:t + 1], m, wmean[:, 1:2], None, ALU.mult).then_inc(f.outstep.sem, 1)
            dve.wait_ge(f.hinv.sem, f.hinv.at(n))
            nc.vector.tensor_scalar(hr[:, t, :], hs[:, t, :], r, ROUND, ALU.mult, ALU.add).then_inc(f.hr.sem, 1)
            dve.wait_ge(f.hr.sem, f.hr.at(n))
            nc.vector.tensor_scalar(hr[:, t, :], hr[:, t, :], ROUND, 127.0, ALU.subtract, ALU.min).then_inc(f.hclip.sem, 1)
            dve.wait_ge(f.hclip.sem, f.hclip.at(n))
            dve.wait_ge(f.hT_ps.sem, f.hT_ps.at(n - 2))
            nc.vector.tensor_scalar(hi8[:, t, :], hr[:, t, :], -128.0, None, ALU.max).then_inc(f.hi.sem, 1)

        def pe_second(pe, j, t):
            n = 2 * j + t + 1
            pe.wait_ge(f.hi.sem, f.hi.at(n))
            for k in range(HC):
                last = nc.tensor.transpose(psTb[t][:, k * P:(k + 1) * P], hi8[:, t, k * P:(k + 1) * P], identb[:])
            last.then_inc(f.hT_ps.sem, 1)
            pe.wait_ge(f.hT.sem, f.hT.at(n))
            pe.wait_ge(f.res.sem, f.res.at(n - 1))
            for k in range(HC):
                last = nc.tensor.matmul(psV[:, t * D:(t + 1) * D], hT[:, t, k * P:(k + 1) * P], w2q[:, k * D:(k + 1) * D],
                                        start=(k == 0), stop=(k == HC - 1))
            last.then_inc(f.out_ps.sem, 1)

        def act_hiddenT(act, j, t):
            n = 2 * j + t + 1
            act.wait_ge(f.hT_ps.sem, f.hT_ps.at(n))
            act.wait_ge(f.out_ps.sem, f.out_ps.at(n - 2))
            nc.scalar.activation(hT[:, t, :], psTb[t][:, 0:HC * P], ACT.Copy).then_inc(f.hT.sem, 1)

        def dve_second_residual(dve, j, t):
            n = 2 * j + t + 1
            dve.wait_ge(f.out_ps.sem, f.out_ps.at(n))
            dve.wait_ge(f.outstep.sem, f.outstep.at(n))
            tile = tile_of(x, j)(t)
            nc.vector.scalar_tensor_tensor(out=tile, in0=psV[:, t * D:(t + 1) * D], scalar=outstep[:, t:t + 1], in1=tile,
                                           op0=ALU.mult, op1=ALU.add).then_inc(f.res.sem, 1)

        def dve_norm(dve, a, j):
            if a.affine:
                norm_stats(dve, a.n0, j, tile_of(x, j), a.n.rstd, j)
                norm_apply(dve, a.n0, j, tile_of(x, j), xm, a.n.normed, 2 * j)
                dve.wait_ge(a.n0.normed.sem, a.n0.normed.at(2 * j + 2))
                norm_stats(dve, a.n, j, lambda t: xm[:, t, :], a.n0.rstd, j + 1)
                norm_apply(dve, a.n, j, lambda t: xm[:, t, :], xn, a.n.xT_ps, j)
            else:
                norm_stats(dve, a.n, j, tile_of(x, j), a.n.rstd, j)
                norm_apply(dve, a.n, j, tile_of(x, j), xn, a.n.xT_ps, j)

        def pool_norm(pool, a, j):
            if a.affine:
                norm_rstd(pool, a.n0, j, a.n.normed, 2 * j)
                norm_rstd(pool, a.n, j, a.n0.normed, 2 * j + 2)
            else:
                norm_rstd(pool, a.n, j, a.n.normed, 2 * j)

        def sync_context(sp, a):
            def step(j):
                sp.wait_ge(a.projected[0].sem, a.projected[0].at(j))
                sp.dma_start(cT[:], ctx_in[:, bass.ds(j * TOK, TOK)]).then_inc(a.s.ctx.sem, 16)
            if a is E2:
                sp.wait_ge(E1.s.k_ps.sem, E1.s.k_ps.at(PAIRS))
                sp.wait_ge(E1.s.ctx.sem, E1.s.ctx.at(16 * PAIRS))
            over_pairs(sp, step, PAIRS)

        def sync_statistics(sp, a):
            def step(j, more=True):
                if more:
                    sp.wait_ge(a.s.k_ps.sem, a.s.k_ps.at(j + 1))
                    sp.dma_start(cT[:], ctx_in[:, bass.ds((j + 1) * TOK, TOK)]).then_inc(a.s.ctx.sem, 16)
                for g in range(G):
                    sp.wait_ge(a.s.shift.sem, a.s.shift.at(G * j + g + 1))
                    sp.dma_start(kept[:, bass.ds(2 * j, 2), g * 256:(g + 1) * 256],
                                 shifted[:, g, :].rearrange("p (t c) -> p t c", t=2)).then_inc(e_stored[g].sem, 16)
            sp.wait_ge(Bx.s.v_ps.sem, Bx.s.v_ps.at(PAIRS))
            sp.wait_ge(Bx.s.ctx.sem, Bx.s.ctx.at(16 * PAIRS))
            sp.dma_start(cT[:], ctx_in[:, 0:TOK]).then_inc(a.s.ctx.sem, 16)
            over_pairs(sp, step, PAIRS - 1)
            step(PAIRS - 1, more=False)

        def over_pairs(eng, step, last):
            step(0)
            with eng.Fori(1, last) as i:
                step(i)

        def attention_pe(pe, a):
            scores = pe_wide_scores if a.wide else pe_scores

            def step(i):
                pe_front(pe, a, i + 1)
                for g in range(G):
                    pe_transpose(pe, a, i, g)
                    if a.queries:
                        scores(pe, a, i + 1, g)
                    pe_values(pe, a, i, g)
                if a.out_proj:
                    pe_out(pe, a, i)

            pe_front(pe, a, 0)
            if a.queries:
                for g in range(G):
                    scores(pe, a, 0, g)
            over_pairs(pe, step, PAIRS - 1)
            for g in range(G):
                pe_transpose(pe, a, PAIRS - 1, g)
                pe_values(pe, a, PAIRS - 1, g)
            if a.out_proj:
                pe_out(pe, a, PAIRS - 1)

        def attention_act(act, a):
            def front(i):
                if a.queries:
                    act_tokens(act, a, i)
                    if not a.wide:
                        act_queries(act, a, i)

            def unit(i, g):
                if a.wide:
                    act_wide_queries(act, a, i, g)
                act_exp(act, a, i, g)

            def step(i):
                front(i + 1)
                for g in range(G):
                    act_probsT(act, a, i, g)
                    unit(i + 1, g)
                if a.out_proj:
                    act_headsT(act, a, i)

            front(0)
            for g in range(G):
                unit(0, g)
            over_pairs(act, step, PAIRS - 1)
            for g in range(G):
                act_probsT(act, a, PAIRS - 1, g)
            if a.out_proj:
                act_headsT(act, a, PAIRS - 1)

        def attention_dve(dve, a):
            def front(i):
                if a.queries and not a.wide:
                    dve_keys(dve, a, i)

            def unit(i, g):
                if a.wide:
                    dve_wide_keys(dve, a, i, g)
                    dve_wide_softmax(dve, a, i, g)
                elif a.queries:
                    dve_softmax(dve, a, i, g)
                else:
                    dve_kept_softmax(dve, a, i, g)

            def step(i, norm=True):
                front(i + 1)
                if norm and a.queries:
                    dve_norm(dve, a, i + 2)
                for g in range(G):
                    unit(i + 1, g)
                dve_values(dve, a, i + 1)
                dve_heads(dve, a, i)
                dve_residual(dve, a, i)

            if a.queries:
                dve_norm(dve, a, 0)
                dve_norm(dve, a, 1)
            front(0)
            dve_values(dve, a, 0)
            for g in range(G):
                unit(0, g)
            over_pairs(dve, step, PAIRS - 2)
            step(PAIRS - 2, norm=False)
            dve_heads(dve, a, PAIRS - 1)
            dve_residual(dve, a, PAIRS - 1)
            dve.wait_ge(a.s.res.sem, a.s.res.at(PAIRS))

        def attention_pool(pool, a):
            over_pairs(pool, lambda j: pool_norm(pool, a, j), PAIRS)

        def statistics_pe(pe, a):
            def step(i, front=True):
                pe_means(pe, a, i)
                for g in range(G):
                    if g == 2 and front:
                        pe_front(pe, a, i + 1)
                    pe_scores(pe, a, i, g)

            pe_front(pe, a, 0)
            over_pairs(pe, step, PAIRS - 1)
            step(PAIRS - 1, front=False)

        def statistics_act(act, a):
            def step(i, front=True):
                for g in range(G):
                    if g == 2 and front:
                        act_tokens(act, a, i + 1)
                    act_exp(act, a, i, g)
                    act_squares(act, a, i, g)
                if front:
                    act_queries(act, a, i + 1)

            act_tokens(act, a, 0)
            act_queries(act, a, 0)
            over_pairs(act, step, PAIRS - 1)
            step(PAIRS - 1, front=False)

        def statistics_dve(dve, a):
            def front(i):
                dve_keysum(dve, a, i)
                dve_keys(dve, a, i)

            def step(i, more=2):
                dve_means(dve, a, i)
                for g in range(G):
                    dve_softmax(dve, a, i, g)
                    if g:
                        dve_sums(dve, a, i, g - 1)
                dve_sums(dve, a, i, G - 1)
                dve_keep(dve, a, i)
                if more > 0:
                    front(i + 1)
                if more > 1:
                    dve_norm(dve, a, i + 2)

            dve_norm(dve, a, 0)
            dve_norm(dve, a, 1)
            front(0)
            over_pairs(dve, step, PAIRS - 2)
            step(PAIRS - 2, more=1)
            step(PAIRS - 1, more=0)

        def experts_pe(pe):
            over_pairs(pe, lambda j: pe_hidden(pe, j), PAIRS)
            route_pe(pe)
            over_pairs(pe, lambda j: pe_down(pe, j), PAIRS)

        def experts_act(act):
            over_pairs(act, lambda j: act_hidden(act, j), PAIRS)
            act.wait_ge(c.logits.sem, c.logits.at(PAIRS))
            nc.scalar.activation(score[:], logits[:], ACT.Sigmoid).then_inc(c.sig.sem, 1)
            def selT_copy(j):
                act.wait_ge(c.sel_ps.sem, c.sel_ps.at(j + 1))
                act.wait_ge(c.mask_ps.sem, c.mask_ps.at(4 * j))
                nc.scalar.activation(selT[:], psK[0:E8, 0:TOK], ACT.Copy).then_inc(c.selT.sem, 1)
            over_pairs(act, selT_copy, PAIRS)

        def experts_dve(dve):
            def step(j, norm=True):
                if norm:
                    dve_stage_norm(dve, cn, j + 1)
                dve_hidden(dve, j)

            dve_stage_norm(dve, cn, 0)
            over_pairs(dve, step, PAIRS - 1)
            step(PAIRS - 1, norm=False)
            nc.vector.tensor_copy(selmat[:], w("C_sel", E8)).then_inc(c.selmat.sem, 1)
            dve.wait_ge(c.selmat.sem, c.selmat.at(1))
            route_dve(dve)
            dve.wait_ge(c.sel.sem, c.sel.at(1))

            def down(j, pick=True):
                dve_down(dve, j)
                if pick:
                    dve_pick(dve, j + 1)
                dve_down_residual(dve, j)

            dve_pick(dve, 0)
            over_pairs(dve, down, PAIRS - 1)
            down(PAIRS - 1, pick=False)
            dve.wait_ge(c.res.sem, c.res.at(PAIRS))

        def dve_stage_norm(dve, n, j):
            norm_stats(dve, n, j, tile_of(x, j), n.rstd, j)
            norm_apply(dve, n, j, tile_of(x, j), xn, n.xT_ps, j)

        def stage_norm_pool(pool, n):
            over_pairs(pool, lambda j: norm_rstd(pool, n, j, n.normed, 2 * j), PAIRS)

        def convolved_pe(pe):
            weights_pe(pe)

            def step(i):
                pe_tokens(pe, i + 1)
                for t in range(2):
                    pe_conv(pe, i + 1, t)
                    pe_second(pe, i, t)

            pe_tokens(pe, 0)
            for t in range(2):
                pe_conv(pe, 0, t)
            over_pairs(pe, step, PAIRS - 1)
            for t in range(2):
                pe_second(pe, PAIRS - 1, t)

        def convolved_act(act):
            def step(i):
                act_shifts(act, i + 1)
                for t in range(2):
                    act_hiddenT(act, i, t)
                    act_silu(act, i + 1, t)

            act.wait_ge(f.edges.sem, f.edges.at(1))
            act_shifts(act, 0)
            for t in range(2):
                act_silu(act, 0, t)
            over_pairs(act, step, PAIRS - 1)
            for t in range(2):
                act_hiddenT(act, PAIRS - 1, t)

        def convolved_dve(dve):
            weights_dve(dve)

            def front(i):
                dve_stage_norm(dve, fn, i)
                dve_quantise(dve, i)

            def unit(i):
                for t in range(2):
                    dve_bias(dve, i, t)
                for t in range(2):
                    dve_quantise_hidden(dve, i, t)

            def step(i, norm=True):
                for t in range(2):
                    dve_bias(dve, i + 1, t)
                if norm:
                    front(i + 2)
                for t in range(2):
                    dve_second_residual(dve, i, t)
                    dve_quantise_hidden(dve, i + 1, t)

            front(0)
            front(1)
            unit(0)
            over_pairs(dve, step, PAIRS - 2)
            step(PAIRS - 2, norm=False)
            for t in range(2):
                dve_second_residual(dve, PAIRS - 1, t)

        A = attention("A", affine=True, out_proj=False)
        Bx = attention("B", cross=True)
        c, cn = sems("C", "xT logits_ps logits gate_up silu hidden sig route sel tally total_ps wd selmat sel_ps selp shared "
                          "selT mask_ps masked down_ps res"), norm_signals()
        Dw = attention("D", wide=True, scale=D ** -0.5)
        E1 = attention("E1", wst="E", cross=True, values=False, out_proj=False)
        E2 = attention("E2", wst="E", cross=True, queries=False, scale=1.0, guard=True)
        e = sems("E", "bk64 ksum ksb mean_ps mean sq z z2 kept kept2 var feat_ps feats h_ps h logt_ps logt inv_t v "
                      "stored0 stored1 stored2 stored3")
        e_stored = [e.stored0, e.stored1, e.stored2, e.stored3]
        f, fn = sems("F", "wstep wsum wsum_ps weights edges amax astep ainv xi clip xq xs h_ps biased silu hmax hstep hinv outstep "
                          "hr hclip hi hT_ps hT out_ps res"), norm_signals()
        block = ctx.enter_context(nc.Block())

        @block.sync
        def _(sp):
            sp.dma_start(x[:].rearrange("p t d -> p (t d)"), x_in).then_inc(load.x.sem, 16)
            for p in STAGES:
                sp.dma_start(wt[p][:], packs_in[p]).then_inc(loads[p].sem, 16)
            for a in (Bx, E1, E2):
                if a.w in STAGES:
                    if a is E1:
                        sync_statistics(sp, E1)
                    else:
                        sync_context(sp, a)
            sp.wait_ge(f.res.sem, f.res.at(TILES))
            sp.dma_start(out, x[:].rearrange("p t d -> p (t d)")).then_inc(load.out.sem, 16)
            sp.wait_ge(load.out.sem, load.out.at(16))

        @block.gpsimd
        def _(pool):
            nc.gpsimd.memset(minus_half[:], -0.5).then_inc(init.pool.sem, 1)
            nc.gpsimd.memset(ones[:], 1.0).then_inc(init.pool.sem, 1)
            nc.gpsimd.memset(zeros[:], 0.0).then_inc(init.pool.sem, 1)
            nc.gpsimd.memset(vbd[:], 0.0).then_inc(init.pool.sem, 1)
            pool.wait_ge(init.pool.sem, init.pool.at(4))
            nc.gpsimd.memset(vbd[0:64, :, :, 0, DH], 1.0).then_inc(init.pool.sem, 1)
            nc.gpsimd.memset(vbd[64:128, :, :, 1, DH], 1.0).then_inc(init.pool.sem, 1)
            for a, p in ((A, "A"), (Bx, "B"), (None, "C"), (Dw, "D"), (E1, "E"), (None, "F")):
                if p not in STAGES:
                    continue
                if a:
                    attention_pool(pool, a)
                elif p == "C":
                    stage_norm_pool(pool, cn)
                else:
                    nc.gpsimd.memset(xs[:], 0.0).then_inc(f.edges.sem, 1)
                    stage_norm_pool(pool, fn)

        @block.scalar
        def _(act):
            for p in STAGES:
                act.wait_ge(loads[p].sem, loads[p].at(16))
                if p == "A":
                    attention_act(act, A)
                elif p == "B":
                    attention_act(act, Bx)
                elif p == "C":
                    experts_act(act)
                elif p == "D":
                    attention_act(act, Dw)
                elif p == "E":
                    statistics_act(act, E1)
                    temperature_act(act)
                    attention_act(act, E2)
                else:
                    convolved_act(act)

        @block.vector
        def _(dve):
            dve.wait_ge(load.x.sem, load.x.at(16))
            dve.wait_ge(init.pool.sem, init.pool.at(6))
            for p in STAGES:
                dve.wait_ge(loads[p].sem, loads[p].at(16))
                if p == "A":
                    attention_dve(dve, A)
                elif p == "B":
                    attention_dve(dve, Bx)
                elif p == "C":
                    experts_dve(dve)
                elif p == "D":
                    attention_dve(dve, Dw)
                elif p == "E":
                    nc.vector.tensor_scalar(bk64[:], w("E_bk"), float(S), None, ALU.mult).then_inc(e.bk64.sem, 1)
                    dve.wait_ge(e.bk64.sem, e.bk64.at(1))
                    statistics_dve(dve, E1)
                    temperature_dve(dve)
                    attention_dve(dve, E2)
                else:
                    convolved_dve(dve)

        @block.tensor
        def _(pe):
            pe.wait_ge(init.pool.sem, init.pool.at(6))
            for p in STAGES:
                pe.wait_ge(loads[p].sem, loads[p].at(16))
                if p == "A":
                    attention_pe(pe, A)
                elif p == "B":
                    attention_pe(pe, Bx)
                elif p == "C":
                    experts_pe(pe)
                elif p == "D":
                    attention_pe(pe, Dw)
                elif p == "E":
                    statistics_pe(pe, E1)
                    temperature_pe(pe)
                    attention_pe(pe, E2)
                else:
                    convolved_pe(pe)


_INS = ["x", "ctx_1024"]


def layouts(i):
    f = np.float32

    def rows(a, n=P):
        a = np.asarray(a)
        return np.concatenate([a, np.zeros((n - a.shape[0], a.shape[1]), a.dtype)]) if a.shape[0] < n else a

    def col(v):
        return rows(np.asarray(v).reshape(-1, 1))

    def over(v):
        v = np.asarray(v).reshape(1, -1)
        return np.repeat(v, P, axis=0)

    def even_odd(a):
        a = np.asarray(a)
        return a.reshape(-1, H // 2, 2, DH).transpose(0, 2, 1, 3).reshape(-1, D)

    r = np.arange(P)
    qkv, bqkv = np.asarray(i["L0_attn_w_qkv"]), np.asarray(i["L0_attn_b_qkv"])
    c = {
        "ident": np.eye(P, dtype=f),
        "headmask": (r[:, None] % 32 // DH == np.arange(HG)[None, :]).astype(f),
        "A_wq": qkv[0:D].T, "A_wk": qkv[D:2 * D].T, "A_wv": even_odd(qkv[2 * D:].T),
        "A_bq": col(bqkv[0:D]), "A_bk": col(bqkv[D:2 * D]), "A_bv": over(even_odd(bqkv[2 * D:])),
        "gamma": col(i["L0_attn_ln_gamma"]), "beta": col(i["L0_attn_ln_beta"]),
    }

    def grouped(a):
        a = np.asarray(a)
        a = a.reshape(4, 1, DH, *a.shape[1:])
        return np.repeat(a, 4, axis=1).reshape(P, *a.shape[3:])

    c.update({
        "B_wq": np.asarray(i["L0_xattn_w_q"]).T, "B_wk": grouped(i["L0_xattn_w_k"]).T, "B_wv": even_odd(grouped(i["L0_xattn_w_v"]).T),
        "B_bq": col(i["L0_xattn_b_q"]), "B_bk": col(grouped(i["L0_xattn_b_k"])), "B_bv": over(even_odd(grouped(i["L0_xattn_b_v"]))),
        "B_wo": np.asarray(i["L0_xattn_w_o"]).T, "B_bo": over(i["L0_xattn_b_o"]),
    })
    def experts(a):
        return np.asarray(a).reshape(E8 * FI, D).T

    lw = np.arange(4)
    c.update({
        "C_gate": i["L0_ffn_gate_w"].T, "C_lb": over(i["L0_ffn_lb_bias"]),
        "C_wg": np.concatenate([experts(i["L0_ffn_expert_gate_w"]), i["L0_ffn_shared_gate_w"].T], axis=1),
        "C_wu": np.concatenate([experts(i["L0_ffn_expert_up_w"]), i["L0_ffn_shared_up_w"].T], axis=1),
        "C_wd": np.concatenate([i["L0_ffn_expert_down_w"].transpose(0, 2, 1).reshape(4, P, D).transpose(1, 0, 2).reshape(P, 4 * D),
                                i["L0_ffn_shared_down_w"].T], axis=1),
        "C_first": over(np.arange(E8, 0, -1).astype(f)),
        "C_sel": rows((np.arange(E8)[:, None, None] == 2 * lw[None, :, None] + (r // 64)[None, None, :]).astype(f).reshape(E8, 4 * P)),
    })
    kqv, bkqv = i["L1_attn_Wkqv"], i["L1_attn_bkqv"]
    c.update({
        "D_wk": kqv[:, :, 0:D].transpose(1, 0, 2).reshape(D, H * D), "D_wq": kqv[:, :, D:2 * D].transpose(1, 0, 2).reshape(D, H * D),
        "D_wv": even_odd(kqv[:, :, 2 * D:].transpose(1, 0, 2).reshape(D, D)),
        "D_bk": bkqv[:, 0:D].T, "D_bq": bkqv[:, D:2 * D].T, "D_bv": over(even_odd(bkqv[:, 2 * D:].reshape(1, D))),
        "D_wo": i["L1_attn_Wp"], "D_bo": over(i["L1_attn_bp"]),
        "D_causal": np.where(np.arange(S)[None, :] <= (r % S)[:, None], 0.0, -1e30).astype(f),
    })
    featsel = np.zeros((P, 2, 3, 3), f)
    for b in range(2):
        for n, v in enumerate((1 / S / DH ** 0.5, 1 / S / DH ** 0.5, 1 / S)):
            featsel[64 * b:64 * b + 64, b, n, n] = v
    c.update({
        "E_wq": i["L1_xattn_Wq"].T, "E_wk": i["L1_xattn_Wk"].T, "E_wv": even_odd(i["L1_xattn_Wv"].T),
        "E_bq": col(i["L1_xattn_bq"]), "E_bk": col(i["L1_xattn_bk"]), "E_bv": over(even_odd(i["L1_xattn_bv"])),
        "E_wo": i["L1_xattn_Wo"].T, "E_bo": over(i["L1_xattn_bo"]),
        "E_w1": rows(i["L1_xattn_w1"].T), "E_b1": col(i["L1_xattn_b1"]), "E_w2": rows(i["L1_xattn_w2"].T),
        "E_b2": col(i["L1_xattn_b2"]), "E_w3": rows(np.repeat(i["L1_xattn_w3"].T, 64, axis=1)), "E_b3": over(i["L1_xattn_b3"]),
        "E_headblk": (r[:, None] // DH == np.arange(H)[None, :]).astype(f), "E_featsel": featsel.reshape(P, 18),
        "F_w1": i["L1_ffn_w1"].T, "F_cw": over(i["L1_ffn_conv_w"][:, 0, :].T), "F_cb": over(i["L1_ffn_conv_b"]),
        "F_w2": i["L1_ffn_w2"].T.reshape(HC, P, D).transpose(1, 0, 2).reshape(P, HC * D),
    })
    return c


def kernel(**inputs):
    import concourse.bacc as bacc
    from concourse.bass_utils import run_bass_kernel_spmd

    nc = bacc.Bacc("TRN2", target_bir_lowering=False, num_devices=1)
    i = {k: np.asarray(v) for k, v in inputs.items()}
    c = layouts(i)
    arrays = {
        "x_tiles": np.ascontiguousarray(i["x"].reshape(TILES, P, D).transpose(1, 0, 2).reshape(P, TILES * D)),
        "ctx_T": np.ascontiguousarray(i["ctx_1024"].reshape(B * S, D).T),
    }
    for pack, parts in PACKS.items():
        if pack in STAGES:
            arrays["weights_" + pack] = np.ascontiguousarray(np.concatenate([c[n] for n, _ in parts], axis=1))
    dram = {n: nc.dram_tensor(n, a.shape, mybir.dt.from_np(a.dtype), kind="ExternalInput").ap() for n, a in arrays.items()}
    out = nc.dram_tensor("out_tiles", (P, TILES * D), F32, kind="ExternalOutput").ap()
    build(nc, dram["x_tiles"], dram["ctx_T"], {p: dram["weights_" + p] for p in PACKS if p in STAGES}, out)
    r = run_bass_kernel_spmd(nc, [arrays], core_ids=[0])
    got = r.results[0]["out_tiles"]
    return got.reshape(P, TILES, D).transpose(1, 0, 2).reshape(B, S, D)
```

```python
from collections import namedtuple
from contextlib import ExitStack

import numpy as np

import concourse.bass as bass
from concourse import mybir

F32 = mybir.dt.float32
BF16 = mybir.dt.bfloat16
I32 = mybir.dt.int32
ALU = mybir.AluOpType
ACT = mybir.ActivationFunctionType
AX = mybir.AxisListType

B, S, D = 32, 64, 128
H, DH = 16, 8
P = 128
TILES = B * S // P
PAIRS = TILES // 2
TOK = 2 * P
PB = TOK // S
G = 4
HG = H // G
UNIT = 2 * HG * S
VW = DH + 1
E8, FI = 8, 64
FC = 5
EPS = 1e-5
HID = 512
HC = HID // P
MLP = 64
ROUND = 1.5 * 2.0 ** 23

PACKS = {
    "A": [("ident", P), ("headmask", HG), ("groupmask", G), ("A_wq", D), ("A_wk", D), ("A_wv", D),
          ("A_bq", 1), ("A_bk", 1), ("A_bv", D), ("gamma", 1), ("beta", 1)],
    "B": [("B_wq", D), ("B_wk", D), ("B_wv", D), ("B_bq", 1), ("B_bk", 1), ("B_bv", D), ("B_wo", D), ("B_bo", D)],
    "C": [("C_gate", E8), ("C_lb", E8), ("C_wg", FC * P), ("C_wu", FC * P), ("C_wd", FC * D),
          ("C_first", E8), ("C_sel", 4 * P)],
    "D": [("D_wqT", H * D), ("D_wkT", H * D), ("D_wv", D), ("D_bq", H), ("D_bk", H), ("D_bv", D),
          ("D_wo", D), ("D_bo", D), ("D_causal", S)],
    "E": [("E_wq", D), ("E_wk", D), ("E_wv", D), ("E_bq", 1), ("E_bk", 1), ("E_bv", D), ("E_wo", D), ("E_bo", D),
          ("E_w1", MLP), ("E_b1", 1), ("E_w2", MLP), ("E_b2", 1), ("E_w3", 64), ("E_b3", 1),
          ("E_headblk", H), ("E_featsel", 18)],
    "F": [("F_w1", HID), ("F_cw", 3 * HID), ("F_cb", HID), ("F_w2", HC * D)],
}


def named(things):
    return namedtuple("Named", list(things))(*things.values())


class Signal:

    def __init__(self, sem, base=0):
        self.sem, self.base = sem, base

    def at(self, n):
        return self.base + (max(n, 0) if isinstance(n, int) else n)


def offsets():
    at, width = {}, {}
    for pack, parts in PACKS.items():
        n = 0
        for name, w in parts:
            at[name] = (pack, n, w)
            n += w
        width[pack] = n
    return at, width


STAGES = "ABCDEF"


def build(nc, x_in, ctx_in, packs_in, out):
    at, width = offsets()
    with ExitStack() as ctx:
        def sb(name, shape, dt=F32):
            return ctx.enter_context(nc.sbuf_tensor(name, shape, dt))

        def sems(stage, names):
            return named({n: Signal(ctx.enter_context(nc.semaphore(f"{stage}_{n}"))) for n in names.split()})

        shared, counted = {}, {}

        def signals(per_pair, prefix=""):
            out = {}
            for item in per_pair.split():
                name, n = item.split(":")
                name = prefix + name
                if name not in shared:
                    shared[name], counted[name] = ctx.enter_context(nc.semaphore(name)), 0
                out[name] = Signal(shared[name], counted[name])
                counted[name] += int(n) * PAIRS
            return named({name[len(prefix):]: signal for name, signal in out.items()})

        def bc(ap, axis, n):
            a = ap.unsqueeze(axis)
            shape = list(a.shape)
            shape[axis] = n
            return a.broadcast_to(shape)

        wt = {p: sb(f"w_{p}", [P, n]) for p, n in width.items() if p in STAGES}

        def w(name, rows=P):
            pack, o, n = at[name]
            return wt[pack][0:rows, o:o + n]

        x = sb("x", [P, TILES, D])
        ones = sb("ones", [P, P])
        xm = sb("xm", [P, 2, D])
        xn = sb("xn", [P, 2, D])
        stats = sb("stats", [P, 2, 6])
        carrier = sb("carrier", [P, 1])
        mv = sb("mv", [P, 2, 2])
        vareps = sb("vareps", [P, 2, 1])
        rstd = sb("rstd", [P, 2, 1])
        minus_half = sb("minus_half", [P, 2, 1])
        xT = sb("xT", [P, TOK])
        cT = sb("cT", [P, TOK])
        vT = sb("vT", [P, TOK])
        qT = sb("qT", [P, TOK])
        keybias = sb("keybias", [P, HG])
        querybias = sb("querybias", [P, G])
        qx = sb("qx", [P, G, TOK])
        kx = sb("kx", [P, HG, TOK])
        vbd = sb("vbd", [P, PB, H // 2, 2, VW])
        rowmax = sb("rowmax", [P, G, 2, HG])
        shifted = sb("shifted", [P, G, UNIT])
        probs = sb("probs", [P, G, UNIT])
        probsT = sb("probsT", [P, 2, 4, P])
        rsum = sb("rsum", [P, 2, H])
        heads = sb("heads", [P, 2, D])
        headsT = sb("headsT", [P, TOK])

        zeros = sb("zeros", [P, 2, D])
        isnan = sb("isnan", [P, 2, D], I32)
        qh = sb("qh", [P, 3, TOK])
        biasprod = sb("biasprod", [P, H])
        rowq = sb("rowq", [P, H])
        colq = sb("colq", [P, H])
        rowterm = sb("rowterm", [P, 2, H])
        cmask = sb("cmask", [P, 2, UNIT])
        big = sb("big", [P, TILES * H * S])
        kept = big[:].rearrange("p (t c) -> p t c", t=TILES)
        maps = big[:, FC * B * S:FC * B * S + H * D]
        hidden = big[:, 0:FC * B * S].rearrange("p (k n) -> p k n", k=FC)
        ksum = sb("ksum", [P, PB])
        bk64 = sb("bk64", [P, 1])
        ksb = sb("ksb", [P, PB, H])
        squares = sb("squares", [P, G, UNIT])
        fpair = sb("fpair", [P, 3, 2, H])
        feat = sb("feat", [P, 4, TILES, H])
        fwork = sb("fwork", [P, TILES, H])
        over_t = sb("over_t", [P, TILES, H])
        feats = sb("feats", [3, 512])
        hid1 = sb("hid1", [MLP, 512])
        hid2 = sb("hid2", [MLP, 512])
        silu = shifted[:].rearrange("p g (t n) -> p (g t) n", n=TOK)
        logits = sb("logits", [P, TILES, E8])
        key = sb("key", [P, TILES, E8])
        eq = sb("eq", [P, TILES, E8])
        hot1 = sb("hot1", [P, TILES, E8])
        hot2 = sb("hot2", [P, TILES, E8])
        score = sb("score", [P, TILES, E8])
        sel = sb("sel", [P, TILES, E8])
        tok1 = sb("tok1", [P, TILES])
        tally = sb("tally", [P, 2 * E8])
        total = sb("total", [P, 2 * E8])
        selp = sb("selp", [P, 2, E8])
        selT = sb("selT", [E8, TOK], BF16)
        selmat = sb("selmat", [E8, 4 * P], BF16)
        hm = [sb("hm", [P, FC, TOK]),
              probs[:].rearrange("p g (t n) -> p (g t) n", n=TOK)]
        wsum = sb("wsum", [P, 2])
        wmean = sb("wmean", [P, 2])
        wscale = sb("wscale", [P, 2])
        taps = big[:, 0:3 * HID].rearrange("p (k f) -> p k f", k=3)
        w2q = sb("w2q", [P, HC * D], BF16)
        identb = sb("identb", [P, P], BF16)
        amax = sb("amax", [P, 2])
        ainv = sb("ainv", [P, 2])
        xi = sb("xi", [P, 2, D])
        xs = qx[:, 0:3, :]
        hb = shifted[:, 0:2, :]
        hs = shifted[:, 2:4, :]
        hr = probs[:, 0:2, :]
        hi8 = squares[:, 0, :].bitcast(BF16).rearrange("p (t f) -> p t f", t=2)
        hT = squares[:, 1, :].bitcast(BF16).rearrange("p (t f) -> p t f", t=2)
        hmax = sb("hmax", [P, 2])
        hinv = sb("hinv", [P, 2])
        outstep = sb("outstep", [P, 2])

        psS = [ctx.enter_context(nc.psum_tensor(f"psS{i}", [P, 512], F32)) for i in range(2)]
        psT = [ctx.enter_context(nc.psum_tensor(f"psT{i}", [P, 512], F32)) for i in range(2)]
        psO = ctx.enter_context(nc.psum_tensor("psO", [P, 512], F32))
        psV = ctx.enter_context(nc.psum_tensor("psV", [P, 512], F32))
        tokensT = [xT, headsT]
        scorebank = [psS[0], psS[1], None]
        psK = ctx.enter_context(nc.psum_tensor("psK", [P, 512], F32))
        psQ = ctx.enter_context(nc.psum_tensor("psQ", [P, 512], F32))
        scorebank[2] = psQ
        hiddenbank = [psS[0], psS[1], psQ, psT[0], psT[1]]
        maskbank = [psS[0], psS[1], psT[0], psT[1]]
        downbank = [psV, psQ]
        psTb = [t[:, :].bitcast(BF16) for t in psT]
        O = psO[:, 0:2 * H * VW].rearrange("p (a h v) -> p a h v", a=2, h=H)

        load = sems("load", "x A B C D E F out")
        loads = {"A": load.A, "B": load.B, "C": load.C, "D": load.D, "E": load.E, "F": load.F}
        init = sems("init", "pool")
        ident = w("ident")

        def pair(t, j):
            return t[:, bass.ds(2 * j, 2), :]

        def tile_of(t, j):
            if isinstance(j, int):
                return lambda a: t[:, 2 * j + a, :]
            return lambda a: t[:, bass.ds(2 * j + a, 1), :].rearrange("p o d -> p (o d)")

        def norm_stats(dve, n, j, src, freed, count):
            for a in range(2):
                nc.vector.bn_stats(stats[:, a, :], src(a)).then_inc(n.stats.sem, 1)
            dve.wait_ge(n.stats.sem, n.stats.at(2 * j + 2))
            nc.vector.memset(carrier[:], 0.0)
            for a in range(2):
                nc.vector.bn_aggr(mv[:, a, :], stats[:, a, :]).then_inc(n.aggr.sem, 1)
            dve.wait_ge(n.aggr.sem, n.aggr.at(2 * j + 2))
            dve.wait_ge(freed.sem, freed.at(count))
            nc.vector.tensor_scalar(vareps[:], mv[:, :, 1:2], EPS, None, ALU.add).then_inc(n.vareps.sem, 1)

        def norm_rstd(pool, n, j, freed, count):
            pool.wait_ge(n.vareps.sem, n.vareps.at(j + 1))
            pool.wait_ge(freed.sem, freed.at(count))
            nc.gpsimd.tensor_tensor(rstd[:], vareps[:], minus_half[:], ALU.pow).then_inc(n.rstd.sem, 1)

        def norm_apply(dve, n, j, src, dst, freed, count):
            dve.wait_ge(n.rstd.sem, n.rstd.at(j + 1))
            dve.wait_ge(freed.sem, freed.at(count))
            for a in range(2):
                nc.vector.tensor_scalar(dst[:, a, :], src(a), mv[:, a, 0:1], rstd[:, a, :],
                                        ALU.subtract, ALU.mult).then_inc(n.normed.sem, 1)

        def norm_signals(prefix=""):
            return signals("stats:2 aggr:2 vareps:1 rstd:1 normed:2 xT_ps:1", prefix)

        def attention(st, wst=None, affine=False, cross=False, wide=False, out_proj=True, scale=DH ** -0.5,
                      queries=True, values=True, guard=False):
            n = norm_signals() if queries else None
            n0 = norm_signals("first_") if affine else None
            s = signals(f"shift:{G} exp:{G} "
                          + ("xT:1 rowmax:4 " + ("q_ps:16 q:16 scores:16 row_ps:1 row:1 cmask:4 " if wide else
                                                 "k_ps:1 q:4 k:4 scores:4 ")) * queries
                          + f"v_ps:1 v:2 tr:{G} pT:{G} pv:{G} recip:1 heads:1 res:1 " * values
                          + "headsT_ps:1 headsT:1 out_ps:1 " * out_proj + "ctx:16 " * cross + "vctx:16 " * (cross and values)
                          + f"masked:{G} " * wide + "nans:2 " * guard)
            projected = (s.scores, H) if wide else (s.k_ps if cross and queries else s.v_ps, 1)
            return named(dict(st=st, w=wst or st, affine=affine, cross=cross, wide=wide, out_proj=out_proj, scale=scale,
                              queries=queries, values=values, guard=guard, n=n, n0=n0, s=s, projected=projected,
                              tbank=(lambda g: 0) if wide else (lambda g: g % 2)))

        def pe_tokens_transposed(pe, a, j):
            n, s = a.n, a.s
            pe.wait_ge(n.normed.sem, n.normed.at(2 * j + 2))
            if a.wide:
                pe.wait_ge(s.q.sem, s.q.at(H * j))
            else:
                pe.wait_ge(s.k.sem, s.k.at(HG * j))
            if a is E1:
                pe.wait_ge(e.ksum.sem, e.ksum.at(j))
            for t in range(2):
                last = nc.tensor.transpose(psK[:, t * P:(t + 1) * P], xn[:, t, :], ident)
            last.then_inc(n.xT_ps.sem, 1)

        def pe_queries(pe, a, j):
            s = a.s
            pe.wait_ge(s.xT.sem, s.xT.at(j + 1))
            if a.wide:
                pe.wait_ge(s.pT.sem, s.pT.at(G * (j - 1)))
                pe.wait_ge(s.row.sem, s.row.at(j))
                for t in range(2):
                    o = psT[0][:, t * H:(t + 1) * H]
                    nc.tensor.matmul(o, xT[:, t * P:(t + 1) * P], rowq[:], start=True, stop=False)
                    last = nc.tensor.matmul(o, ones[:], biasprod[:], start=False, stop=True)
                last.then_inc(s.row_ps.sem, 1)
                return
            nc.tensor.matmul(psK[:, 0:TOK], w(a.w + "_wq"), xT[:], start=True, stop=True)
            if a.cross:
                pe.wait_ge(s.ctx.sem, s.ctx.at(16 * j + 16))
            nc.tensor.matmul(psK[:, TOK:2 * TOK], w(a.w + "_wk"), (cT if a.cross else xT)[:], start=True,
                             stop=True).then_inc(s.k_ps.sem, 1)

        def pe_front(pe, a, j):
            if a.queries:
                pe_tokens_transposed(pe, a, j)
                pe_queries(pe, a, j)

        def pe_value_projection(pe, a, j):
            s = a.s
            pe.wait_ge(s.v.sem, s.v.at(2 * j))
            if a.out_proj:
                pe.wait_ge(s.res.sem, s.res.at(j - 1))
            if a.cross:
                pe.wait_ge(s.vctx.sem, s.vctx.at(16 * j + 16))
            for b in range(PB):
                for e in range(2):
                    last = nc.tensor.matmul(psV[64 * e:64 * e + 64, b * 64:b * 64 + 64], (vT if a.cross else xT)[:, b * S:(b + 1) * S],
                                            w(a.w + "_wv")[:, 64 * e:64 * e + 64], start=True, stop=True)
            last.then_inc(s.v_ps.sem, 1)

        def act_tokens(act, a, j):
            n, s = a.n, a.s
            act.wait_ge(n.xT_ps.sem, n.xT_ps.at(j + 1))
            act.wait_ge(a.projected[0].sem, a.projected[0].at(a.projected[1] * j))
            if a.affine:
                nc.scalar.activation(xT[:], psK[:, 0:TOK], ACT.Identity, bias=w("beta"), scale=w("gamma")).then_inc(s.xT.sem, 1)
            else:
                nc.scalar.activation(xT[:], psK[:, 0:TOK], ACT.Copy).then_inc(s.xT.sem, 1)

        def act_queries(act, a, j, units=range(G)):
            s = a.s
            if isinstance(j, int) and j == 0:
                act.wait_ge(kb[a.st].sem, kb[a.st].at(2))
            act.wait_ge(s.k_ps.sem, s.k_ps.at(j + 1))
            for g in units:
                act.wait_ge(s.scores.sem, s.scores.at(G * j + g - 3))
                nc.scalar.activation(qx[:, g, :], psK[:, 0:TOK], ACT.Identity, bias=querybias[:, g:g + 1],
                                     scale=w("groupmask")[:, g:g + 1]).then_inc(s.q.sem, 1)
            if a is E1:
                act.wait_ge(e.mean_ps.sem, e.mean_ps.at(j))
                nc.scalar.activation(qT[:], psK[:, 0:TOK], ACT.Identity, bias=w(a.w + "_bq")).then_inc(e.q.sem, 1)

        def act_keys(act, a, j):
            s = a.s
            act.wait_ge(s.k_ps.sem, s.k_ps.at(j + 1))
            act.wait_ge(s.scores.sem, s.scores.at(G * j))
            for h in range(HG):
                nc.scalar.activation(kx[:, h, :], psK[:, TOK:2 * TOK], ACT.Identity, bias=keybias[:, h:h + 1],
                                     scale=w("headmask")[:, h:h + 1]).then_inc(s.k.sem, 1)

        def dve_values(dve, a, j):
            s = a.s
            dve.wait_ge(s.v_ps.sem, s.v_ps.at(j + 1))
            dve.wait_ge(s.pv.sem, s.pv.at(G * j))
            v = psV[:, 0:PB * 64].rearrange("p (b q d) -> p b q d", b=PB, d=DH)
            bias = w(a.w + "_bv").rearrange("p (e q d) -> p e q d", e=2, d=DH)
            for e in range(2):
                r = slice(64 * e, 64 * e + 64)
                nc.vector.tensor_tensor(vbd[r, :, :, e, 0:DH], v[r, :, :, :], bc(bias[r, e, :, :], 1, PB),
                                        ALU.add).then_inc(s.v.sem, 1)

        def pe_scores(pe, a, j, units):
            s = a.s
            pe.wait_ge(s.q.sem, s.q.at(G * j + units[-1] + 1))
            pe.wait_ge(s.k.sem, s.k.at(HG * j + HG))
            pe.wait_ge(s.shift.sem, s.shift.at(G * j + max(units[-1] - 2, 0)))
            for g in units:
                for b in range(PB):
                    o = 64 * (b % 2)
                    last = nc.tensor.matmul(scorebank[g % 3][o:o + 64, (b // 2) * 256:(b // 2) * 256 + 256],
                                            qx[:, g, b * S:(b + 1) * S], kx[:, :, b * S:(b + 1) * S], start=True, stop=True)
                    if b == PB - 1:
                        last.then_inc(s.scores.sem, 1)

        def dve_rowmax(dve, a, j, g):
            s = a.s
            if a is E1 and g == 0:
                dve.wait_ge(e.kept.sem, e.kept.at(j))
            dve.wait_ge(s.scores.sem, s.scores.at(G * j + g + 1))
            nc.vector.tensor_reduce(rowmax[:, g, :, :].rearrange("p t h -> p (t h)"),
                                    scorebank[g % 3][:, :].rearrange("p (r m) -> p r m", m=S), AX.X, ALU.max).then_inc(s.rowmax.sem, 1)

        def dve_shift(dve, a, j, g):
            s = a.s
            dve.wait_ge(s.rowmax.sem, s.rowmax.at(G * j + g + 1))
            dve.wait_ge(s.exp.sem, s.exp.at(G * j + g - 3))
            if a is E1:
                dve.wait_ge(e_stored[g].sem, e_stored[g].at(16 * j))
            nc.vector.tensor_tensor(shifted[:, g, :].rearrange("p (r m) -> p r m", m=S),
                                    scorebank[g % 3][:, :].rearrange("p (r m) -> p r m", m=S),
                                    bc(rowmax[:, g, :, :].rearrange("p t h -> p (t h)"), 2, S), ALU.subtract).then_inc(s.shift.sem, 1)

        def act_exp(act, a, j, g):
            s = a.s
            act.wait_ge(s.shift.sem, s.shift.at(G * j + g + 1))
            if a is E1:
                act.wait_ge(e.z.sem, e.z.at(G * j + g - 3))
                act.wait_ge(e.sq.sem, e.sq.at(G * j + g - 3))
            else:
                act.wait_ge(s.tr.sem, s.tr.at(G * j + g - 3))
            nc.scalar.activation(probs[:, g, :], shifted[:, g, :], ACT.Exp, scale=a.scale).then_inc(s.exp.sem, 1)

        def pe_transpose(pe, a, j, g):
            s = a.s
            pe.wait_ge(s.exp.sem, s.exp.at(G * j + g + 1))
            for k in range(4):
                last = nc.tensor.transpose(psT[a.tbank(g)][:, k * P:(k + 1) * P], probs[:, g, k * P:(k + 1) * P], ident)
            last.then_inc(s.tr.sem, 1)

        def act_probsT(act, a, j, g):
            s = a.s
            act.wait_ge(s.tr.sem, s.tr.at(G * j + g + 1))
            nc.scalar.activation(probsT[:, g % 2, :, :].rearrange("p k n -> p (k n)"), psT[a.tbank(g)][:, :],
                                 ACT.Copy).then_inc(s.pT.sem, 1)

        def pe_values(pe, a, j, g):
            s = a.s
            if g == 0:
                pe.wait_ge(s.v.sem, s.v.at(2 * j + 2))
                pe.wait_ge(s.heads.sem, s.heads.at(j))
            pe.wait_ge(s.pT.sem, s.pT.at(G * j + g + 1))
            for t in range(2):
                for q in range(2):
                    hp = 2 * g + q
                    for b in range(2):
                        last = nc.tensor.matmul(O[64 * b:64 * b + 64, t, 2 * hp:2 * hp + 2, :],
                                                probsT[:, g % 2, 2 * t + q, 64 * b:64 * b + 64],
                                                vbd[:, 2 * t + b, hp, :, :], start=True, stop=True)
            last.then_inc(s.pv.sem, 1)

        def dve_reciprocal(dve, a, j):
            s = a.s
            dve.wait_ge(s.pv.sem, s.pv.at(G * j + G))
            nc.vector.reciprocal(rsum[:, :, :], O[:, :, :, DH]).then_inc(s.recip.sem, 1)

        def dve_heads(dve, a, j):
            s = a.s
            dve.wait_ge(s.recip.sem, s.recip.at(j + 1))
            if a.out_proj:
                dve.wait_ge(s.headsT_ps.sem, s.headsT_ps.at(j))
            for t in range(2):
                ins = nc.vector.tensor_tensor(heads[:, t, :].rearrange("p (h d) -> p h d", h=H), O[:, t, :, 0:DH],
                                              bc(rsum[:, t, :], 2, DH), ALU.mult)
            if not a.guard:
                ins.then_inc(s.heads.sem, 1)
                return
            ins.then_inc(s.nans.sem, 1)
            dve.wait_ge(s.nans.sem, s.nans.at(2 * j + 1))
            nc.vector.tensor_tensor(isnan[:], heads[:], heads[:], ALU.not_equal).then_inc(s.nans.sem, 1)
            dve.wait_ge(s.nans.sem, s.nans.at(2 * j + 2))
            nc.vector.memset(carrier[:], 0.0)
            nc.vector.copy_predicated(heads[:], isnan[:], zeros[:]).then_inc(s.heads.sem, 1)

        def pe_headsT(pe, a, j, more=True):
            s = a.s
            pe.wait_ge(s.heads.sem, s.heads.at(j + 1))
            pe.wait_ge(s.v.sem, s.v.at(2 * j + (4 if more else 2)))
            for t in range(2):
                last = nc.tensor.transpose(psV[:, TOK + t * P:TOK + (t + 1) * P], heads[:, t, :], ident)
            last.then_inc(s.headsT_ps.sem, 1)

        def pe_out(pe, a, j):
            s = a.s
            pe.wait_ge(s.headsT.sem, s.headsT.at(j + 1))
            for t in range(2):
                o = psV[:, TOK + t * D:TOK + (t + 1) * D]
                nc.tensor.matmul(o, headsT[:, t * P:(t + 1) * P], w(a.w + "_wo"), start=True, stop=False)
                last = nc.tensor.matmul(o, ones[0:1, 0:P], w(a.w + "_bo")[0:1, :], start=False, stop=True)
            last.then_inc(s.out_ps.sem, 1)

        def act_headsT(act, a, j):
            s = a.s
            act.wait_ge(s.headsT_ps.sem, s.headsT_ps.at(j + 1))
            act.wait_ge(s.out_ps.sem, s.out_ps.at(j))
            nc.scalar.activation(headsT[:], psV[:, TOK:2 * TOK], ACT.Copy).then_inc(s.headsT.sem, 1)

        def dve_residual(dve, a, j):
            s = a.s
            if a.out_proj:
                dve.wait_ge(s.out_ps.sem, s.out_ps.at(j + 1))
                add = psV[:, TOK:2 * TOK].rearrange("p (t d) -> p t d", t=2)
            else:
                dve.wait_ge(s.heads.sem, s.heads.at(j + 1))
                add = heads[:]
            nc.vector.tensor_tensor(pair(x, j), add, pair(x, j), ALU.add).then_inc(s.res.sem, 1)

        slots = [psK[:, 0:TOK], psQ[:, 0:TOK], psT[1][:, 0:TOK]]

        def maps_dve(dve):
            nc.vector.tensor_tensor(biasprod[:], w("D_bq"), w("D_bk"), ALU.mult).then_inc(d.maps.sem, 1)
            dve.wait_ge(d.maps_ps.sem, d.maps_ps.at(1))
            nc.vector.tensor_copy(rowq[:], psV[:, 0:H]).then_inc(d.maps.sem, 1)
            nc.vector.tensor_copy(colq[:], psV[:, H:2 * H]).then_inc(d.maps.sem, 1)

        def maps_pe(pe):
            if "C" in STAGES:
                pe.wait_ge(c.res.sem, c.res.at(PAIRS))
            for h in range(H):
                col = slice(h * D, (h + 1) * D)
                nc.tensor.matmul(psV[:, h:h + 1], w("D_wqT")[:, col], w("D_bk")[:, h:h + 1], start=True, stop=True)
                last = nc.tensor.matmul(psV[:, H + h:H + h + 1], w("D_wkT")[:, col], w("D_bq")[:, h:h + 1], start=True, stop=True)
            last.then_inc(d.maps_ps.sem, 1)
            for k in range(4):
                for h in range(4 * k, 4 * k + 4):
                    col = slice(h * D, (h + 1) * D)
                    last = nc.tensor.matmul(mapbank[k][:, (h - 4 * k) * D:(h - 4 * k + 1) * D], w("D_wqT")[:, col], w("D_wkT")[:, col],
                                            start=True, stop=True)
                last.then_inc(d.maps_ps.sem, 1)
            pe.wait_ge(d.maps.sem, d.maps.at(3))
            pe.wait_ge(d.inplace.sem, d.inplace.at(4))

        def maps_act(act):
            for k in range(4):
                act.wait_ge(d.maps_ps.sem, d.maps_ps.at(k + 2))
                nc.scalar.activation(maps[:, k * 512:(k + 1) * 512], mapbank[k][:, :], ACT.Copy).then_inc(d.inplace.sem, 1)
            act.wait_ge(d.maps.sem, d.maps.at(3))

        def pe_project(pe, a, j, h):
            s = a.s
            pe.wait_ge(s.q.sem, s.q.at(H * j + max(h - 2, 0)))
            nc.tensor.matmul(slots[h % 3], maps[:, h * D:(h + 1) * D], xT[:], start=True, stop=True).then_inc(s.q_ps.sem, 1)

        def pe_wide_scores(pe, a, j, g):
            s = a.s
            for h in range(HG * g, HG * g + HG):
                if h + 2 < H:
                    pe_project(pe, a, j, h + 2)
                pe.wait_ge(s.q.sem, s.q.at(H * j + h + 1))
                if h == HG * g:
                    pe.wait_ge(s.masked.sem, s.masked.at(G * j + g - 1))
                for b in range(PB):
                    o, c = 64 * (b % 2), (b // 2) * 256 + (h % HG) * S
                    last = nc.tensor.matmul(psS[g % 2][o:o + 64, c:c + S], qh[:, h % 3, b * S:(b + 1) * S],
                                            xT[:, b * S:(b + 1) * S], start=True, stop=True)
                last.then_inc(s.scores.sem, 1)

        def act_wide_queries(act, a, j, heads_):
            s = a.s
            for h in heads_:
                act.wait_ge(s.q_ps.sem, s.q_ps.at(H * j + h + 1))
                act.wait_ge(s.scores.sem, s.scores.at(H * j + h - 2))
                nc.scalar.activation(qh[:, h % 3, :], slots[h % 3], ACT.Identity, bias=colq[:, h:h + 1]).then_inc(s.q.sem, 1)

        def act_rowterm(act, a, j):
            s = a.s
            act.wait_ge(s.row_ps.sem, s.row_ps.at(j + 1))
            act.wait_ge(s.cmask.sem, s.cmask.at(G * j))
            nc.scalar.activation(rowterm[:].rearrange("p t h -> p (t h)"), psT[0][:, 0:2 * H], ACT.Copy).then_inc(s.row.sem, 1)

        def pool_cmask(pool, a, j):
            s = a.s
            pool.wait_ge(s.row.sem, s.row.at(j + 1))
            for g in range(G):
                pool.wait_ge(s.masked.sem, s.masked.at(G * j + g - 1))
                nc.gpsimd.tensor_tensor(cmask[:, g % 2, :].rearrange("p (t h m) -> p t h m", t=2, m=S),
                                        bc(bc(w("D_causal"), 1, HG), 1, 2),
                                        bc(rowterm[:, :, HG * g:HG * g + HG], 3, S), ALU.add).then_inc(s.cmask.sem, 1)

        def dve_wide_softmax(dve, a, j, g):
            s = a.s
            sh = shifted[:, g, :].rearrange("p (r m) -> p r m", m=S)
            mx = rowmax[:, g, :, :].rearrange("p t h -> p (t h)")
            dve.wait_ge(s.scores.sem, s.scores.at(H * j + HG * g + HG))
            dve.wait_ge(s.cmask.sem, s.cmask.at(G * j + g + 1))
            dve.wait_ge(s.exp.sem, s.exp.at(G * j + g - 3))
            nc.vector.tensor_tensor(shifted[:, g, :], psS[g % 2][:, :], cmask[:, g % 2, :], ALU.add).then_inc(s.masked.sem, 1)
            dve.wait_ge(s.masked.sem, s.masked.at(G * j + g + 1))
            nc.vector.tensor_reduce(mx, sh, AX.X, ALU.max).then_inc(s.rowmax.sem, 1)
            dve.wait_ge(s.rowmax.sem, s.rowmax.at(G * j + g + 1))
            nc.vector.tensor_tensor(sh, sh, bc(mx, 2, S), ALU.subtract).then_inc(s.shift.sem, 1)

        def dve_keysum(dve, a, j):
            s = a.s
            dve.wait_ge(s.k.sem, s.k.at(HG * j + HG))
            nc.vector.tensor_reduce(ksum[:], psK[:, TOK:2 * TOK].rearrange("p (b m) -> p b m", m=S), AX.X, ALU.add).then_inc(e.ksum.sem, 1)
            dve.wait_ge(e.ksum.sem, e.ksum.at(j + 1))
            dve.wait_ge(e.mean_ps.sem, e.mean_ps.at(j))
            nc.vector.scalar_tensor_tensor(out=ksb[:], in0=bc(ksum[:], 2, H), scalar=bk64[:], in1=bc(w("E_headblk"), 1, PB),
                                           op0=ALU.add, op1=ALU.mult).then_inc(e.ksb.sem, 1)

        def pe_means(pe, a, j):
            s = a.s
            pe.wait_ge(e.ksb.sem, e.ksb.at(j + 1))
            pe.wait_ge(e.q.sem, e.q.at(j + 1))
            pe.wait_ge(e.mean.sem, e.mean.at(j))
            for b in range(PB):
                o = 64 * (b % 2)
                last = nc.tensor.matmul(psO[o:o + 64, (b // 2) * H:(b // 2 + 1) * H], qT[:, b * S:(b + 1) * S], ksb[:, b, :],
                                        start=True, stop=True)
            last.then_inc(e.mean_ps.sem, 1)

        def dve_means(dve, a, j):
            dve.wait_ge(e.mean_ps.sem, e.mean_ps.at(j + 1))
            nc.vector.tensor_scalar(feat[:, 0, bass.ds(2 * j, 2), :], psO[:, 0:2 * H].rearrange("p (t h) -> p t h", h=H),
                                    1.0 / S, None, ALU.mult).then_inc(e.mean.sem, 1)

        def act_squares(act, a, j, g):
            s = a.s
            act.wait_ge(s.exp.sem, s.exp.at(G * j + g + 1))
            act.wait_ge(e.z2.sem, e.z2.at(G * j + g - 3))
            nc.scalar.activation(squares[:, g, :], probs[:, g, :], ACT.Square).then_inc(e.sq.sem, 1)

        def dve_sums(dve, a, j, g):
            s = a.s
            h4 = slice(HG * g, HG * g + HG)
            if g == 0:
                dve.wait_ge(e.kept.sem, e.kept.at(j))
            dve.wait_ge(s.exp.sem, s.exp.at(G * j + g + 1))
            nc.vector.tensor_reduce(fpair[:, 1, :, h4], probs[:, g, :].rearrange("p (t h m) -> p t h m", t=2, m=S), AX.X, ALU.add).then_inc(e.z.sem, 1)
            dve.wait_ge(e.sq.sem, e.sq.at(G * j + g + 1))
            nc.vector.tensor_reduce(fpair[:, 2, :, h4], squares[:, g, :].rearrange("p (t h m) -> p t h m", t=2, m=S), AX.X, ALU.add).then_inc(e.z2.sem, 1)

        def dve_keep(dve, a, j):
            dve.wait_ge(e.z2.sem, e.z2.at(G * j + G))
            dve.wait_ge(e.z.sem, e.z.at(G * j + G))
            nc.vector.tensor_scalar(feat[:, 2:4, bass.ds(2 * j, 2), :], fpair[:, 1:3, :, :], 1.0, None, ALU.mult).then_inc(e.kept2.sem, 1)
            nc.vector.tensor_scalar(feat[:, 1, bass.ds(2 * j, 2), :].rearrange("p t (g h) -> p t g h", h=HG),
                                    rowmax[:].rearrange("p g t h -> p t g h"), 1.0, None, ALU.mult).then_inc(e.kept.sem, 1)

        def dve_kept_softmax(dve, a, j, g):
            s = a.s
            if isinstance(j, int) and j == 0:
                dve.wait_ge(e_stored[g].sem, e_stored[g].at(16 * PAIRS))
            dve.wait_ge(s.exp.sem, s.exp.at(G * j + g - 3))
            nc.vector.tensor_tensor(shifted[:, g, :].rearrange("p (t h m) -> p t h m", t=2, m=S),
                                    kept[:, bass.ds(2 * j, 2), g * 256:(g + 1) * 256].rearrange("p t (h m) -> p t h m", m=S),
                                    bc(over_t[:, bass.ds(2 * j, 2), HG * g:HG * g + HG], 3, S), ALU.mult).then_inc(s.shift.sem, 1)

        def temperature_dve(dve):
            z, p2, r = feat[:, 2, :, :], feat[:, 3, :, :], fwork[:]
            dve.wait_ge(e.kept.sem, e.kept.at(PAIRS))
            nc.vector.reciprocal(r, z).then_inc(e.v.sem, 1)
            dve.wait_ge(e.v.sem, e.v.at(1))
            nc.vector.tensor_tensor(p2, p2, r, ALU.mult).then_inc(e.v.sem, 1)
            dve.wait_ge(e.v.sem, e.v.at(2))
            nc.vector.tensor_tensor(p2, p2, r, ALU.mult).then_inc(e.v.sem, 1)
            dve.wait_ge(e.v.sem, e.v.at(3))
            nc.vector.tensor_scalar(z, p2, 1.0 / S, 1.0 / (S - 1), ALU.subtract, ALU.mult).then_inc(e.var.sem, 1)
            dve.wait_ge(e.feat_ps.sem, e.feat_ps.at(1))
            nc.vector.tensor_copy(feats[:], psS[0][0:3, :]).then_inc(e.feats.sem, 1)
            dve.wait_ge(e.logt_ps.sem, e.logt_ps.at(1))
            lt = psT[0][:, 0:TOK].rearrange("p (t h) -> p t h", h=H)
            nc.vector.tensor_scalar(fwork[:], lt, w("E_b3"), float(np.log(0.1)), ALU.add, ALU.max).then_inc(e.v.sem, 1)
            dve.wait_ge(e.v.sem, e.v.at(4))
            nc.vector.tensor_scalar(fwork[:], fwork[:], float(np.log(10.0)), None, ALU.min).then_inc(e.logt.sem, 1)
            dve.wait_ge(e.inv_t.sem, e.inv_t.at(1))
            nc.vector.tensor_scalar(over_t[:], over_t[:], 0.5, None, ALU.mult).then_inc(e.v.sem, 1)
            dve.wait_ge(e.v.sem, e.v.at(5))

        def temperature_pe(pe):
            pe.wait_ge(e.var.sem, e.var.at(1))
            for b in range(2):
                for f in range(3):
                    last = nc.tensor.matmul(psS[0][0:3, b * 256:(b + 1) * 256], w("E_featsel")[:, 9 * b + 3 * f:9 * b + 3 * f + 3],
                                            feat[:, f, :, :].rearrange("p t h -> p (t h)"), start=(f == 0), stop=(f == 2))
            last.then_inc(e.feat_ps.sem, 1)
            pe.wait_ge(e.feats.sem, e.feats.at(1))
            nc.tensor.matmul(psS[1][0:MLP, :], w("E_w1", 3), feats[:], start=True, stop=True).then_inc(e.h_ps.sem, 1)
            pe.wait_ge(e.h.sem, e.h.at(1))
            nc.tensor.matmul(psS[0][0:MLP, :], w("E_w2", MLP), hid1[:], start=True, stop=True).then_inc(e.h_ps.sem, 1)
            pe.wait_ge(e.h.sem, e.h.at(2))
            for b in range(2):
                last = nc.tensor.matmul(psT[0][64 * b:64 * b + 64, 0:TOK], w("E_w3", MLP), hid2[:, b * 256:(b + 1) * 256],
                                        start=True, stop=True)
            last.then_inc(e.logt_ps.sem, 1)

        def temperature_act(act):
            act.wait_ge(e.h_ps.sem, e.h_ps.at(1))
            nc.scalar.activation(hid1[:], psS[1][0:MLP, :], ACT.Gelu, bias=w("E_b1", MLP)).then_inc(e.h.sem, 1)
            act.wait_ge(e.h_ps.sem, e.h_ps.at(2))
            nc.scalar.activation(hid2[:], psS[0][0:MLP, :], ACT.Gelu, bias=w("E_b2", MLP)).then_inc(e.h.sem, 1)
            act.wait_ge(e.logt.sem, e.logt.at(1))
            nc.scalar.activation(over_t[:], fwork[:], ACT.Exp, scale=-1.0).then_inc(e.inv_t.sem, 1)

        def pe_hidden_tokens(pe, j):
            pe.wait_ge(cn.normed.sem, cn.normed.at(2 * j + 2))
            pe.wait_ge(c.xT.sem, c.xT.at(j))
            for t in range(2):
                last = nc.tensor.transpose(psK[:, t * P:(t + 1) * P], xn[:, t, :], ident)
            last.then_inc(cn.xT_ps.sem, 1)

        def pe_router(pe, j, odd):
            pe.wait_ge(c.xT.sem, c.xT.at(j + 1))
            pe.wait_ge(c.logits.sem, c.logits.at(j))
            for t in range(2):
                last = nc.tensor.matmul(psO[:, t * E8:(t + 1) * E8], tokensT[odd][:, t * P:(t + 1) * P], w("C_gate"),
                                        start=True, stop=True)
            last.then_inc(c.logits_ps.sem, 1)

        def pe_hidden(pe, j, odd, chunks):
            for k in chunks:
                pe.wait_ge(c.hidden.sem, c.hidden.at(FC * j + k + 1 - FC))
                nc.tensor.matmul(hiddenbank[k][:, 0:TOK], w("C_wg")[:, k * P:(k + 1) * P], tokensT[odd][:], start=True, stop=True)
                nc.tensor.matmul(hiddenbank[k][:, TOK:2 * TOK], w("C_wu")[:, k * P:(k + 1) * P], tokensT[odd][:], start=True,
                                 stop=True).then_inc(c.gate_up.sem, 1)

        def act_hidden_tokens(act, j, odd):
            act.wait_ge(cn.xT_ps.sem, cn.xT_ps.at(j + 1))
            act.wait_ge(c.gate_up.sem, c.gate_up.at(FC * (j - 1)))
            nc.scalar.activation(tokensT[odd][:], psK[:, 0:TOK], ACT.Copy).then_inc(c.xT.sem, 1)

        def act_hidden(act, j, chunks):
            for k in chunks:
                act.wait_ge(c.gate_up.sem, c.gate_up.at(FC * j + k + 1))
                act.wait_ge(c.hidden.sem, c.hidden.at(FC * j + k + 1 - FC))
                nc.scalar.activation(silu[:, k, :], hiddenbank[k][:, 0:TOK], ACT.Silu).then_inc(c.silu.sem, 1)

        def dve_logits(dve, j):
            dve.wait_ge(c.logits_ps.sem, c.logits_ps.at(j + 1))
            nc.vector.tensor_tensor(logits[:, bass.ds(2 * j, 2), :], psO[:, 0:2 * E8].rearrange("p (t e) -> p t e", e=E8),
                                    bc(w("C_lb"), 1, 2), ALU.add).then_inc(c.logits.sem, 1)

        def dve_hidden(dve, j, chunks):
            for k in chunks:
                dve.wait_ge(c.silu.sem, c.silu.at(FC * j + k + 1))
                nc.vector.tensor_tensor(hidden[:, k, bass.ds(j * TOK, TOK)], silu[:, k, :], hiddenbank[k][:, TOK:2 * TOK],
                                        ALU.mult).then_inc(c.hidden.sem, 1)

        def route_dve(dve):
            seq = [0]

            def then(ins):
                seq[0] += 1
                ins.then_inc(c.route.sem, 1)
                dve.wait_ge(c.route.sem, c.route.at(seq[0]))

            def best(key, one):
                then(nc.vector.tensor_reduce(tok1[:], key, AX.X, ALU.max))
                then(nc.vector.tensor_tensor(eq[:], key, bc(tok1[:], 2, E8), ALU.is_equal))
                then(nc.vector.tensor_tensor(eq[:], eq[:], bc(w("C_first"), 1, TILES), ALU.mult))
                then(nc.vector.tensor_reduce(tok1[:], eq[:], AX.X, ALU.max))
                then(nc.vector.tensor_tensor(one, eq[:], bc(tok1[:], 2, E8), ALU.is_equal))

            dve.wait_ge(c.logits.sem, c.logits.at(PAIRS))
            then(nc.vector.tensor_scalar(key[:], logits[:], 17.0, None, ALU.min))
            best(key[:], hot1[:])
            then(nc.vector.scalar_tensor_tensor(out=key[:], in0=hot1[:], scalar=-1e30, in1=key[:], op0=ALU.mult, op1=ALU.add))
            best(key[:], hot2[:])
            dve.wait_ge(c.sig.sem, c.sig.at(1))
            then(nc.vector.tensor_tensor(eq[:], hot1[:], hot2[:], ALU.add))
            nc.vector.tensor_tensor(sel[:], hot1[:], hot2[:], ALU.add).then_inc(c.sel.sem, 1)
            then(nc.vector.tensor_tensor(key[:], eq[:], score[:], ALU.mult))
            then(nc.vector.tensor_reduce(tok1[:], key[:], AX.X, ALU.add))
            then(nc.vector.tensor_scalar(tok1[:], tok1[:], 1e-8, None, ALU.add))
            then(nc.vector.reciprocal(tok1[:], tok1[:]))
            then(nc.vector.tensor_tensor(key[:], key[:], bc(tok1[:], 2, E8), ALU.mult))
            then(nc.vector.tensor_reduce(tally[:, 0:E8], eq[:].rearrange("p t e -> p e t"), AX.X, ALU.add))
            then(nc.vector.tensor_reduce(tally[:, E8:2 * E8], key[:].rearrange("p t e -> p e t"), AX.X, ALU.add))
            nc.vector.memset(carrier[:], 0.0).then_inc(c.tally.sem, 1)
            dve.wait_ge(c.total_ps.sem, c.total_ps.at(1))
            then(nc.vector.tensor_scalar(total[:, 0:E8], psO[:, 0:E8], 1.0, None, ALU.max))
            then(nc.vector.reciprocal(total[:, 0:E8], total[:, 0:E8]))
            then(nc.vector.tensor_tensor(total[:, E8:2 * E8], total[:, 0:E8], psO[:, E8:2 * E8], ALU.mult))
            means = total[:, E8:2 * E8].rearrange("p (k e) -> p e k", e=2)
            wd = w("C_wd").rearrange("p (k d) -> p k d", k=FC)
            for half in range(2):
                r = slice(64 * half, 64 * half + 64)
                then(nc.vector.tensor_tensor(wd[r, 0:4, :], wd[r, 0:4, :], bc(means[r, half, :], 2, D), ALU.mult))
            nc.vector.memset(carrier[:], 0.0).then_inc(c.wd.sem, 1)

        def route_pe(pe):
            pe.wait_ge(c.tally.sem, c.tally.at(1))
            nc.tensor.matmul(psO[:, 0:2 * E8], ones[:], tally[:], start=True, stop=True).then_inc(c.total_ps.sem, 1)
            pe.wait_ge(c.wd.sem, c.wd.at(1))

        def dve_pick(dve, j):
            dve.wait_ge(c.sel_ps.sem, c.sel_ps.at(j))
            nc.vector.tensor_scalar(selp[:], sel[:, bass.ds(2 * j, 2), :], 1.0, None, ALU.mult).then_inc(c.selp.sem, 1)

        def pe_choices(pe, j):
            pe.wait_ge(c.selp.sem, c.selp.at(j + 1))
            pe.wait_ge(c.selT.sem, c.selT.at(j))
            for t in range(2):
                last = nc.tensor.transpose(psK[0:E8, t * P:(t + 1) * P], selp[:, t, :], ident)
            last.then_inc(c.sel_ps.sem, 1)

        def pe_masks(pe, j):
            pe.wait_ge(c.selT.sem, c.selT.at(j + 1))
            for k in range(4):
                pe.wait_ge(c.masked.sem, c.masked.at(4 * j + k - 3))
                nc.tensor.matmul(maskbank[k][:, 0:TOK], selmat[:, k * P:(k + 1) * P], selT[:], start=True,
                                 stop=True).then_inc(c.mask_ps.sem, 1)

        def pe_down(pe, j, odd, t):
            if t == 0:
                pe.wait_ge(c.masked.sem, c.masked.at(4 * j + 4))
                pe.wait_ge(c.shared.sem, c.shared.at(j + 1))
                pe.wait_ge(c.res.sem, c.res.at(j - 1))
            for k in range(FC):
                last = nc.tensor.matmul(downbank[odd][:, t * D:(t + 1) * D], hm[odd][:, k, t * P:(t + 1) * P],
                                        w("C_wd")[:, k * D:(k + 1) * D], start=(k == 0), stop=(k == FC - 1))
            if t == 1:
                last.then_inc(c.down_ps.sem, 1)

        def dve_masked(dve, j, odd):
            dve.wait_ge(c.down_ps.sem, c.down_ps.at(j - 1))
            nc.vector.tensor_scalar(hm[odd][:, 4, :], hidden[:, 4, bass.ds(j * TOK, TOK)], 1.0, None, ALU.mult).then_inc(c.shared.sem, 1)
            for k in range(4):
                dve.wait_ge(c.mask_ps.sem, c.mask_ps.at(4 * j + k + 1))
                nc.vector.tensor_tensor(hm[odd][:, k, :], maskbank[k][:, 0:TOK], hidden[:, k, bass.ds(j * TOK, TOK)],
                                        ALU.mult).then_inc(c.masked.sem, 1)

        def dve_down_residual(dve, j, odd):
            dve.wait_ge(c.down_ps.sem, c.down_ps.at(j + 1))
            nc.vector.tensor_tensor(pair(x, j), downbank[odd][:, 0:TOK].rearrange("p (t d) -> p t d", t=2), pair(x, j),
                                    ALU.add).then_inc(c.res.sem, 1)

        def weights_dve(dve):
            seq = [0]

            def then(ins):
                seq[0] += 1
                ins.then_inc(f.wstep.sem, 1)
                dve.wait_ge(f.wstep.sem, f.wstep.at(seq[0]))

            then(nc.vector.tensor_reduce(wsum[:, 0:1], w("F_w1"), AX.X, ALU.add, apply_absolute_value=True))
            then(nc.vector.tensor_reduce(wsum[:, 1:2], w("F_w2"), AX.X, ALU.add, apply_absolute_value=True))
            nc.vector.memset(carrier[:], 0.0).then_inc(f.wsum.sem, 1)
            dve.wait_ge(f.wsum_ps.sem, f.wsum_ps.at(1))
            then(nc.vector.tensor_scalar(wmean[:], psO[:, 0:2], 1.0 / (D * HID), 1e-5, ALU.mult, ALU.max))
            then(nc.vector.reciprocal(wscale[:], wmean[:]))
            for n, name in enumerate(("F_w1", "F_w2")):
                wq = w(name)
                then(nc.vector.tensor_scalar(wq, wq, wscale[:, n:n + 1], ROUND, ALU.mult, ALU.add))
                then(nc.vector.tensor_scalar(wq, wq, ROUND, 1.0, ALU.subtract, ALU.min))
                if n == 0:
                    then(nc.vector.tensor_scalar(wq, wq, -1.0, wmean[:, 0:1], ALU.max, ALU.mult))
                    then(nc.vector.tensor_tensor(taps[:], w("F_cw").rearrange("p (k f) -> p k f", k=3), bc(wq, 1, 3), ALU.mult))
                else:
                    then(nc.vector.tensor_scalar(w2q[:], wq, -1.0, None, ALU.max))
            then(nc.vector.tensor_copy(identb[:], ident))
            nc.vector.memset(carrier[:], 0.0).then_inc(f.weights.sem, 1)

        def weights_pe(pe):
            pe.wait_ge(f.wsum.sem, f.wsum.at(1))
            nc.tensor.matmul(psO[:, 0:2], ones[:], wsum[:], start=True, stop=True).then_inc(f.wsum_ps.sem, 1)
            pe.wait_ge(f.weights.sem, f.weights.at(1))

        def dve_quantise(dve, j):
            dve.wait_ge(fn.normed.sem, fn.normed.at(2 * j + 2))
            dve.wait_ge(fn.xT_ps.sem, fn.xT_ps.at(j))
            nc.vector.tensor_reduce(amax[:], xn[:], AX.X, ALU.max, apply_absolute_value=True).then_inc(f.amax.sem, 1)
            dve.wait_ge(f.amax.sem, f.amax.at(j + 1))
            nc.vector.tensor_scalar(amax[:], amax[:], 1e-5, 1.0 / 127.0, ALU.max, ALU.mult).then_inc(f.astep.sem, 1)
            dve.wait_ge(f.astep.sem, f.astep.at(j + 1))
            nc.vector.reciprocal(ainv[:], amax[:]).then_inc(f.ainv.sem, 1)
            dve.wait_ge(f.ainv.sem, f.ainv.at(j + 1))
            for t in range(2):
                nc.vector.tensor_scalar(xi[:, t, :], xn[:, t, :], ainv[:, t:t + 1], ROUND, ALU.mult, ALU.add).then_inc(f.xi.sem, 1)
            dve.wait_ge(f.xi.sem, f.xi.at(2 * j + 2))
            nc.vector.tensor_scalar(xi[:], xi[:], ROUND + 127.0, ROUND - 128.0, ALU.min, ALU.max).then_inc(f.clip.sem, 1)
            dve.wait_ge(f.clip.sem, f.clip.at(j + 1))
            for t in range(2):
                nc.vector.tensor_scalar(xi[:, t, :], xi[:, t, :], ROUND, amax[:, t:t + 1], ALU.subtract, ALU.mult).then_inc(f.xq.sem, 1)

        def pe_tokens(pe, j):
            pe.wait_ge(f.xq.sem, f.xq.at(2 * j + 2))
            pe.wait_ge(f.xs.sem, f.xs.at(3 * j))
            for t in range(2):
                last = nc.tensor.transpose(psK[:, t * P:(t + 1) * P], xi[:, t, :], ident)
            last.then_inc(fn.xT_ps.sem, 1)

        def act_shifts(act, j):
            act.wait_ge(fn.xT_ps.sem, fn.xT_ps.at(j + 1))
            act.wait_ge(f.h_ps.sem, f.h_ps.at(2 * j))
            src = psK[:, 0:TOK].rearrange("p (b m) -> p b m", m=S)
            for k in range(3):
                dst = xs[:, k, :].rearrange("p (b m) -> p b m", m=S)
                lo, hi = max(1 - k, 0), S - max(k - 1, 0)
                nc.scalar.activation(dst[:, :, lo:hi], src[:, :, lo + k - 1:hi + k - 1], ACT.Copy).then_inc(f.xs.sem, 1)

        def pe_conv(pe, j, t):
            pe.wait_ge(f.xs.sem, f.xs.at(3 * j + 3))
            pe.wait_ge(f.biased.sem, f.biased.at(2 * j + t - 1))
            for k in range(3):
                last = nc.tensor.matmul(psS[t][:, :], xs[:, k, t * P:(t + 1) * P], taps[:, k, :], start=(k == 0), stop=(k == 2))
            last.then_inc(f.h_ps.sem, 1)

        def dve_bias(dve, j, t):
            dve.wait_ge(f.h_ps.sem, f.h_ps.at(2 * j + t + 1))
            dve.wait_ge(f.hi.sem, f.hi.at(2 * j + t - 1))
            nc.vector.tensor_tensor(hb[:, t, :], psS[t][:, :], w("F_cb"), ALU.add).then_inc(f.biased.sem, 1)

        def act_silu(act, j, t):
            act.wait_ge(f.biased.sem, f.biased.at(2 * j + t + 1))
            act.wait_ge(f.hr.sem, f.hr.at(2 * j + t - 1))
            nc.scalar.activation(hs[:, t, :], hb[:, t, :], ACT.Silu).then_inc(f.silu.sem, 1)

        def dve_quantise_hidden(dve, j, t):
            n = 2 * j + t + 1
            m, r = hmax[:, t:t + 1], hinv[:, t:t + 1]
            dve.wait_ge(f.silu.sem, f.silu.at(n))
            nc.vector.tensor_reduce(m, hs[:, t, :], AX.X, ALU.max, apply_absolute_value=True).then_inc(f.hmax.sem, 1)
            dve.wait_ge(f.hmax.sem, f.hmax.at(n))
            dve.wait_ge(f.res.sem, f.res.at(n - 2))
            nc.vector.tensor_scalar(m, m, 1e-5, 1.0 / 127.0, ALU.max, ALU.mult).then_inc(f.hstep.sem, 1)
            dve.wait_ge(f.hstep.sem, f.hstep.at(n))
            nc.vector.reciprocal(r, m).then_inc(f.hinv.sem, 1)
            nc.vector.tensor_scalar(outstep[:, t:t + 1], m, wmean[:, 1:2], None, ALU.mult).then_inc(f.outstep.sem, 1)
            dve.wait_ge(f.hinv.sem, f.hinv.at(n))
            nc.vector.tensor_scalar(hr[:, t, :], hs[:, t, :], r, ROUND, ALU.mult, ALU.add).then_inc(f.hr.sem, 1)
            dve.wait_ge(f.hr.sem, f.hr.at(n))
            nc.vector.tensor_scalar(hr[:, t, :], hr[:, t, :], ROUND, 127.0, ALU.subtract, ALU.min).then_inc(f.hclip.sem, 1)
            dve.wait_ge(f.hclip.sem, f.hclip.at(n))
            dve.wait_ge(f.hT_ps.sem, f.hT_ps.at(n - 2))
            nc.vector.tensor_scalar(hi8[:, t, :], hr[:, t, :], -128.0, None, ALU.max).then_inc(f.hi.sem, 1)

        def pe_second(pe, j, t):
            n = 2 * j + t + 1
            pe.wait_ge(f.hi.sem, f.hi.at(n))
            for k in range(HC):
                last = nc.tensor.transpose(psTb[t][:, k * P:(k + 1) * P], hi8[:, t, k * P:(k + 1) * P], identb[:])
            last.then_inc(f.hT_ps.sem, 1)
            pe.wait_ge(f.hT.sem, f.hT.at(n))
            pe.wait_ge(f.res.sem, f.res.at(n - 1))
            for k in range(HC):
                last = nc.tensor.matmul(psV[:, t * D:(t + 1) * D], hT[:, t, k * P:(k + 1) * P], w2q[:, k * D:(k + 1) * D],
                                        start=(k == 0), stop=(k == HC - 1))
            last.then_inc(f.out_ps.sem, 1)

        def act_hiddenT(act, j, t):
            n = 2 * j + t + 1
            act.wait_ge(f.hT_ps.sem, f.hT_ps.at(n))
            act.wait_ge(f.out_ps.sem, f.out_ps.at(n - 2))
            nc.scalar.activation(hT[:, t, :], psTb[t][:, 0:HC * P], ACT.Copy).then_inc(f.hT.sem, 1)

        def dve_second_residual(dve, j, t):
            n = 2 * j + t + 1
            dve.wait_ge(f.out_ps.sem, f.out_ps.at(n))
            dve.wait_ge(f.outstep.sem, f.outstep.at(n))
            tile = tile_of(x, j)(t)
            nc.vector.scalar_tensor_tensor(out=tile, in0=psV[:, t * D:(t + 1) * D], scalar=outstep[:, t:t + 1], in1=tile,
                                           op0=ALU.mult, op1=ALU.add).then_inc(f.res.sem, 1)

        def dve_norm_stats(dve, a, j):
            n = a.n0 if a.affine else a.n
            norm_stats(dve, n, j, tile_of(x, j), a.n.rstd, j)

        def dve_norm_plain(dve, a, j):
            norm_apply(dve, a.n0, j, tile_of(x, j), xm, a.n.normed, 2 * j)
            dve.wait_ge(a.n0.normed.sem, a.n0.normed.at(2 * j + 2))
            norm_stats(dve, a.n, j, lambda t: xm[:, t, :], a.n0.rstd, j + 1)

        def dve_norm_apply(dve, a, j):
            norm_apply(dve, a.n, j, (lambda t: xm[:, t, :]) if a.affine else tile_of(x, j), xn, a.n.xT_ps, j)

        def dve_norm(dve, a, j):
            dve_norm_stats(dve, a, j)
            if a.affine:
                dve_norm_plain(dve, a, j)
            dve_norm_apply(dve, a, j)

        def pool_norm(pool, a, j):
            if a.affine:
                norm_rstd(pool, a.n0, j, a.n.normed, 2 * j)
                norm_rstd(pool, a.n, j, a.n0.normed, 2 * j + 2)
            else:
                norm_rstd(pool, a.n, j, a.n.normed, 2 * j)

        def sync_context(sp, a):
            def step(j):
                if a.queries:
                    sp.wait_ge(a.s.k_ps.sem, a.s.k_ps.at(j))
                    sp.dma_start(cT[:], ctx_in[:, bass.ds(j * TOK, TOK)]).then_inc(a.s.ctx.sem, 16)
                sp.wait_ge(a.s.v_ps.sem, a.s.v_ps.at(j))
                sp.dma_start(vT[:], ctx_in[:, bass.ds(j * TOK, TOK)]).then_inc(a.s.vctx.sem, 16)
            over_pairs(sp, step, PAIRS)

        def sync_statistics(sp, a):
            def step(j, more=True):
                if more:
                    sp.wait_ge(a.s.k_ps.sem, a.s.k_ps.at(j + 1))
                    sp.dma_start(cT[:], ctx_in[:, bass.ds((j + 1) * TOK, TOK)]).then_inc(a.s.ctx.sem, 16)
                for g in range(G):
                    sp.wait_ge(a.s.shift.sem, a.s.shift.at(G * j + g + 1))
                    sp.dma_start(kept[:, bass.ds(2 * j, 2), g * 256:(g + 1) * 256],
                                 shifted[:, g, :].rearrange("p (t c) -> p t c", t=2)).then_inc(e_stored[g].sem, 16)
            sp.wait_ge(Bx.s.v_ps.sem, Bx.s.v_ps.at(PAIRS))
            sp.wait_ge(Bx.s.ctx.sem, Bx.s.ctx.at(16 * PAIRS))
            sp.dma_start(cT[:], ctx_in[:, 0:TOK]).then_inc(a.s.ctx.sem, 16)
            over_pairs(sp, step, PAIRS - 1)
            step(PAIRS - 1, more=False)

        def over_pairs(eng, step, last):
            step(0)
            with eng.Fori(1, last) as i:
                step(i)

        def over_bodies(eng, step, ahead=2):
            step(0, before=False)
            with eng.Fori(1, PAIRS - ahead) as i:
                step(i)
            for i in range(PAIRS - ahead, PAIRS):
                step(i, tokens=False, scores=i < PAIRS - 1)

        def attention_pe(pe, a):
            def step(i, before=True, tokens=True, scores=True):
                before = before and a.out_proj
                queries, tokens = scores and a.queries, tokens and a.queries
                if before:
                    pe_headsT(pe, a, i - 1)
                if queries:
                    pe_scores(pe, a, i + 1, (0,))
                pe_transpose(pe, a, i, 0)
                if before:
                    pe_out(pe, a, i - 1)
                if queries:
                    pe_scores(pe, a, i + 1, (1,))
                pe_transpose(pe, a, i, 1)
                if queries:
                    pe_scores(pe, a, i + 1, (2,))
                if scores:
                    pe_value_projection(pe, a, i + 1)
                if tokens:
                    pe_tokens_transposed(pe, a, i + 2)
                pe_values(pe, a, i, 0)
                if queries:
                    pe_scores(pe, a, i + 1, (3,))
                if tokens:
                    pe_queries(pe, a, i + 2)
                pe_transpose(pe, a, i, 2)
                pe_values(pe, a, i, 1)
                pe_transpose(pe, a, i, 3)
                pe_values(pe, a, i, 2)
                pe_values(pe, a, i, 3)

            def wide_step(i, before=True, tokens=True, scores=True):
                pe.wait_ge(a.s.row.sem, a.s.row.at(i + 2 if scores else PAIRS))
                if scores:
                    pe_project(pe, a, i + 1, 0)
                    pe_project(pe, a, i + 1, 1)
                for g in range(G):
                    pe_transpose(pe, a, i, g)
                    if before and g == 1:
                        pe_out(pe, a, i - 1)
                    if scores:
                        pe_wide_scores(pe, a, i + 1, g)
                    if before and g == 0:
                        pe_headsT(pe, a, i - 1)
                    if scores and g == 3:
                        pe_value_projection(pe, a, i + 1)
                    if tokens and g == 3:
                        pe_tokens_transposed(pe, a, i + 2)
                    pe_values(pe, a, i, g)
                if tokens:
                    pe_queries(pe, a, i + 2)

            if a.wide:
                maps_pe(pe)
            pe_front(pe, a, 0)
            if a.wide:
                pe_project(pe, a, 0, 0)
                pe_project(pe, a, 0, 1)
                for g in range(G):
                    pe_wide_scores(pe, a, 0, g)
            elif a.queries:
                pe_scores(pe, a, 0, (0, 1, 2))
                pe_scores(pe, a, 0, (3,))
            pe_value_projection(pe, a, 0)
            pe_front(pe, a, 1)
            over_bodies(pe, wide_step if a.wide else step)
            if a.out_proj:
                pe_headsT(pe, a, PAIRS - 1, more=False)
                pe_out(pe, a, PAIRS - 1)

        def attention_act(act, a):
            def front(i):
                if a.queries:
                    act_tokens(act, a, i)
                    if a.wide:
                        act_rowterm(act, a, i)
                    else:
                        act_queries(act, a, i)
                        act_keys(act, a, i)

            def step(i, before=True, tokens=True, scores=True):
                tokens = tokens and a.queries
                if before and a.out_proj:
                    act_headsT(act, a, i - 1)
                act_probsT(act, a, i, 0)
                act_probsT(act, a, i, 1)
                if tokens:
                    act_tokens(act, a, i + 2)
                if scores:
                    act_exp(act, a, i + 1, 0)
                if tokens:
                    act_queries(act, a, i + 2, (0, 1))
                act_probsT(act, a, i, 2)
                act_probsT(act, a, i, 3)
                if tokens:
                    act_keys(act, a, i + 2)
                    act_queries(act, a, i + 2, (2, 3))
                if scores:
                    act_exp(act, a, i + 1, 1)
                    act_exp(act, a, i + 1, 2)
                    act_exp(act, a, i + 1, 3)

            def wide_step(i, before=True, tokens=True, scores=True):
                for g in range(G):
                    if scores:
                        act_wide_queries(act, a, i + 1, range(HG * g, HG * g + 2))
                    act_probsT(act, a, i, g)
                    if before and g == 1:
                        act_headsT(act, a, i - 1)
                    if scores:
                        act_wide_queries(act, a, i + 1, range(HG * g + 2, HG * g + 3))
                        if g:
                            act_exp(act, a, i + 1, g - 1)
                        act_wide_queries(act, a, i + 1, range(HG * g + 3, HG * g + HG))
                if tokens:
                    front(i + 2)
                if scores:
                    act_exp(act, a, i + 1, 3)

            if a.wide:
                maps_act(act)
            front(0)
            if a.wide:
                act_wide_queries(act, a, 0, range(0, H))
            for g in range(G):
                if g == 3:
                    front(1)
                act_exp(act, a, 0, g)
            over_bodies(act, wide_step if a.wide else step)
            if a.out_proj:
                act_headsT(act, a, PAIRS - 1)

        def bias_copies(dve, a):
            nc.vector.tensor_scalar(querybias[:], w("groupmask"), w(a.w + "_bq"), None, ALU.mult).then_inc(kb[a.st].sem, 1)
            nc.vector.tensor_scalar(keybias[:], w("headmask"), w(a.w + "_bk"), None, ALU.mult).then_inc(kb[a.st].sem, 1)

        def attention_dve(dve, a):
            def softmax(i, after_first, after_second, residual):
                if a.wide:
                    dve_wide_softmax(dve, a, i, 0)
                    after_first()
                    dve_wide_softmax(dve, a, i, 1)
                    dve_wide_softmax(dve, a, i, 2)
                    after_second()
                    dve_wide_softmax(dve, a, i, 3)
                elif a.queries:
                    dve_rowmax(dve, a, i, 0)
                    dve_rowmax(dve, a, i, 1)
                    residual()
                    dve_shift(dve, a, i, 0)
                    after_first()
                    dve_rowmax(dve, a, i, 2)
                    dve_shift(dve, a, i, 1)
                    dve_rowmax(dve, a, i, 3)
                    dve_shift(dve, a, i, 2)
                    after_second()
                    dve_shift(dve, a, i, 3)
                else:
                    dve_kept_softmax(dve, a, i, 0)
                    after_first()
                    dve_kept_softmax(dve, a, i, 1)
                    dve_kept_softmax(dve, a, i, 2)
                    dve_kept_softmax(dve, a, i, 3)

            def step(i, before=True, tokens=True, scores=True):
                tokens = tokens and a.queries

                def residual(j):
                    if before and a.out_proj:
                        dve_residual(dve, a, j)

                def after_first():
                    if tokens and a.affine:
                        dve_norm_plain(dve, a, i + 3)
                    elif tokens and a.wide:
                        dve_norm_apply(dve, a, i + 2)
                    if not a.queries:
                        residual(i - 1)

                def after_second():
                    if tokens and not a.wide:
                        dve_norm_apply(dve, a, i + 3)
                    if a.wide:
                        residual(i - 1)

                if tokens:
                    dve_norm_stats(dve, a, i + (2 if a.wide else 3))
                if scores:
                    softmax(i + 1, after_first, after_second, lambda: residual(i - 1))
                if before and not scores:
                    residual(i - 1)
                dve_reciprocal(dve, a, i)
                if scores:
                    dve_values(dve, a, i + 1)
                dve_heads(dve, a, i)
                if not a.out_proj:
                    dve_residual(dve, a, i)

            if a.wide:
                maps_dve(dve)
            if a.st in kb:
                bias_copies(dve, a)
            if a.queries:
                dve_norm(dve, a, 0)
                dve_norm(dve, a, 1)
            softmax(0, lambda: None, lambda: None, lambda: None)
            dve_values(dve, a, 0)
            if a.queries and not a.wide:
                dve_norm(dve, a, 2)
            over_bodies(dve, step, 2 if a.wide else 3)
            if a.out_proj:
                dve_residual(dve, a, PAIRS - 1)
            dve.wait_ge(a.s.res.sem, a.s.res.at(PAIRS))

        def attention_pool(pool, a):
            def step(j):
                pool_norm(pool, a, j)

            def wide_step(j):
                pool_cmask(pool, a, j)
                pool_norm(pool, a, j + 2)

            if not a.queries:
                return
            if a.wide:
                pool.wait_ge(loads["D"].sem, loads["D"].at(16))
                pool_norm(pool, a, 0)
                pool_norm(pool, a, 1)
                over_pairs(pool, wide_step, PAIRS - 2)
                pool_cmask(pool, a, PAIRS - 2)
                pool_cmask(pool, a, PAIRS - 1)
            else:
                over_pairs(pool, step, PAIRS)

        def statistics_pe(pe, a):
            def step(i, front=True):
                pe_scores(pe, a, i, (0, 1, 2))
                pe_means(pe, a, i)
                pe_scores(pe, a, i, (3,))
                if front:
                    pe_front(pe, a, i + 1)

            pe_front(pe, a, 0)
            over_pairs(pe, step, PAIRS - 1)
            step(PAIRS - 1, front=False)

        def statistics_act(act, a):
            def front(i):
                act_tokens(act, a, i)
                act_queries(act, a, i)
                act_keys(act, a, i)

            def step(i, more=True):
                act_exp(act, a, i, 0)
                act_squares(act, a, i, 0)
                if more:
                    act_tokens(act, a, i + 1)
                act_exp(act, a, i, 1)
                act_squares(act, a, i, 1)
                if more:
                    act_queries(act, a, i + 1)
                    act_keys(act, a, i + 1)
                for g in (2, 3):
                    act_exp(act, a, i, g)
                    act_squares(act, a, i, g)

            front(0)
            over_pairs(act, step, PAIRS - 1)
            step(PAIRS - 1, more=False)

        def statistics_dve(dve, a):
            def step(i, more=2):
                if more > 1:
                    dve_norm_stats(dve, a, i + 2)
                dve_rowmax(dve, a, i, 0)
                dve_rowmax(dve, a, i, 1)
                dve_shift(dve, a, i, 0)
                dve_rowmax(dve, a, i, 2)
                dve_shift(dve, a, i, 1)
                if more > 1:
                    dve_norm_apply(dve, a, i + 2)
                dve_sums(dve, a, i, 0)
                dve_rowmax(dve, a, i, 3)
                dve_shift(dve, a, i, 2)
                dve_sums(dve, a, i, 1)
                dve_shift(dve, a, i, 3)
                dve_means(dve, a, i)
                if more > 0:
                    dve_keysum(dve, a, i + 1)
                dve_sums(dve, a, i, 2)
                dve_sums(dve, a, i, 3)
                dve_keep(dve, a, i)

            bias_copies(dve, a)
            dve_norm(dve, a, 0)
            dve_norm(dve, a, 1)
            dve_keysum(dve, a, 0)
            over_pairs(dve, step, PAIRS - 2)
            step(PAIRS - 2, more=1)
            step(PAIRS - 1, more=0)

        def over_twos(eng, step):
            step(0, 0)
            step(1, 1)
            with eng.Fori(1, PAIRS // 2 - 1) as i:
                step(2 * i, 0)
                step(2 * i + 1, 1)
            step(PAIRS - 2, 0)
            step(PAIRS - 1, 1, more=False)

        def experts_pe(pe):
            def hidden_step(j, odd, more=True):
                pe_router(pe, j, odd)
                pe_hidden(pe, j, odd, (0, 1))
                if more:
                    pe_hidden_tokens(pe, j + 1)
                pe_hidden(pe, j, odd, (2, 3, 4))

            def down_step(j, odd, more=True):
                if more:
                    pe_choices(pe, j + 1)
                pe_down(pe, j, odd, 0)
                if more:
                    pe_masks(pe, j + 1)
                pe_down(pe, j, odd, 1)

            pe_hidden_tokens(pe, 0)
            over_twos(pe, hidden_step)
            route_pe(pe)
            pe_choices(pe, 0)
            pe_masks(pe, 0)
            over_twos(pe, down_step)

        def experts_act(act):
            def hidden_step(j, odd, more=True):
                act_hidden(act, j, (0, 1))
                if more:
                    act_hidden_tokens(act, j + 1, 1 - odd)
                act_hidden(act, j, (2, 3, 4))

            def choices_copy(j):
                act.wait_ge(c.sel_ps.sem, c.sel_ps.at(j + 1))
                act.wait_ge(c.mask_ps.sem, c.mask_ps.at(4 * j))
                nc.scalar.activation(selT[:], psK[0:E8, 0:TOK], ACT.Copy).then_inc(c.selT.sem, 1)

            act_hidden_tokens(act, 0, 0)
            over_twos(act, hidden_step)
            act.wait_ge(c.logits.sem, c.logits.at(PAIRS))
            nc.scalar.activation(score[:], logits[:], ACT.Sigmoid).then_inc(c.sig.sem, 1)
            over_pairs(act, choices_copy, PAIRS)

        def experts_dve(dve):
            def hidden_step(j, norm=True):
                dve_logits(dve, j)
                dve_hidden(dve, j, (0, 1, 2))
                if norm:
                    dve_stage_norm(dve, cn, j + 2)
                dve_hidden(dve, j, (3, 4))

            def down_step(j, odd, more=True):
                if more:
                    dve_masked(dve, j + 1, 1 - odd)
                    if not isinstance(j, int) or j + 2 < PAIRS:
                        dve_pick(dve, j + 2)
                dve_down_residual(dve, j, odd)

            dve_stage_norm(dve, cn, 0)
            dve_stage_norm(dve, cn, 1)
            over_pairs(dve, hidden_step, PAIRS - 2)
            hidden_step(PAIRS - 2, norm=False)
            hidden_step(PAIRS - 1, norm=False)
            nc.vector.tensor_copy(selmat[:], w("C_sel", E8)).then_inc(c.selmat.sem, 1)
            dve.wait_ge(c.selmat.sem, c.selmat.at(1))
            route_dve(dve)
            dve.wait_ge(c.sel.sem, c.sel.at(1))
            dve_pick(dve, 0)
            dve_masked(dve, 0, 0)
            dve_pick(dve, 1)
            over_twos(dve, down_step)
            dve.wait_ge(c.res.sem, c.res.at(PAIRS))

        def dve_stage_norm(dve, n, j):
            norm_stats(dve, n, j, tile_of(x, j), n.rstd, j)
            norm_apply(dve, n, j, tile_of(x, j), xn, n.xT_ps, j)

        def stage_norm_pool(pool, n):
            over_pairs(pool, lambda j: norm_rstd(pool, n, j, n.normed, 2 * j), PAIRS)

        def convolved_pe(pe):
            weights_pe(pe)

            def step(i, more=True):
                pe_conv(pe, i + 1, 0)
                pe_second(pe, i, 0)
                if more:
                    pe_tokens(pe, i + 2)
                pe_conv(pe, i + 1, 1)
                pe_second(pe, i, 1)

            pe_tokens(pe, 0)
            pe_conv(pe, 0, 0)
            pe_conv(pe, 0, 1)
            pe_tokens(pe, 1)
            over_pairs(pe, step, PAIRS - 2)
            step(PAIRS - 2, more=False)
            for t in range(2):
                pe_second(pe, PAIRS - 1, t)

        def convolved_act(act):
            def step(i, more=True):
                act_hiddenT(act, i, 0)
                act_silu(act, i + 1, 0)
                if more:
                    act_shifts(act, i + 2)
                act_hiddenT(act, i, 1)
                act_silu(act, i + 1, 1)

            act.wait_ge(f.edges.sem, f.edges.at(1))
            act_shifts(act, 0)
            act_shifts(act, 1)
            for t in range(2):
                act_silu(act, 0, t)
            over_pairs(act, step, PAIRS - 2)
            step(PAIRS - 2, more=False)
            for t in range(2):
                act_hiddenT(act, PAIRS - 1, t)

        def convolved_dve(dve):
            weights_dve(dve)

            def front(i):
                dve_stage_norm(dve, fn, i)
                dve_quantise(dve, i)

            def step(i, norm=True):
                dve_bias(dve, i + 1, 0)
                dve_second_residual(dve, i, 0)
                if norm:
                    front(i + 3)
                dve_bias(dve, i + 1, 1)
                dve_quantise_hidden(dve, i + 1, 0)
                dve_second_residual(dve, i, 1)
                dve_quantise_hidden(dve, i + 1, 1)

            front(0)
            front(1)
            for t in range(2):
                dve_bias(dve, 0, t)
            for t in range(2):
                dve_quantise_hidden(dve, 0, t)
            front(2)
            over_pairs(dve, step, PAIRS - 3)
            step(PAIRS - 3, norm=False)
            step(PAIRS - 2, norm=False)
            for t in range(2):
                dve_second_residual(dve, PAIRS - 1, t)

        A = attention("A", affine=True, out_proj=False)
        Bx = attention("B", cross=True)
        c, cn = sems("C", "xT logits_ps logits gate_up silu hidden sig route sel tally total_ps wd selmat sel_ps selp shared "
                          "selT mask_ps masked down_ps res"), norm_signals()
        Dw = attention("D", wide=True, scale=D ** -0.5)
        E1 = attention("E1", wst="E", cross=True, values=False, out_proj=False)
        E2 = attention("E2", wst="E", cross=True, queries=False, scale=1.0, guard=True)
        e = sems("E", "q bk64 ksum ksb mean_ps mean sq z z2 kept kept2 var feat_ps feats h_ps h logt_ps logt inv_t v "
                      "stored0 stored1 stored2 stored3")
        kb_sems = sems("keybias", "A B E1")
        kb = {"A": kb_sems.A, "B": kb_sems.B, "E1": kb_sems.E1}
        d = sems("D", "maps_ps maps inplace")
        mapbank = [psS[0], psS[1], psT[0], psT[1]]
        e_stored = [e.stored0, e.stored1, e.stored2, e.stored3]
        f, fn = sems("F", "wstep wsum wsum_ps weights edges amax astep ainv xi clip xq xs h_ps biased silu hmax hstep hinv outstep "
                          "hr hclip hi hT_ps hT out_ps res"), norm_signals()
        block = ctx.enter_context(nc.Block())

        @block.sync
        def _(sp):
            sp.dma_start(x[:].rearrange("p t d -> p (t d)"), x_in).then_inc(load.x.sem, 16)
            for p in STAGES:
                sp.dma_start(wt[p][:], packs_in[p]).then_inc(loads[p].sem, 16)
            for a in (Bx, E1, E2):
                if a.w in STAGES:
                    if a is E1:
                        sync_statistics(sp, E1)
                    else:
                        sync_context(sp, a)
            sp.wait_ge(f.res.sem, f.res.at(TILES))
            sp.dma_start(out, x[:].rearrange("p t d -> p (t d)")).then_inc(load.out.sem, 16)
            sp.wait_ge(load.out.sem, load.out.at(16))

        @block.gpsimd
        def _(pool):
            nc.gpsimd.memset(minus_half[:], -0.5).then_inc(init.pool.sem, 1)
            nc.gpsimd.memset(ones[:], 1.0).then_inc(init.pool.sem, 1)
            nc.gpsimd.memset(zeros[:], 0.0).then_inc(init.pool.sem, 1)
            nc.gpsimd.memset(vbd[:], 0.0).then_inc(init.pool.sem, 1)
            pool.wait_ge(init.pool.sem, init.pool.at(4))
            nc.gpsimd.memset(vbd[0:64, :, :, 0, DH], 1.0).then_inc(init.pool.sem, 1)
            nc.gpsimd.memset(vbd[64:128, :, :, 1, DH], 1.0).then_inc(init.pool.sem, 1)
            for a, p in ((A, "A"), (Bx, "B"), (None, "C"), (Dw, "D"), (E1, "E"), (None, "F")):
                if p not in STAGES:
                    continue
                if a:
                    attention_pool(pool, a)
                elif p == "C":
                    stage_norm_pool(pool, cn)
                else:
                    pool.wait_ge(E1.s.scores.sem, E1.s.scores.at(G * PAIRS))
                    nc.gpsimd.memset(xs, 0.0).then_inc(f.edges.sem, 1)
                    stage_norm_pool(pool, fn)

        @block.scalar
        def _(act):
            for p in STAGES:
                act.wait_ge(loads[p].sem, loads[p].at(16))
                if p == "A":
                    attention_act(act, A)
                elif p == "B":
                    attention_act(act, Bx)
                elif p == "C":
                    experts_act(act)
                elif p == "D":
                    attention_act(act, Dw)
                elif p == "E":
                    statistics_act(act, E1)
                    temperature_act(act)
                    attention_act(act, E2)
                else:
                    convolved_act(act)

        @block.vector
        def _(dve):
            dve.wait_ge(load.x.sem, load.x.at(16))
            dve.wait_ge(init.pool.sem, init.pool.at(6))
            for p in STAGES:
                dve.wait_ge(loads[p].sem, loads[p].at(16))
                if p == "A":
                    attention_dve(dve, A)
                elif p == "B":
                    attention_dve(dve, Bx)
                elif p == "C":
                    experts_dve(dve)
                elif p == "D":
                    attention_dve(dve, Dw)
                elif p == "E":
                    nc.vector.tensor_scalar(bk64[:], w("E_bk"), float(S), None, ALU.mult).then_inc(e.bk64.sem, 1)
                    dve.wait_ge(e.bk64.sem, e.bk64.at(1))
                    statistics_dve(dve, E1)
                    temperature_dve(dve)
                    attention_dve(dve, E2)
                else:
                    convolved_dve(dve)

        @block.tensor
        def _(pe):
            pe.wait_ge(init.pool.sem, init.pool.at(6))
            for p in STAGES:
                pe.wait_ge(loads[p].sem, loads[p].at(16))
                if p == "A":
                    attention_pe(pe, A)
                elif p == "B":
                    attention_pe(pe, Bx)
                elif p == "C":
                    experts_pe(pe)
                elif p == "D":
                    attention_pe(pe, Dw)
                elif p == "E":
                    statistics_pe(pe, E1)
                    temperature_pe(pe)
                    attention_pe(pe, E2)
                else:
                    convolved_pe(pe)


_INS = ["x", "ctx_1024"]


def layouts(i):
    f = np.float32

    def rows(a, n=P):
        a = np.asarray(a)
        return np.concatenate([a, np.zeros((n - a.shape[0], a.shape[1]), a.dtype)]) if a.shape[0] < n else a

    def col(v):
        return rows(np.asarray(v).reshape(-1, 1))

    def over(v):
        v = np.asarray(v).reshape(1, -1)
        return np.repeat(v, P, axis=0)

    def even_odd(a):
        a = np.asarray(a)
        return a.reshape(-1, H // 2, 2, DH).transpose(0, 2, 1, 3).reshape(-1, D)

    r = np.arange(P)
    qkv, bqkv = np.asarray(i["L0_attn_w_qkv"]), np.asarray(i["L0_attn_b_qkv"])
    c = {
        "ident": np.eye(P, dtype=f),
        "headmask": (r[:, None] % 32 // DH == np.arange(HG)[None, :]).astype(f),
        "groupmask": (r[:, None] // 32 == np.arange(G)[None, :]).astype(f),
        "A_wq": qkv[0:D].T, "A_wk": qkv[D:2 * D].T, "A_wv": even_odd(qkv[2 * D:].T),
        "A_bq": col(bqkv[0:D]), "A_bk": col(bqkv[D:2 * D]), "A_bv": over(even_odd(bqkv[2 * D:])),
        "gamma": col(i["L0_attn_ln_gamma"]), "beta": col(i["L0_attn_ln_beta"]),
    }

    def grouped(a):
        a = np.asarray(a)
        a = a.reshape(4, 1, DH, *a.shape[1:])
        return np.repeat(a, 4, axis=1).reshape(P, *a.shape[3:])

    c.update({
        "B_wq": np.asarray(i["L0_xattn_w_q"]).T, "B_wk": grouped(i["L0_xattn_w_k"]).T, "B_wv": even_odd(grouped(i["L0_xattn_w_v"]).T),
        "B_bq": col(i["L0_xattn_b_q"]), "B_bk": col(grouped(i["L0_xattn_b_k"])), "B_bv": over(even_odd(grouped(i["L0_xattn_b_v"]))),
        "B_wo": np.asarray(i["L0_xattn_w_o"]).T, "B_bo": over(i["L0_xattn_b_o"]),
    })
    def experts(a):
        return np.asarray(a).reshape(E8 * FI, D).T

    lw = np.arange(4)
    c.update({
        "C_gate": i["L0_ffn_gate_w"].T, "C_lb": over(i["L0_ffn_lb_bias"]),
        "C_wg": np.concatenate([experts(i["L0_ffn_expert_gate_w"]), i["L0_ffn_shared_gate_w"].T], axis=1),
        "C_wu": np.concatenate([experts(i["L0_ffn_expert_up_w"]), i["L0_ffn_shared_up_w"].T], axis=1),
        "C_wd": np.concatenate([i["L0_ffn_expert_down_w"].transpose(0, 2, 1).reshape(4, P, D).transpose(1, 0, 2).reshape(P, 4 * D),
                                i["L0_ffn_shared_down_w"].T], axis=1),
        "C_first": over(np.arange(E8, 0, -1).astype(f)),
        "C_sel": rows((np.arange(E8)[:, None, None] == 2 * lw[None, :, None] + (r // 64)[None, None, :]).astype(f).reshape(E8, 4 * P)),
    })
    kqv, bkqv = i["L1_attn_Wkqv"], i["L1_attn_bkqv"]
    c.update({
        "D_wkT": kqv[:, :, 0:D].transpose(2, 0, 1).reshape(D, H * D), "D_wqT": kqv[:, :, D:2 * D].transpose(2, 0, 1).reshape(D, H * D),
        "D_wv": even_odd(kqv[:, :, 2 * D:].transpose(1, 0, 2).reshape(D, D)),
        "D_bk": bkqv[:, 0:D].T, "D_bq": bkqv[:, D:2 * D].T, "D_bv": over(even_odd(bkqv[:, 2 * D:].reshape(1, D))),
        "D_wo": i["L1_attn_Wp"], "D_bo": over(i["L1_attn_bp"]),
        "D_causal": np.where(np.arange(S)[None, :] <= (r % S)[:, None], 0.0, -1e30).astype(f),
    })
    featsel = np.zeros((P, 2, 3, 3), f)
    for b in range(2):
        for n, v in enumerate((1 / S / DH ** 0.5, 1 / S / DH ** 0.5, 1 / S)):
            featsel[64 * b:64 * b + 64, b, n, n] = v
    c.update({
        "E_wq": i["L1_xattn_Wq"].T, "E_wk": i["L1_xattn_Wk"].T, "E_wv": even_odd(i["L1_xattn_Wv"].T),
        "E_bq": col(i["L1_xattn_bq"]), "E_bk": col(i["L1_xattn_bk"]), "E_bv": over(even_odd(i["L1_xattn_bv"])),
        "E_wo": i["L1_xattn_Wo"].T, "E_bo": over(i["L1_xattn_bo"]),
        "E_w1": rows(i["L1_xattn_w1"].T), "E_b1": col(i["L1_xattn_b1"]), "E_w2": rows(i["L1_xattn_w2"].T),
        "E_b2": col(i["L1_xattn_b2"]), "E_w3": rows(np.repeat(i["L1_xattn_w3"].T, 64, axis=1)), "E_b3": over(i["L1_xattn_b3"]),
        "E_headblk": (r[:, None] // DH == np.arange(H)[None, :]).astype(f), "E_featsel": featsel.reshape(P, 18),
        "F_w1": i["L1_ffn_w1"].T, "F_cw": over(i["L1_ffn_conv_w"][:, 0, :].T), "F_cb": over(i["L1_ffn_conv_b"]),
        "F_w2": i["L1_ffn_w2"].T.reshape(HC, P, D).transpose(1, 0, 2).reshape(P, HC * D),
    })
    return c


def kernel(**inputs):
    import concourse.bacc as bacc
    from concourse.bass_utils import run_bass_kernel_spmd

    nc = bacc.Bacc("TRN2", target_bir_lowering=False, num_devices=1)
    i = {k: np.asarray(v) for k, v in inputs.items()}
    c = layouts(i)
    arrays = {
        "x_tiles": np.ascontiguousarray(i["x"].reshape(TILES, P, D).transpose(1, 0, 2).reshape(P, TILES * D)),
        "ctx_T": np.ascontiguousarray(i["ctx_1024"].reshape(B * S, D).T),
    }
    for pack, parts in PACKS.items():
        if pack in STAGES:
            arrays["weights_" + pack] = np.ascontiguousarray(np.concatenate([c[n] for n, _ in parts], axis=1))
    dram = {n: nc.dram_tensor(n, a.shape, mybir.dt.from_np(a.dtype), kind="ExternalInput").ap() for n, a in arrays.items()}
    out = nc.dram_tensor("out_tiles", (P, TILES * D), F32, kind="ExternalOutput").ap()
    build(nc, dram["x_tiles"], dram["ctx_T"], {p: dram["weights_" + p] for p in PACKS if p in STAGES}, out)
    r = run_bass_kernel_spmd(nc, [arrays], core_ids=[0])
    got = r.results[0]["out_tiles"]
    return got.reshape(P, TILES, D).transpose(1, 0, 2).reshape(B, S, D)
```

```python
from collections import namedtuple
from contextlib import ExitStack

import numpy as np

import concourse.bass as bass
from concourse import mybir

F32 = mybir.dt.float32
BF16 = mybir.dt.bfloat16
I32 = mybir.dt.int32
ALU = mybir.AluOpType
ACT = mybir.ActivationFunctionType
AX = mybir.AxisListType

B, S, D = 32, 64, 128
H, DH = 16, 8
P = 128
TILES = B * S // P
PAIRS = TILES // 2
TOK = 2 * P
PB = TOK // S
G = 4
HG = H // G
UNIT = 2 * HG * S
VW = DH + 1
E8, FI = 8, 64
FC = 5
EPS = 1e-5
HID = 512
HC = HID // P
MLP = 64
ROUND = 1.5 * 2.0 ** 23

PACKS = {
    "A": [("ident", P), ("headmask", HG), ("groupmask", G), ("A_wq", D), ("A_wk", D), ("A_wv", D),
          ("A_bq", 1), ("A_bk", 1), ("A_bv", D), ("gamma", 1), ("beta", 1)],
    "B": [("B_wq", D), ("B_wk", D), ("B_wv", D), ("B_bq", 1), ("B_bk", 1), ("B_bv", D), ("B_wo", D), ("B_bo", D)],
    "C": [("C_gate", E8), ("C_lb", E8), ("C_wg", FC * P), ("C_wu", FC * P), ("C_wd", FC * D),
          ("C_first", E8), ("C_sel", 4 * P)],
    "D": [("D_wqT", H * D), ("D_wkT", H * D), ("D_wv", D), ("D_bq", H), ("D_bk", H), ("D_bv", D),
          ("D_wo", D), ("D_bo", D), ("D_causal", S)],
    "E": [("E_wq", D), ("E_wk", D), ("E_wv", D), ("E_bq", 1), ("E_bk", 1), ("E_bv", D), ("E_wo", D), ("E_bo", D),
          ("E_w1", P), ("E_b1", 1), ("E_w2", P), ("E_b2", 1), ("E_w3", 64), ("E_b3", 1),
          ("E_headblk", H), ("E_featsel", 18)],
    "F": [("F_w1", HID), ("F_cw", 3 * HID), ("F_cb", HID), ("F_w2", HC * D)],
}


def named(things):
    return namedtuple("Named", list(things))(*things.values())


class Signal:

    def __init__(self, sem, base=0):
        self.sem, self.base = sem, base

    def at(self, n):
        return self.base + (max(n, 0) if isinstance(n, int) else n)


def offsets():
    at, width = {}, {}
    for pack, parts in PACKS.items():
        n = 0
        for name, w in parts:
            at[name] = (pack, n, w)
            n += w
        width[pack] = n
    return at, width


STAGES = "ABCDEF"


def build(nc, x_in, ctx_in, packs_in, out):
    at, width = offsets()
    with ExitStack() as ctx:
        def sb(name, shape, dt=F32):
            return ctx.enter_context(nc.sbuf_tensor(name, shape, dt))

        def sems(stage, names):
            return named({n: Signal(ctx.enter_context(nc.semaphore(f"{stage}_{n}"))) for n in names.split()})

        shared, counted = {}, {}

        def signals(per_pair, prefix=""):
            out = {}
            for item in per_pair.split():
                name, n = item.split(":")
                name = prefix + name
                if name not in shared:
                    shared[name], counted[name] = ctx.enter_context(nc.semaphore(name)), 0
                out[name] = Signal(shared[name], counted[name])
                counted[name] += int(n) * PAIRS
            return named({name[len(prefix):]: signal for name, signal in out.items()})

        def bc(ap, axis, n):
            a = ap.unsqueeze(axis)
            shape = list(a.shape)
            shape[axis] = n
            return a.broadcast_to(shape)

        wt = {p: sb(f"w_{p}", [P, n]) for p, n in width.items() if p in STAGES}

        def w(name, rows=P):
            pack, o, n = at[name]
            return wt[pack][0:rows, o:o + n]

        x = sb("x", [P, TILES, D])
        ones = sb("ones", [P, P])
        xm = sb("xm", [P, 2, D])
        xn = sb("xn", [P, 2, D])
        stats = sb("stats", [P, 2, 6])
        minus_round = sb("minus_round", [P, 1])
        carrier = sb("carrier", [P, 1])
        mv = sb("mv", [P, 2, 2])
        vareps = sb("vareps", [P, 2, 1])
        rstd = sb("rstd", [P, 2, 1])
        minus_half = sb("minus_half", [P, 2, 1])
        xT = sb("xT", [P, TOK])
        cT = sb("cT", [P, TOK])
        vT = sb("vT", [P, TOK])
        qT = sb("qT", [P, TOK])
        keybias = sb("keybias", [P, HG])
        querybias = sb("querybias", [P, G])
        qx = sb("qx", [P, G, TOK])
        kx = sb("kx", [P, HG, TOK])
        vbd = sb("vbd", [P, PB, H // 2, 2, VW])
        rowmax = sb("rowmax", [P, G, 2, HG])
        shifted = sb("shifted", [P, G, UNIT])
        probs = sb("probs", [P, G, UNIT])
        probsT = sb("probsT", [P, 2, 4, P])
        rsum = sb("rsum", [P, 2, H])
        heads = sb("heads", [P, 2, D])
        headsT = sb("headsT", [P, TOK])

        zeros = sb("zeros", [P, 2, D])
        isnan = sb("isnan", [P, 2, D], I32)
        qh = sb("qh", [P, 3, TOK])
        biasprod = sb("biasprod", [P, H])
        biasmaps = sb("biasmaps", [P, 2, H])
        rowq, colq = biasmaps[:, 0, :], biasmaps[:, 1, :]
        rowterm = sb("rowterm", [P, 2, H])
        cmask = sb("cmask", [P, 2, UNIT])
        big = sb("big", [P, TILES * H * S])
        kept = big[:].rearrange("p (t c) -> p t c", t=TILES)
        maps = big[:, FC * B * S:FC * B * S + H * D]
        hidden = big[:, 0:FC * B * S].rearrange("p (k n) -> p k n", k=FC)
        ksum = sb("ksum", [P, PB])
        bk64 = sb("bk64", [P, 1])
        ksb = sb("ksb", [P, PB, H])
        squares = sb("squares", [P, G, UNIT])
        esums = sb("esums", [P, 2, 2, H])
        feat = sb("feat", [P, 3, 2, H])
        recipz = sb("recipz", [P, 2, H])
        feats = sb("feats", [3, PB * H])
        hid1 = sb("hid1", [P, PB * H])
        hid2 = sb("hid2", [P, PB * H])
        logt = sb("logt", [P, 2, H])
        over_t = sb("over_t", [P, 2, H])
        half_over_t = sb("half_over_t", [P, 2, H])
        tempered = wt["D"][:, 0:G * UNIT].rearrange("p (g c) -> p g c", g=G)
        silu = shifted[:].rearrange("p g (t n) -> p (g t) n", n=TOK)
        logits = sb("logits", [P, TILES, E8])
        key = sb("key", [P, TILES, E8])
        eq = sb("eq", [P, TILES, E8])
        hot1 = sb("hot1", [P, TILES, E8])
        hot2 = sb("hot2", [P, TILES, E8])
        score = sb("score", [P, TILES, E8])
        sel = sb("sel", [P, TILES, E8])
        tok1 = sb("tok1", [P, TILES])
        tally = sb("tally", [P, 2 * E8])
        total = sb("total", [P, 2 * E8])
        selp = sb("selp", [P, 2, E8])
        selT = sb("selT", [E8, TOK], BF16)
        selmat = sb("selmat", [E8, 4 * P], BF16)
        hm = [sb("hm", [P, FC, TOK]),
              probs[:].rearrange("p g (t n) -> p (g t) n", n=TOK)]
        wsum = sb("wsum", [P, 2])
        wmean = sb("wmean", [P, 2])
        wscale = sb("wscale", [P, 2])
        taps = big[:, 0:3 * HID].rearrange("p (k f) -> p k f", k=3)
        w2q = sb("w2q", [P, HC * D], BF16)
        identb = sb("identb", [P, P], BF16)
        amax = sb("amax", [P, 2])
        ainv = sb("ainv", [P, 2])
        xi = sb("xi", [P, 2, D])
        xs = qx[:, 0:3, :]
        hs = shifted[:, 2:4, :]
        hr = probs[:, 0:2, :]
        hi8 = squares[:, 0, :].bitcast(BF16).rearrange("p (t f) -> p t f", t=2)
        hT = squares[:, 1, :].bitcast(BF16).rearrange("p (t f) -> p t f", t=2)
        hmax = sb("hmax", [P, 2])
        hinv = sb("hinv", [P, 2])
        outstep = sb("outstep", [P, 2])

        psS = [ctx.enter_context(nc.psum_tensor(f"psS{i}", [P, 512], F32)) for i in range(2)]
        psT = [ctx.enter_context(nc.psum_tensor(f"psT{i}", [P, 512], F32)) for i in range(2)]
        psO = ctx.enter_context(nc.psum_tensor("psO", [P, 512], F32))
        psV = ctx.enter_context(nc.psum_tensor("psV", [P, 512], F32))
        tokensT = [xT, headsT]
        scorebank = [psS[0], psS[1], None]
        psK = ctx.enter_context(nc.psum_tensor("psK", [P, 512], F32))
        psQ = ctx.enter_context(nc.psum_tensor("psQ", [P, 512], F32))
        scorebank[2] = psQ
        hiddenbank = [psS[0], psS[1], psQ, psT[0], psT[1]]
        maskbank = [psS[0], psS[1], psT[0], psT[1]]
        downbank = [psV, psQ]
        psTb = [t[:, :].bitcast(BF16) for t in psT]
        O = psO[:, 0:2 * H * VW].rearrange("p (a h v) -> p a h v", a=2, h=H)

        load = sems("load", "first x A B C D E F out")
        loads = {"A": load.A, "B": load.B, "C": load.C, "D": load.D, "E": load.E, "F": load.F}
        init = sems("init", "pool round")
        ident = w("ident")

        def pair(t, j):
            return t[:, bass.ds(2 * j, 2), :]

        def tile_of(t, j):
            if isinstance(j, int):
                return lambda a: t[:, 2 * j + a, :]
            return lambda a: t[:, bass.ds(2 * j + a, 1), :].rearrange("p o d -> p (o d)")

        def norm_stats(dve, n, j, src, freed, count):
            for a in range(2):
                nc.vector.bn_stats(stats[:, a, :], src(a)).then_inc(n.stats.sem, 1)
            dve.wait_ge(n.stats.sem, n.stats.at(2 * j + 2))
            nc.vector.memset(carrier[:], 0.0)
            for a in range(2):
                nc.vector.bn_aggr(mv[:, a, :], stats[:, a, :]).then_inc(n.aggr.sem, 1)
            dve.wait_ge(n.aggr.sem, n.aggr.at(2 * j + 2))
            dve.wait_ge(freed.sem, freed.at(count))
            nc.vector.tensor_scalar(vareps[:], mv[:, :, 1:2], EPS, None, ALU.add).then_inc(n.vareps.sem, 1)

        def norm_rstd(pool, n, j, freed, count):
            pool.wait_ge(n.vareps.sem, n.vareps.at(j + 1))
            pool.wait_ge(freed.sem, freed.at(count))
            nc.gpsimd.tensor_tensor(rstd[:], vareps[:], minus_half[:], ALU.pow).then_inc(n.rstd.sem, 1)

        def norm_apply(dve, n, j, src, dst, freed, count):
            dve.wait_ge(n.rstd.sem, n.rstd.at(j + 1))
            dve.wait_ge(freed.sem, freed.at(count))
            for a in range(2):
                nc.vector.tensor_scalar(dst[:, a, :], src(a), mv[:, a, 0:1], rstd[:, a, :],
                                        ALU.subtract, ALU.mult).then_inc(n.normed.sem, 1)

        def norm_signals(prefix=""):
            return signals("stats:2 aggr:2 vareps:1 rstd:1 normed:2 xT_ps:1", prefix)

        def attention(st, wst=None, affine=False, cross=False, wide=False, out_proj=True, scale=DH ** -0.5,
                      queries=True, values=True, guard=False):
            n = norm_signals() if queries else None
            n0 = norm_signals("first_") if affine else None
            own = signals(f"shift:{G} exp:{G}", "" if queries else "tempered_")
            s = signals(("xT:1 rowmax:4 " + ("q_ps:16 q:16 scores:16 row_ps:1 row:1 cmask:4 " if wide else
                                                 "k_ps:1 q:4 k:4 scores:4 ")) * queries
                          + f"v_ps:1 v:2 tr:{G} pT:{G} pv:{G} recip:1 heads:1 res:1 " * values
                          + "headsT_ps:1 headsT:1 out_ps:1 " * out_proj + "ctx:16 " * cross + "vctx:16 " * (cross and values)
                          + f"masked:{G} " * wide + "nans:2 " * guard)
            s = named(dict(s._asdict(), shift=own.shift, exp=own.exp))
            projected = (s.scores, H) if wide else (s.k_ps if cross and queries else s.v_ps, 1)
            return named(dict(st=st, w=wst or st, affine=affine, cross=cross, wide=wide, out_proj=out_proj, scale=scale,
                              queries=queries, values=values, guard=guard, n=n, n0=n0, s=s, projected=projected,
                              p=probs if queries else tempered, tbank=(lambda g: g % 2) if queries and not wide else (lambda g: 0)))

        def pe_tokens_transposed(pe, a, j):
            n, s = a.n, a.s
            pe.wait_ge(n.normed.sem, n.normed.at(2 * j + 2))
            if a.wide:
                pe.wait_ge(s.q.sem, s.q.at(H * j))
            else:
                pe.wait_ge(s.k.sem, s.k.at(HG * j))
            if a is E1:
                pe.wait_ge(e.ksum.sem, e.ksum.at(j))
            for t in range(2):
                last = nc.tensor.transpose(psK[:, t * P:(t + 1) * P], xn[:, t, :], ident)
            last.then_inc(n.xT_ps.sem, 1)

        def pe_queries(pe, a, j):
            s = a.s
            pe.wait_ge(s.xT.sem, s.xT.at(j + 1))
            if a.wide:
                pe.wait_ge(s.pT.sem, s.pT.at(G * (j - 1)))
                pe.wait_ge(s.row.sem, s.row.at(j))
                for t in range(2):
                    o = psT[0][:, t * H:(t + 1) * H]
                    nc.tensor.matmul(o, xT[:, t * P:(t + 1) * P], rowq, start=True, stop=False)
                    last = nc.tensor.matmul(o, ones[:], biasprod[:], start=False, stop=True)
                last.then_inc(s.row_ps.sem, 1)
                return
            nc.tensor.matmul(psK[:, 0:TOK], w(a.w + "_wq"), xT[:], start=True, stop=True)
            if a.cross:
                pe.wait_ge(s.ctx.sem, s.ctx.at(16 * j + 16))
            nc.tensor.matmul(psK[:, TOK:2 * TOK], w(a.w + "_wk"), (cT if a.cross else xT)[:], start=True,
                             stop=True).then_inc(s.k_ps.sem, 1)

        def pe_front(pe, a, j):
            if a.queries:
                pe_tokens_transposed(pe, a, j)
                pe_queries(pe, a, j)

        def pe_value_projection(pe, a, j):
            s = a.s
            pe.wait_ge(s.v.sem, s.v.at(2 * j))
            if a.out_proj:
                pe.wait_ge(s.res.sem, s.res.at(j - 1))
            if a.cross:
                pe.wait_ge(s.vctx.sem, s.vctx.at(16 * j + 16))
            for b in range(PB):
                for e in range(2):
                    last = nc.tensor.matmul(psV[64 * e:64 * e + 64, b * 64:b * 64 + 64], (vT if a.cross else xT)[:, b * S:(b + 1) * S],
                                            w(a.w + "_wv")[:, 64 * e:64 * e + 64], start=True, stop=True)
            last.then_inc(s.v_ps.sem, 1)

        def act_tokens(act, a, j):
            n, s = a.n, a.s
            act.wait_ge(n.xT_ps.sem, n.xT_ps.at(j + 1))
            act.wait_ge(a.projected[0].sem, a.projected[0].at(a.projected[1] * j))
            if a.affine:
                nc.scalar.activation(xT[:], psK[:, 0:TOK], ACT.Identity, bias=w("beta"), scale=w("gamma")).then_inc(s.xT.sem, 1)
            else:
                nc.scalar.activation(xT[:], psK[:, 0:TOK], ACT.Copy).then_inc(s.xT.sem, 1)

        def act_queries(act, a, j, units=range(G)):
            s = a.s
            if isinstance(j, int) and j == 0:
                act.wait_ge(kb[a.st].sem, kb[a.st].at(2))
            act.wait_ge(s.k_ps.sem, s.k_ps.at(j + 1))
            for g in units:
                act.wait_ge(s.scores.sem, s.scores.at(G * j + g - 3))
                nc.scalar.activation(qx[:, g, :], psK[:, 0:TOK], ACT.Identity, bias=querybias[:, g:g + 1],
                                     scale=w("groupmask")[:, g:g + 1]).then_inc(s.q.sem, 1)

        def act_plain_queries(act, a, j):
            act.wait_ge(e.mean_ps.sem, e.mean_ps.at(j))
            nc.scalar.activation(qT[:], psK[:, 0:TOK], ACT.Identity, bias=w(a.w + "_bq")).then_inc(e.q.sem, 1)

        def act_keys(act, a, j):
            s = a.s
            act.wait_ge(s.k_ps.sem, s.k_ps.at(j + 1))
            act.wait_ge(s.scores.sem, s.scores.at(G * j))
            for h in range(HG):
                nc.scalar.activation(kx[:, h, :], psK[:, TOK:2 * TOK], ACT.Identity, bias=keybias[:, h:h + 1],
                                     scale=w("headmask")[:, h:h + 1]).then_inc(s.k.sem, 1)

        def dve_values(dve, a, j):
            s = a.s
            dve.wait_ge(s.v_ps.sem, s.v_ps.at(j + 1))
            dve.wait_ge(s.pv.sem, s.pv.at(G * j))
            v = psV[:, 0:PB * 64].rearrange("p (b q d) -> p b q d", b=PB, d=DH)
            bias = w(a.w + "_bv").rearrange("p (e q d) -> p e q d", e=2, d=DH)
            for e in range(2):
                r = slice(64 * e, 64 * e + 64)
                nc.vector.tensor_tensor(vbd[r, :, :, e, 0:DH], v[r, :, :, :], bc(bias[r, e, :, :], 1, PB),
                                        ALU.add).then_inc(s.v.sem, 1)

        def pe_scores(pe, a, j, units):
            s = a.s
            pe.wait_ge(s.q.sem, s.q.at(G * j + units[-1] + 1))
            pe.wait_ge(s.k.sem, s.k.at(HG * j + HG))
            pe.wait_ge(s.shift.sem, s.shift.at(G * j + max(units[-1] - 2, 0)))
            for g in units:
                for b in range(PB):
                    o = 64 * (b % 2)
                    last = nc.tensor.matmul(scorebank[g % 3][o:o + 64, (b // 2) * 256:(b // 2) * 256 + 256],
                                            qx[:, g, b * S:(b + 1) * S], kx[:, :, b * S:(b + 1) * S], start=True, stop=True)
                    if b == PB - 1:
                        last.then_inc(s.scores.sem, 1)

        def dve_rowmax(dve, a, j, g):
            s = a.s
            if a is E1 and g == 0:
                dve.wait_ge(e.kept.sem, e.kept.at(j))
            dve.wait_ge(s.scores.sem, s.scores.at(G * j + g + 1))
            nc.vector.tensor_reduce(rowmax[:, g, :, :].rearrange("p t h -> p (t h)"),
                                    scorebank[g % 3][:, :].rearrange("p (r m) -> p r m", m=S), AX.X, ALU.max).then_inc(s.rowmax.sem, 1)

        def dve_shift(dve, a, j, g):
            s = a.s
            dve.wait_ge(s.rowmax.sem, s.rowmax.at(G * j + g + 1))
            dve.wait_ge(s.exp.sem, s.exp.at(G * j + g - 3))
            if a is E1:
                dve.wait_ge(e_stored[g].sem, e_stored[g].at(16 * j))
            nc.vector.tensor_tensor(shifted[:, g, :].rearrange("p (r m) -> p r m", m=S),
                                    scorebank[g % 3][:, :].rearrange("p (r m) -> p r m", m=S),
                                    bc(rowmax[:, g, :, :].rearrange("p t h -> p (t h)"), 2, S), ALU.subtract).then_inc(s.shift.sem, 1)

        def act_exp(act, a, j, g):
            s = a.s
            act.wait_ge(s.shift.sem, s.shift.at(G * j + g + 1))
            if a is E2:
                nc.scalar.activation(tempered[:, g, :], tempered[:, g, :], ACT.Exp, scale=a.scale).then_inc(s.exp.sem, 1)
                return
            if a is E1:
                act.wait_ge(e.z.sem, e.z.at(G * j + g - 3))
                act.wait_ge(e.sq.sem, e.sq.at(G * j + g - 3))
            else:
                act.wait_ge(s.tr.sem, s.tr.at(G * j + g - 3))
            nc.scalar.activation(probs[:, g, :], shifted[:, g, :], ACT.Exp, scale=a.scale).then_inc(s.exp.sem, 1)

        def pe_transpose(pe, a, j, g):
            s = a.s
            pe.wait_ge(s.exp.sem, s.exp.at(G * j + g + 1))
            if a is E2:
                pe.wait_ge(s.pT.sem, s.pT.at(G * j + g))
            for k in range(4):
                last = nc.tensor.transpose(psT[a.tbank(g)][:, k * P:(k + 1) * P], a.p[:, g, k * P:(k + 1) * P], ident)
            last.then_inc(s.tr.sem, 1)

        def act_probsT(act, a, j, g):
            s = a.s
            act.wait_ge(s.tr.sem, s.tr.at(G * j + g + 1))
            nc.scalar.activation(probsT[:, g % 2, :, :].rearrange("p k n -> p (k n)"), psT[a.tbank(g)][:, :],
                                 ACT.Copy).then_inc(s.pT.sem, 1)

        def pe_values(pe, a, j, g):
            s = a.s
            if g == 0:
                pe.wait_ge(s.v.sem, s.v.at(2 * j + 2))
                pe.wait_ge(s.heads.sem, s.heads.at(j))
            pe.wait_ge(s.pT.sem, s.pT.at(G * j + g + 1))
            for t in range(2):
                for q in range(2):
                    hp = 2 * g + q
                    for b in range(2):
                        last = nc.tensor.matmul(O[64 * b:64 * b + 64, t, 2 * hp:2 * hp + 2, :],
                                                probsT[:, g % 2, 2 * t + q, 64 * b:64 * b + 64],
                                                vbd[:, 2 * t + b, hp, :, :], start=True, stop=True)
            last.then_inc(s.pv.sem, 1)

        def dve_reciprocal(dve, a, j):
            s = a.s
            dve.wait_ge(s.pv.sem, s.pv.at(G * j + G))
            nc.vector.reciprocal(rsum[:, :, :], O[:, :, :, DH]).then_inc(s.recip.sem, 1)

        def dve_heads(dve, a, j):
            s = a.s
            dve.wait_ge(s.recip.sem, s.recip.at(j + 1))
            if a.out_proj:
                dve.wait_ge(s.headsT_ps.sem, s.headsT_ps.at(j))
            for t in range(2):
                ins = nc.vector.tensor_tensor(heads[:, t, :].rearrange("p (h d) -> p h d", h=H), O[:, t, :, 0:DH],
                                              bc(rsum[:, t, :], 2, DH), ALU.mult)
            if not a.guard:
                ins.then_inc(s.heads.sem, 1)
                return
            ins.then_inc(s.nans.sem, 1)
            dve.wait_ge(s.nans.sem, s.nans.at(2 * j + 1))
            nc.vector.tensor_tensor(isnan[:], heads[:], heads[:], ALU.not_equal).then_inc(s.nans.sem, 1)
            dve.wait_ge(s.nans.sem, s.nans.at(2 * j + 2))
            nc.vector.memset(carrier[:], 0.0)
            nc.vector.copy_predicated(heads[:], isnan[:], zeros[:]).then_inc(s.heads.sem, 1)

        def pe_headsT(pe, a, j, more=True):
            s = a.s
            pe.wait_ge(s.heads.sem, s.heads.at(j + 1))
            pe.wait_ge(s.v.sem, s.v.at(2 * j + (4 if more else 2)))
            for t in range(2):
                last = nc.tensor.transpose(psV[:, TOK + t * P:TOK + (t + 1) * P], heads[:, t, :], ident)
            last.then_inc(s.headsT_ps.sem, 1)

        def pe_out(pe, a, j):
            s = a.s
            pe.wait_ge(s.headsT.sem, s.headsT.at(j + 1))
            for t in range(2):
                o = psV[:, TOK + t * D:TOK + (t + 1) * D]
                nc.tensor.matmul(o, headsT[:, t * P:(t + 1) * P], w(a.w + "_wo"), start=True, stop=False)
                last = nc.tensor.matmul(o, ones[0:1, 0:P], w(a.w + "_bo")[0:1, :], start=False, stop=True)
            last.then_inc(s.out_ps.sem, 1)

        def act_headsT(act, a, j):
            s = a.s
            act.wait_ge(s.headsT_ps.sem, s.headsT_ps.at(j + 1))
            act.wait_ge(s.out_ps.sem, s.out_ps.at(j))
            nc.scalar.activation(headsT[:], psV[:, TOK:2 * TOK], ACT.Copy).then_inc(s.headsT.sem, 1)

        def dve_residual(dve, a, j):
            s = a.s
            if a.out_proj:
                dve.wait_ge(s.out_ps.sem, s.out_ps.at(j + 1))
                add = psV[:, TOK:2 * TOK].rearrange("p (t d) -> p t d", t=2)
            else:
                dve.wait_ge(s.heads.sem, s.heads.at(j + 1))
                add = heads[:]
            nc.vector.tensor_tensor(pair(x, j), add, pair(x, j), ALU.add).then_inc(s.res.sem, 1)

        slots = [psK[:, 0:TOK], psQ[:, 0:TOK], psT[1][:, 0:TOK]]

        def maps_pe(pe):
            pe.wait_ge(loads["D"].sem, loads["D"].at(16))
            pe.wait_ge(c.hidden.sem, c.hidden.at(FC * PAIRS))
            for k in range(4):
                for h in range(4 * k, 4 * k + 4):
                    col = slice(h * D, (h + 1) * D)
                    last = nc.tensor.matmul(mapbank[k][:, (h - 4 * k) * D:(h - 4 * k + 1) * D], w("D_wqT")[:, col], w("D_wkT")[:, col],
                                            start=True, stop=True)
                last.then_inc(d.maps_ps.sem, 1)

        def bias_maps_pe(pe, n):
            pe.wait_ge(c.xT.sem, c.xT.at(PAIRS))
            for h in range(H):
                last = nc.tensor.matmul(psK[:, n * H + h:n * H + h + 1], w(("D_wqT", "D_wkT")[n])[:, h * D:(h + 1) * D],
                                        w(("D_bk", "D_bq")[n])[:, h:h + 1], start=True, stop=True)
            if n == 1:
                last.then_inc(d.maps_ps.sem, 1)

        def maps_act(act):
            for k in range(4):
                act.wait_ge(d.maps_ps.sem, d.maps_ps.at(k + 1))
                nc.scalar.activation(maps[:, k * 512:(k + 1) * 512], mapbank[k][:, :], ACT.Copy).then_inc(d.inplace.sem, 1)
            act.wait_ge(d.maps_ps.sem, d.maps_ps.at(5))
            nc.scalar.activation(biasmaps[:].rearrange("p n h -> p (n h)"), psK[:, 0:2 * H], ACT.Copy).then_inc(d.inplace.sem, 1)

        def pe_project(pe, a, j, h):
            s = a.s
            pe.wait_ge(s.q.sem, s.q.at(H * j + max(h - 2, 0)))
            nc.tensor.matmul(slots[h % 3], maps[:, h * D:(h + 1) * D], xT[:], start=True, stop=True).then_inc(s.q_ps.sem, 1)

        def pe_wide_scores(pe, a, j, g):
            s = a.s
            for h in range(HG * g, HG * g + HG):
                if h + 2 < H:
                    pe_project(pe, a, j, h + 2)
                pe.wait_ge(s.q.sem, s.q.at(H * j + h + 1))
                if h == HG * g:
                    pe.wait_ge(s.masked.sem, s.masked.at(G * j + g - 1))
                for b in range(PB):
                    o, c = 64 * (b % 2), (b // 2) * 256 + (h % HG) * S
                    last = nc.tensor.matmul(psS[g % 2][o:o + 64, c:c + S], qh[:, h % 3, b * S:(b + 1) * S],
                                            xT[:, b * S:(b + 1) * S], start=True, stop=True)
                last.then_inc(s.scores.sem, 1)

        def act_wide_queries(act, a, j, heads_):
            s = a.s
            for h in heads_:
                act.wait_ge(s.q_ps.sem, s.q_ps.at(H * j + h + 1))
                act.wait_ge(s.scores.sem, s.scores.at(H * j + h - 2))
                nc.scalar.activation(qh[:, h % 3, :], slots[h % 3], ACT.Identity, bias=colq[:, h:h + 1]).then_inc(s.q.sem, 1)

        def act_rowterm(act, a, j):
            s = a.s
            act.wait_ge(s.row_ps.sem, s.row_ps.at(j + 1))
            act.wait_ge(s.cmask.sem, s.cmask.at(G * j))
            nc.scalar.activation(rowterm[:].rearrange("p t h -> p (t h)"), psT[0][:, 0:2 * H], ACT.Copy).then_inc(s.row.sem, 1)

        def pool_cmask(pool, a, j):
            s = a.s
            pool.wait_ge(s.row.sem, s.row.at(j + 1))
            for g in range(G):
                pool.wait_ge(s.masked.sem, s.masked.at(G * j + g - 1))
                nc.gpsimd.tensor_tensor(cmask[:, g % 2, :].rearrange("p (t h m) -> p t h m", t=2, m=S),
                                        bc(bc(w("D_causal"), 1, HG), 1, 2),
                                        bc(rowterm[:, :, HG * g:HG * g + HG], 3, S), ALU.add).then_inc(s.cmask.sem, 1)

        def dve_wide_softmax(dve, a, j, g):
            s = a.s
            sh = shifted[:, g, :].rearrange("p (r m) -> p r m", m=S)
            mx = rowmax[:, g, :, :].rearrange("p t h -> p (t h)")
            dve.wait_ge(s.scores.sem, s.scores.at(H * j + HG * g + HG))
            dve.wait_ge(s.cmask.sem, s.cmask.at(G * j + g + 1))
            dve.wait_ge(s.exp.sem, s.exp.at(G * j + g - 3))
            nc.vector.tensor_tensor(shifted[:, g, :], psS[g % 2][:, :], cmask[:, g % 2, :], ALU.add).then_inc(s.masked.sem, 1)
            dve.wait_ge(s.masked.sem, s.masked.at(G * j + g + 1))
            nc.vector.tensor_reduce(mx, sh, AX.X, ALU.max).then_inc(s.rowmax.sem, 1)
            dve.wait_ge(s.rowmax.sem, s.rowmax.at(G * j + g + 1))
            nc.vector.tensor_tensor(sh, sh, bc(mx, 2, S), ALU.subtract).then_inc(s.shift.sem, 1)

        def dve_keysum(dve, a, j):
            s = a.s
            dve.wait_ge(s.k.sem, s.k.at(HG * j + HG))
            dve.wait_ge(e.q.sem, e.q.at(j + 1))
            nc.vector.tensor_reduce(ksum[:], psK[:, TOK:2 * TOK].rearrange("p (b m) -> p b m", m=S), AX.X, ALU.add).then_inc(e.ksum.sem, 1)
            dve.wait_ge(e.ksum.sem, e.ksum.at(j + 1))
            dve.wait_ge(e.mean_ps.sem, e.mean_ps.at(j))
            nc.vector.scalar_tensor_tensor(out=ksb[:], in0=bc(ksum[:], 2, H), scalar=bk64[:], in1=bc(w("E_headblk"), 1, PB),
                                           op0=ALU.add, op1=ALU.mult).then_inc(e.ksb.sem, 1)

        def pe_means(pe, a, j):
            pe.wait_ge(e.ksb.sem, e.ksb.at(j + 1))
            pe.wait_ge(e.q.sem, e.q.at(j + 1))
            pe.wait_ge(E2.s.v.sem, E2.s.v.at(2 * (j - 1)))
            for b in range(PB):
                o = 64 * (b % 2)
                last = nc.tensor.matmul(psV[o:o + 64, (b // 2) * H:(b // 2 + 1) * H], qT[:, b * S:(b + 1) * S], ksb[:, b, :],
                                        start=True, stop=True)
            last.then_inc(e.mean_ps.sem, 1)

        def dve_means(dve, a, j):
            dve.wait_ge(e.mean_ps.sem, e.mean_ps.at(j + 1))
            dve.wait_ge(e.feat_ps.sem, e.feat_ps.at(j))
            nc.vector.tensor_scalar(feat[:, 0, :, :], psV[:, 0:2 * H].rearrange("p (t h) -> p t h", h=H),
                                    1.0 / S, None, ALU.mult).then_inc(e.mean.sem, 1)

        def act_squares(act, a, j, g):
            s = a.s
            act.wait_ge(s.exp.sem, s.exp.at(G * j + g + 1))
            act.wait_ge(e.z2.sem, e.z2.at(G * j + g - 3))
            nc.scalar.activation(squares[:, g, :], probs[:, g, :], ACT.Square).then_inc(e.sq.sem, 1)

        def dve_sums(dve, a, j, g):
            s = a.s
            h4 = slice(HG * g, HG * g + HG)
            if g == 0:
                dve.wait_ge(e.var.sem, e.var.at(j))
            dve.wait_ge(s.exp.sem, s.exp.at(G * j + g + 1))
            nc.vector.tensor_reduce(esums[:, 0, :, h4], probs[:, g, :].rearrange("p (t h m) -> p t h m", t=2, m=S), AX.X,
                                    ALU.add).then_inc(e.z.sem, 1)
            dve.wait_ge(e.sq.sem, e.sq.at(G * j + g + 1))
            nc.vector.tensor_reduce(esums[:, 1, :, h4], squares[:, g, :].rearrange("p (t h m) -> p t h m", t=2, m=S), AX.X,
                                    ALU.add).then_inc(e.z2.sem, 1)

        def dve_keep(dve, a, j):
            dve.wait_ge(a.s.rowmax.sem, a.s.rowmax.at(G * j + G))
            dve.wait_ge(e.feat_ps.sem, e.feat_ps.at(j))
            nc.vector.tensor_scalar(feat[:, 1, :, :].rearrange("p t (g h) -> p t g h", h=HG),
                                    rowmax[:].rearrange("p g t h -> p t g h"), 1.0, None, ALU.mult).then_inc(e.kept.sem, 1)

        def dve_kept_softmax(dve, a, j, g):
            s = a.s
            dve.wait_ge(e_stored[g].sem, e_stored[g].at(16 * j + 16))
            dve.wait_ge(e.over_t.sem, e.over_t.at(j + 1))
            dve.wait_ge(s.tr.sem, s.tr.at(G * j + g - 3))
            nc.vector.tensor_tensor(tempered[:, g, :].rearrange("p (t h m) -> p t h m", t=2, m=S),
                                    kept[:, bass.ds(2 * j, 2), g * 256:(g + 1) * 256].rearrange("p t (h m) -> p t h m", m=S),
                                    bc(half_over_t[:, :, HG * g:HG * g + HG], 3, S), ALU.mult).then_inc(s.shift.sem, 1)

        def dve_variance(dve, j, step):
            z, z2 = esums[:, 0, :, :], esums[:, 1, :, :]
            if step == 0:
                dve.wait_ge(e.z.sem, e.z.at(G * j + G))
                nc.vector.reciprocal(recipz[:], z).then_inc(e.v.sem, 1)
            elif step < 3:
                dve.wait_ge(e.z2.sem, e.z2.at(G * j + G))
                dve.wait_ge(e.v.sem, e.v.at(3 * j + step))
                nc.vector.tensor_tensor(z2, z2, recipz[:], ALU.mult).then_inc(e.v.sem, 1)
            else:
                dve.wait_ge(e.v.sem, e.v.at(3 * j + 3))
                dve.wait_ge(e.feat_ps.sem, e.feat_ps.at(j))
                nc.vector.tensor_scalar(feat[:, 2, :, :], z2, 1.0 / S, 1.0 / (S - 1), ALU.subtract, ALU.mult).then_inc(e.var.sem, 1)

        def dve_features(dve, j):
            dve.wait_ge(e.feat_ps.sem, e.feat_ps.at(j + 1))
            dve.wait_ge(e.h_ps.sem, e.h_ps.at(2 * j))
            nc.vector.tensor_copy(feats[:], psT[1][0:3, 0:PB * H]).then_inc(e.feats.sem, 1)

        def dve_log_t(dve, j):
            dve.wait_ge(e.logt_ps.sem, e.logt_ps.at(j + 1))
            dve.wait_ge(e.inv_t.sem, e.inv_t.at(j))
            nc.vector.tensor_scalar(logt[:], psT[1][:, 0:2 * H].rearrange("p (t h) -> p t h", h=H), w("E_b3"),
                                    float(np.log(0.1)), ALU.add, ALU.max).then_inc(e.logt.sem, 1)
            dve.wait_ge(e.logt.sem, e.logt.at(j + 1))
            nc.vector.tensor_scalar(logt[:], logt[:], float(np.log(10.0)), None, ALU.min).then_inc(e.clipped.sem, 1)

        def dve_over_t(dve, j):
            dve.wait_ge(e.inv_t.sem, e.inv_t.at(j + 1))
            dve.wait_ge(E2.s.shift.sem, E2.s.shift.at(G * j))
            nc.vector.tensor_scalar(half_over_t[:], over_t[:], 0.5, None, ALU.mult).then_inc(e.over_t.sem, 1)

        def pe_features(pe, j):
            pe.wait_ge(e.var.sem, e.var.at(j + 1))
            pe.wait_ge(e.kept.sem, e.kept.at(j + 1))
            pe.wait_ge(e.mean.sem, e.mean.at(j + 1))
            pe.wait_ge(e.logt.sem, e.logt.at(j))
            for b in range(2):
                for f in range(3):
                    last = nc.tensor.matmul(psT[1][0:3, b * 2 * H:(b + 1) * 2 * H], w("E_featsel")[:, 9 * b + 3 * f:9 * b + 3 * f + 3],
                                            feat[:, f, :, :].rearrange("p t h -> p (t h)"), start=(f == 0), stop=(f == 2))
            last.then_inc(e.feat_ps.sem, 1)

        def pe_network(pe, j, layer):
            if layer == 0:
                pe.wait_ge(e.feats.sem, e.feats.at(j + 1))
                nc.tensor.matmul(psT[1][:, 0:PB * H], w("E_w1", 3), feats[:], start=True, stop=True).then_inc(e.h_ps.sem, 1)
            elif layer == 1:
                pe.wait_ge(e.h.sem, e.h.at(2 * j + 1))
                nc.tensor.matmul(psT[1][:, 0:PB * H], w("E_w2"), hid1[:], start=True, stop=True).then_inc(e.h_ps.sem, 1)
            else:
                pe.wait_ge(e.h.sem, e.h.at(2 * j + 2))
                for b in range(2):
                    last = nc.tensor.matmul(psT[1][64 * b:64 * b + 64, 0:2 * H], w("E_w3"), hid2[:, b * 2 * H:(b + 1) * 2 * H],
                                            start=True, stop=True)
                last.then_inc(e.logt_ps.sem, 1)

        def act_network(act, j, layer):
            if layer == 0:
                act.wait_ge(e.h_ps.sem, e.h_ps.at(2 * j + 1))
                nc.scalar.activation(hid1[:], psT[1][:, 0:PB * H], ACT.Gelu, bias=w("E_b1")).then_inc(e.h.sem, 1)
                return
            act.wait_ge(e.h_ps.sem, e.h_ps.at(2 * j + 2))
            act.wait_ge(e.logt_ps.sem, e.logt_ps.at(j))
            nc.scalar.activation(hid2[:], psT[1][:, 0:PB * H], ACT.Gelu, bias=w("E_b2")).then_inc(e.h.sem, 1)

        def act_inverse_t(act, j):
            act.wait_ge(e.clipped.sem, e.clipped.at(j + 1))
            act.wait_ge(e.over_t.sem, e.over_t.at(j))
            nc.scalar.activation(over_t[:], logt[:], ACT.Exp, scale=-1.0).then_inc(e.inv_t.sem, 1)

        def pe_hidden_tokens(pe, j):
            pe.wait_ge(cn.normed.sem, cn.normed.at(2 * j + 2))
            pe.wait_ge(c.xT.sem, c.xT.at(j))
            for t in range(2):
                last = nc.tensor.transpose(psK[:, t * P:(t + 1) * P], xn[:, t, :], ident)
            last.then_inc(cn.xT_ps.sem, 1)

        def pe_router(pe, j, odd):
            pe.wait_ge(c.xT.sem, c.xT.at(j + 1))
            pe.wait_ge(c.logits.sem, c.logits.at(j))
            for t in range(2):
                last = nc.tensor.matmul(psO[:, t * E8:(t + 1) * E8], tokensT[odd][:, t * P:(t + 1) * P], w("C_gate"),
                                        start=True, stop=True)
            last.then_inc(c.logits_ps.sem, 1)

        def pe_hidden(pe, j, odd, chunks):
            for k in chunks:
                pe.wait_ge(c.hidden.sem, c.hidden.at(FC * j + k + 1 - FC))
                nc.tensor.matmul(hiddenbank[k][:, 0:TOK], w("C_wg")[:, k * P:(k + 1) * P], tokensT[odd][:], start=True, stop=True)
                nc.tensor.matmul(hiddenbank[k][:, TOK:2 * TOK], w("C_wu")[:, k * P:(k + 1) * P], tokensT[odd][:], start=True,
                                 stop=True).then_inc(c.gate_up.sem, 1)

        def act_hidden_tokens(act, j, odd):
            act.wait_ge(cn.xT_ps.sem, cn.xT_ps.at(j + 1))
            act.wait_ge(c.gate_up.sem, c.gate_up.at(FC * (j - 1)))
            nc.scalar.activation(tokensT[odd][:], psK[:, 0:TOK], ACT.Copy).then_inc(c.xT.sem, 1)

        def act_hidden(act, j, chunks):
            for k in chunks:
                act.wait_ge(c.gate_up.sem, c.gate_up.at(FC * j + k + 1))
                act.wait_ge(c.hidden.sem, c.hidden.at(FC * j + k + 1 - FC))
                nc.scalar.activation(silu[:, k, :], hiddenbank[k][:, 0:TOK], ACT.Silu).then_inc(c.silu.sem, 1)

        def dve_logits(dve, j):
            dve.wait_ge(c.logits_ps.sem, c.logits_ps.at(j + 1))
            nc.vector.tensor_tensor(logits[:, bass.ds(2 * j, 2), :], psO[:, 0:2 * E8].rearrange("p (t e) -> p t e", e=E8),
                                    bc(w("C_lb"), 1, 2), ALU.add).then_inc(c.logits.sem, 1)

        def dve_hidden(dve, j, chunks):
            for k in chunks:
                dve.wait_ge(c.silu.sem, c.silu.at(FC * j + k + 1))
                nc.vector.tensor_tensor(hidden[:, k, bass.ds(j * TOK, TOK)], silu[:, k, :], hiddenbank[k][:, TOK:2 * TOK],
                                        ALU.mult).then_inc(c.hidden.sem, 1)

        def route_dve(dve):
            seq = [0]

            def then(ins):
                seq[0] += 1
                ins.then_inc(c.route.sem, 1)
                dve.wait_ge(c.route.sem, c.route.at(seq[0]))

            def best(key, one):
                then(nc.vector.tensor_reduce(tok1[:], key, AX.X, ALU.max))
                then(nc.vector.tensor_tensor(eq[:], key, bc(tok1[:], 2, E8), ALU.is_equal))
                then(nc.vector.tensor_tensor(eq[:], eq[:], bc(w("C_first"), 1, TILES), ALU.mult))
                then(nc.vector.tensor_reduce(tok1[:], eq[:], AX.X, ALU.max))
                then(nc.vector.tensor_tensor(one, eq[:], bc(tok1[:], 2, E8), ALU.is_equal))

            dve.wait_ge(c.logits.sem, c.logits.at(PAIRS))
            then(nc.vector.tensor_scalar(key[:], logits[:], 17.0, None, ALU.min))
            best(key[:], hot1[:])
            then(nc.vector.scalar_tensor_tensor(out=key[:], in0=hot1[:], scalar=-1e30, in1=key[:], op0=ALU.mult, op1=ALU.add))
            best(key[:], hot2[:])
            dve.wait_ge(c.sig.sem, c.sig.at(1))
            then(nc.vector.tensor_tensor(eq[:], hot1[:], hot2[:], ALU.add))
            nc.vector.tensor_tensor(sel[:], hot1[:], hot2[:], ALU.add).then_inc(c.sel.sem, 1)
            then(nc.vector.tensor_tensor(key[:], eq[:], score[:], ALU.mult))
            then(nc.vector.tensor_reduce(tok1[:], key[:], AX.X, ALU.add))
            then(nc.vector.tensor_scalar(tok1[:], tok1[:], 1e-8, None, ALU.add))
            then(nc.vector.reciprocal(tok1[:], tok1[:]))
            then(nc.vector.tensor_tensor(key[:], key[:], bc(tok1[:], 2, E8), ALU.mult))
            then(nc.vector.tensor_reduce(tally[:, 0:E8], eq[:].rearrange("p t e -> p e t"), AX.X, ALU.add))
            then(nc.vector.tensor_reduce(tally[:, E8:2 * E8], key[:].rearrange("p t e -> p e t"), AX.X, ALU.add))
            nc.vector.memset(carrier[:], 0.0).then_inc(c.tally.sem, 1)
            dve.wait_ge(c.total_ps.sem, c.total_ps.at(1))
            then(nc.vector.tensor_scalar(total[:, 0:E8], psO[:, 0:E8], 1.0, None, ALU.max))
            then(nc.vector.reciprocal(total[:, 0:E8], total[:, 0:E8]))
            then(nc.vector.tensor_tensor(total[:, E8:2 * E8], total[:, 0:E8], psO[:, E8:2 * E8], ALU.mult))
            means = total[:, E8:2 * E8].rearrange("p (k e) -> p e k", e=2)
            wd = w("C_wd").rearrange("p (k d) -> p k d", k=FC)
            for half in range(2):
                r = slice(64 * half, 64 * half + 64)
                then(nc.vector.tensor_tensor(wd[r, 0:4, :], wd[r, 0:4, :], bc(means[r, half, :], 2, D), ALU.mult))
            nc.vector.memset(carrier[:], 0.0).then_inc(c.wd.sem, 1)

        def route_pe(pe):
            pe.wait_ge(c.tally.sem, c.tally.at(1))
            nc.tensor.matmul(psO[:, 0:2 * E8], ones[:], tally[:], start=True, stop=True).then_inc(c.total_ps.sem, 1)

        def dve_pick(dve, j):
            dve.wait_ge(c.sel_ps.sem, c.sel_ps.at(j))
            nc.vector.tensor_scalar(selp[:], sel[:, bass.ds(2 * j, 2), :], 1.0, None, ALU.mult).then_inc(c.selp.sem, 1)

        def pe_choices(pe, j):
            pe.wait_ge(c.selp.sem, c.selp.at(j + 1))
            pe.wait_ge(c.selT.sem, c.selT.at(j))
            for t in range(2):
                last = nc.tensor.transpose(psK[0:E8, t * P:(t + 1) * P], selp[:, t, :], ident)
            last.then_inc(c.sel_ps.sem, 1)

        def pe_masks(pe, j):
            pe.wait_ge(c.selT.sem, c.selT.at(j + 1))
            for k in range(4):
                pe.wait_ge(c.masked.sem, c.masked.at(4 * j + k - 3))
                nc.tensor.matmul(maskbank[k][:, 0:TOK], selmat[:, k * P:(k + 1) * P], selT[:], start=True,
                                 stop=True).then_inc(c.mask_ps.sem, 1)

        def pe_down(pe, j, odd, t):
            if t == 0:
                pe.wait_ge(c.masked.sem, c.masked.at(4 * j + 4))
                pe.wait_ge(c.shared.sem, c.shared.at(j + 1))
                pe.wait_ge(c.res.sem, c.res.at(j - 1))
            for k in range(FC):
                last = nc.tensor.matmul(downbank[odd][:, t * D:(t + 1) * D], hm[odd][:, k, t * P:(t + 1) * P],
                                        w("C_wd")[:, k * D:(k + 1) * D], start=(k == 0), stop=(k == FC - 1))
            if t == 1:
                last.then_inc(c.down_ps.sem, 1)

        def dve_masked(dve, j, odd):
            dve.wait_ge(c.down_ps.sem, c.down_ps.at(j - 1))
            nc.vector.tensor_scalar(hm[odd][:, 4, :], hidden[:, 4, bass.ds(j * TOK, TOK)], 1.0, None, ALU.mult).then_inc(c.shared.sem, 1)
            for k in range(4):
                dve.wait_ge(c.mask_ps.sem, c.mask_ps.at(4 * j + k + 1))
                nc.vector.tensor_tensor(hm[odd][:, k, :], maskbank[k][:, 0:TOK], hidden[:, k, bass.ds(j * TOK, TOK)],
                                        ALU.mult).then_inc(c.masked.sem, 1)

        def dve_down_residual(dve, j, odd):
            dve.wait_ge(c.down_ps.sem, c.down_ps.at(j + 1))
            nc.vector.tensor_tensor(pair(x, j), downbank[odd][:, 0:TOK].rearrange("p (t d) -> p t d", t=2), pair(x, j),
                                    ALU.add).then_inc(c.res.sem, 1)

        def weight_sums_dve(dve):
            nc.vector.tensor_reduce(wsum[:, 0:1], w("F_w1"), AX.X, ALU.add, apply_absolute_value=True).then_inc(f.wsum.sem, 1)
            nc.vector.tensor_reduce(wsum[:, 1:2], w("F_w2"), AX.X, ALU.add, apply_absolute_value=True).then_inc(f.wsum.sem, 1)

        def weights_dve(dve):
            seq = [0]

            def then(ins):
                seq[0] += 1
                ins.then_inc(f.wstep.sem, 1)
                dve.wait_ge(f.wstep.sem, f.wstep.at(seq[0]))

            dve.wait_ge(f.wsum_ps.sem, f.wsum_ps.at(1))
            then(nc.vector.tensor_scalar(wmean[:], psO[:, 0:2], 1.0 / (D * HID), 1e-5, ALU.mult, ALU.max))
            then(nc.vector.reciprocal(wscale[:], wmean[:]))
            for n, name in enumerate(("F_w1", "F_w2")):
                wq = w(name)
                then(nc.vector.tensor_scalar(wq, wq, wscale[:, n:n + 1], ROUND, ALU.mult, ALU.add))
                then(nc.vector.tensor_scalar(wq, wq, ROUND, 1.0, ALU.subtract, ALU.min))
                if n == 0:
                    then(nc.vector.tensor_scalar(wq, wq, -1.0, wmean[:, 0:1], ALU.max, ALU.mult))
                else:
                    then(nc.vector.tensor_scalar(w2q[:], wq, -1.0, None, ALU.max))
            then(nc.vector.tensor_copy(identb[:], ident))

        def taps_dve(dve):
            nc.vector.tensor_tensor(taps[:], w("F_cw").rearrange("p (k f) -> p k f", k=3), bc(w("F_w1"), 1, 3), ALU.mult).then_inc(f.weights.sem, 1)

        def weights_pe(pe):
            pe.wait_ge(f.wsum.sem, f.wsum.at(2))
            nc.tensor.matmul(psO[:, 0:2], ones[:], wsum[:], start=True, stop=True).then_inc(f.wsum_ps.sem, 1)

        def dve_quantise(dve, j):
            dve.wait_ge(fn.normed.sem, fn.normed.at(2 * j + 2))
            dve.wait_ge(fn.xT_ps.sem, fn.xT_ps.at(j))
            nc.vector.tensor_reduce(amax[:], xn[:], AX.X, ALU.max, apply_absolute_value=True).then_inc(f.amax.sem, 1)
            dve.wait_ge(f.amax.sem, f.amax.at(j + 1))
            nc.vector.tensor_scalar(amax[:], amax[:], 1e-5, 1.0 / 127.0, ALU.max, ALU.mult).then_inc(f.astep.sem, 1)
            dve.wait_ge(f.astep.sem, f.astep.at(j + 1))
            nc.vector.reciprocal(ainv[:], amax[:]).then_inc(f.ainv.sem, 1)
            dve.wait_ge(f.ainv.sem, f.ainv.at(j + 1))
            for t in range(2):
                nc.vector.tensor_scalar(xi[:, t, :], xn[:, t, :], ainv[:, t:t + 1], ROUND, ALU.mult, ALU.add).then_inc(f.xi.sem, 1)
            dve.wait_ge(f.xi.sem, f.xi.at(2 * j + 2))
            nc.vector.tensor_scalar(xi[:], xi[:], ROUND + 127.0, ROUND - 128.0, ALU.min, ALU.max).then_inc(f.clip.sem, 1)
            dve.wait_ge(f.clip.sem, f.clip.at(j + 1))
            for t in range(2):
                nc.vector.tensor_scalar(xi[:, t, :], xi[:, t, :], ROUND, amax[:, t:t + 1], ALU.subtract, ALU.mult).then_inc(f.xq.sem, 1)

        def pe_tokens(pe, j):
            pe.wait_ge(f.xq.sem, f.xq.at(2 * j + 2))
            pe.wait_ge(f.xs.sem, f.xs.at(3 * j))
            for t in range(2):
                last = nc.tensor.transpose(psK[:, t * P:(t + 1) * P], xi[:, t, :], ident)
            last.then_inc(fn.xT_ps.sem, 1)

        def act_shifts(act, j):
            act.wait_ge(fn.xT_ps.sem, fn.xT_ps.at(j + 1))
            act.wait_ge(f.h_ps.sem, f.h_ps.at(2 * j))
            src = psK[:, 0:TOK].rearrange("p (b m) -> p b m", m=S)
            for k in range(3):
                dst = xs[:, k, :].rearrange("p (b m) -> p b m", m=S)
                lo, hi = max(1 - k, 0), S - max(k - 1, 0)
                nc.scalar.activation(dst[:, :, lo:hi], src[:, :, lo + k - 1:hi + k - 1], ACT.Copy).then_inc(f.xs.sem, 1)

        def pe_conv(pe, j, t):
            pe.wait_ge(f.xs.sem, f.xs.at(3 * j + 3))
            pe.wait_ge(f.silu.sem, f.silu.at(2 * j + t - 1))
            for k in range(3):
                nc.tensor.matmul(psS[t][:, :], xs[:, k, t * P:(t + 1) * P], taps[:, k, :], start=(k == 0), stop=False)
            nc.tensor.matmul(psS[t][:, :], ones[0:1, 0:P], w("F_cb")[0:1, :], start=False, stop=True).then_inc(f.h_ps.sem, 1)

        def act_silu(act, j, t):
            act.wait_ge(f.h_ps.sem, f.h_ps.at(2 * j + t + 1))
            act.wait_ge(f.hr.sem, f.hr.at(2 * j + t - 1))
            nc.scalar.activation(hs[:, t, :], psS[t][:, :], ACT.Silu).then_inc(f.silu.sem, 1)

        def dve_quantise_hidden(dve, j, t):
            n = 2 * j + t + 1
            m, r = hmax[:, t:t + 1], hinv[:, t:t + 1]
            dve.wait_ge(f.silu.sem, f.silu.at(n))
            nc.vector.tensor_reduce(m, hs[:, t, :], AX.X, ALU.max, apply_absolute_value=True).then_inc(f.hmax.sem, 1)
            dve.wait_ge(f.hmax.sem, f.hmax.at(n))
            dve.wait_ge(f.res.sem, f.res.at(n - 2))
            nc.vector.tensor_scalar(m, m, 1e-5, 1.0 / 127.0, ALU.max, ALU.mult).then_inc(f.hstep.sem, 1)
            dve.wait_ge(f.hstep.sem, f.hstep.at(n))
            nc.vector.reciprocal(r, m).then_inc(f.hinv.sem, 1)
            nc.vector.tensor_scalar(outstep[:, t:t + 1], m, wmean[:, 1:2], None, ALU.mult).then_inc(f.outstep.sem, 1)
            dve.wait_ge(f.hinv.sem, f.hinv.at(n))
            dve.wait_ge(f.hi.sem, f.hi.at(n - 2))
            nc.vector.tensor_scalar(hr[:, t, :], hs[:, t, :], r, ROUND, ALU.mult, ALU.add).then_inc(f.hr.sem, 1)
            dve.wait_ge(f.hr.sem, f.hr.at(n))
            nc.vector.tensor_scalar(hr[:, t, :], hr[:, t, :], ROUND + 127.0, ROUND - 128.0, ALU.min, ALU.max).then_inc(f.hclip.sem, 1)

        def act_integers(act, j, t):
            n = 2 * j + t + 1
            if isinstance(j, int) and j == 0 and t == 0:
                act.wait_ge(init.round.sem, init.round.at(1))
            act.wait_ge(f.hclip.sem, f.hclip.at(n))
            act.wait_ge(f.hT_ps.sem, f.hT_ps.at(n - 2))
            nc.scalar.activation(hi8[:, t, :], hr[:, t, :], ACT.Identity, bias=minus_round[:]).then_inc(f.hi.sem, 1)

        def pe_second(pe, j, t):
            n = 2 * j + t + 1
            pe.wait_ge(f.hi.sem, f.hi.at(n))
            for k in range(HC):
                last = nc.tensor.transpose(psTb[t][:, k * P:(k + 1) * P], hi8[:, t, k * P:(k + 1) * P], identb[:])
            last.then_inc(f.hT_ps.sem, 1)
            pe.wait_ge(f.hT.sem, f.hT.at(n))
            pe.wait_ge(f.res.sem, f.res.at(n - 1))
            for k in range(HC):
                last = nc.tensor.matmul(psV[:, t * D:(t + 1) * D], hT[:, t, k * P:(k + 1) * P], w2q[:, k * D:(k + 1) * D],
                                        start=(k == 0), stop=(k == HC - 1))
            last.then_inc(f.out_ps.sem, 1)

        def act_hiddenT(act, j, t):
            n = 2 * j + t + 1
            act.wait_ge(f.hT_ps.sem, f.hT_ps.at(n))
            act.wait_ge(f.out_ps.sem, f.out_ps.at(n - 2))
            nc.scalar.activation(hT[:, t, :], psTb[t][:, 0:HC * P], ACT.Copy).then_inc(f.hT.sem, 1)

        def dve_second_residual(dve, j, t):
            n = 2 * j + t + 1
            dve.wait_ge(f.out_ps.sem, f.out_ps.at(n))
            dve.wait_ge(f.outstep.sem, f.outstep.at(n))
            tile = tile_of(x, j)(t)
            nc.vector.scalar_tensor_tensor(out=tile, in0=psV[:, t * D:(t + 1) * D], scalar=outstep[:, t:t + 1], in1=tile,
                                           op0=ALU.mult, op1=ALU.add).then_inc(f.res.sem, 1)

        def dve_norm_stats(dve, a, j):
            n = a.n0 if a.affine else a.n
            norm_stats(dve, n, j, tile_of(x, j), a.n.rstd, j)

        def dve_norm_plain(dve, a, j):
            norm_apply(dve, a.n0, j, tile_of(x, j), xm, a.n.normed, 2 * j)
            dve.wait_ge(a.n0.normed.sem, a.n0.normed.at(2 * j + 2))
            norm_stats(dve, a.n, j, lambda t: xm[:, t, :], a.n0.rstd, j + 1)

        def dve_norm_apply(dve, a, j):
            norm_apply(dve, a.n, j, (lambda t: xm[:, t, :]) if a.affine else tile_of(x, j), xn, a.n.xT_ps, j)

        def dve_norm(dve, a, j):
            dve_norm_stats(dve, a, j)
            if a.affine:
                dve_norm_plain(dve, a, j)
            dve_norm_apply(dve, a, j)

        def pool_norm(pool, a, j):
            if a.affine:
                norm_rstd(pool, a.n0, j, a.n.normed, 2 * j)
                norm_rstd(pool, a.n, j, a.n0.normed, 2 * j + 2)
            else:
                norm_rstd(pool, a.n, j, a.n.normed, 2 * j)

        def sync_context(sp, a):
            def step(j):
                if a.queries:
                    sp.wait_ge(a.s.k_ps.sem, a.s.k_ps.at(j))
                    sp.dma_start(cT[:], ctx_in[:, bass.ds(j * TOK, TOK)]).then_inc(a.s.ctx.sem, 16)
                sp.wait_ge(a.s.v_ps.sem, a.s.v_ps.at(j))
                sp.dma_start(vT[:], ctx_in[:, bass.ds(j * TOK, TOK)]).then_inc(a.s.vctx.sem, 16)
            over_pairs(sp, step, PAIRS)

        def tempered_sync(sp):
            def step(i):
                if within(i, 0, PAIRS - 1):
                    sp.wait_ge(E1.s.k_ps.sem, E1.s.k_ps.at(i + 1))
                    sp.dma_start(cT[:], ctx_in[:, bass.ds((i + 1) * TOK, TOK)]).then_inc(E1.s.ctx.sem, 16)
                if within(i, 0, PAIRS):
                    sp.wait_ge(E2.s.v_ps.sem, E2.s.v_ps.at(i))
                    sp.dma_start(vT[:], ctx_in[:, bass.ds(i * TOK, TOK)]).then_inc(E2.s.vctx.sem, 16)
                    for g in range(G):
                        sp.wait_ge(E1.s.shift.sem, E1.s.shift.at(G * i + g + 1))
                        sp.dma_start(kept[:, bass.ds(2 * i, 2), g * 256:(g + 1) * 256],
                                     shifted[:, g, :].rearrange("p (t c) -> p t c", t=2)).then_inc(e_stored[g].sem, 16)

            sp.wait_ge(Bx.s.v_ps.sem, Bx.s.v_ps.at(PAIRS))
            sp.wait_ge(Bx.s.ctx.sem, Bx.s.ctx.at(16 * PAIRS))
            sp.wait_ge(Bx.s.vctx.sem, Bx.s.vctx.at(16 * PAIRS))
            sp.dma_start(cT[:], ctx_in[:, 0:TOK]).then_inc(E1.s.ctx.sem, 16)
            over_tempered(sp, step, PAIRS - 1)

        def over_pairs(eng, step, last):
            step(0)
            with eng.Fori(1, last) as i:
                step(i)

        def over_bodies(eng, step, ahead=2):
            step(0, before=False)
            with eng.Fori(1, PAIRS - ahead) as i:
                step(i)
            for i in range(PAIRS - ahead, PAIRS):
                step(i, tokens=False, scores=i < PAIRS - 1)

        def attention_pe(pe, a):
            def step(i, before=True, tokens=True, scores=True):
                before = before and a.out_proj
                queries, tokens = scores and a.queries, tokens and a.queries
                if queries:
                    pe_scores(pe, a, i + 1, (0,))
                if before:
                    pe_headsT(pe, a, i - 1)
                if queries:
                    pe_scores(pe, a, i + 1, (1,))
                pe_transpose(pe, a, i, 0)
                if before:
                    pe_out(pe, a, i - 1)
                if queries:
                    pe_scores(pe, a, i + 1, (2,))
                pe_transpose(pe, a, i, 1)
                if scores:
                    pe_value_projection(pe, a, i + 1)
                if tokens:
                    pe_tokens_transposed(pe, a, i + 2)
                pe_values(pe, a, i, 0)
                if queries:
                    pe_scores(pe, a, i + 1, (3,))
                if tokens:
                    pe_queries(pe, a, i + 2)
                pe_transpose(pe, a, i, 2)
                pe_values(pe, a, i, 1)
                pe_transpose(pe, a, i, 3)
                pe_values(pe, a, i, 2)
                pe_values(pe, a, i, 3)

            def wide_step(i, before=True, tokens=True, scores=True):
                if scores:
                    pe_project(pe, a, i + 1, 0)
                    pe_project(pe, a, i + 1, 1)
                pe.wait_ge(a.s.row.sem, a.s.row.at(i + 2 if scores else PAIRS))
                for g in range(G):
                    pe_transpose(pe, a, i, g)
                    if before and g == 1:
                        pe_out(pe, a, i - 1)
                    if scores:
                        pe_wide_scores(pe, a, i + 1, g)
                    if before and g == 0:
                        pe_headsT(pe, a, i - 1)
                    if scores and g == 2:
                        pe_value_projection(pe, a, i + 1)
                    if tokens and g == 3:
                        pe_tokens_transposed(pe, a, i + 2)
                    pe_values(pe, a, i, g)
                if tokens:
                    pe_queries(pe, a, i + 2)

            if a.wide:
                pe.wait_ge(d.biasprod.sem, d.biasprod.at(1))
            pe_front(pe, a, 0)
            if a.wide:
                pe_project(pe, a, 0, 0)
                pe_project(pe, a, 0, 1)
                for g in range(G):
                    pe_wide_scores(pe, a, 0, g)
                    if g == 0:
                        weights_pe(pe)
            elif a.queries:
                pe_scores(pe, a, 0, (0, 1, 2))
                pe_scores(pe, a, 0, (3,))
            pe_value_projection(pe, a, 0)
            pe_front(pe, a, 1)
            over_bodies(pe, wide_step if a.wide else step)
            if a.out_proj:
                pe_headsT(pe, a, PAIRS - 1, more=False)
                pe_out(pe, a, PAIRS - 1)

        def attention_act(act, a):
            def front(i):
                if a.queries:
                    act_tokens(act, a, i)
                    if a.wide:
                        act_rowterm(act, a, i)
                    else:
                        act_queries(act, a, i)
                        act_keys(act, a, i)

            def step(i, before=True, tokens=True, scores=True):
                tokens = tokens and a.queries
                if before and a.out_proj:
                    act_headsT(act, a, i - 1)
                act_probsT(act, a, i, 0)
                act_probsT(act, a, i, 1)
                if tokens:
                    act_tokens(act, a, i + 2)
                if scores:
                    act_exp(act, a, i + 1, 0)
                if tokens:
                    act_queries(act, a, i + 2, (0, 1))
                act_probsT(act, a, i, 2)
                act_probsT(act, a, i, 3)
                if tokens:
                    act_keys(act, a, i + 2)
                    act_queries(act, a, i + 2, (2, 3))
                if scores:
                    act_exp(act, a, i + 1, 1)
                    act_exp(act, a, i + 1, 2)
                    act_exp(act, a, i + 1, 3)

            def wide_step(i, before=True, tokens=True, scores=True):
                for g in range(G):
                    if scores:
                        act_wide_queries(act, a, i + 1, range(HG * g, HG * g + 2))
                    act_probsT(act, a, i, g)
                    if before and g == 1:
                        act_headsT(act, a, i - 1)
                    if scores:
                        act_wide_queries(act, a, i + 1, range(HG * g + 2, HG * g + 3))
                        if g:
                            act_exp(act, a, i + 1, g - 1)
                        act_wide_queries(act, a, i + 1, range(HG * g + 3, HG * g + HG))
                if tokens:
                    front(i + 2)
                if scores:
                    act_exp(act, a, i + 1, 3)

            if a.wide:
                act.wait_ge(d.inplace.sem, d.inplace.at(5))
            front(0)
            if a.wide:
                act_wide_queries(act, a, 0, range(0, H))
            for g in range(G):
                if g == 3:
                    front(1)
                act_exp(act, a, 0, g)
            over_bodies(act, wide_step if a.wide else step)
            if a.out_proj:
                act_headsT(act, a, PAIRS - 1)

        def bias_copies(dve, a):
            nc.vector.tensor_scalar(querybias[:], w("groupmask"), w(a.w + "_bq"), None, ALU.mult).then_inc(kb[a.st].sem, 1)
            nc.vector.tensor_scalar(keybias[:], w("headmask"), w(a.w + "_bk"), None, ALU.mult).then_inc(kb[a.st].sem, 1)

        def attention_dve(dve, a):
            def softmax(i, after_first, after_second, residual):
                if a.wide:
                    dve_wide_softmax(dve, a, i, 0)
                    after_first()
                    dve_wide_softmax(dve, a, i, 1)
                    after_second()
                    dve_wide_softmax(dve, a, i, 2)
                    dve_wide_softmax(dve, a, i, 3)
                elif a.queries:
                    dve_rowmax(dve, a, i, 0)
                    dve_rowmax(dve, a, i, 1)
                    dve_shift(dve, a, i, 0)
                    residual()
                    after_first()
                    dve_rowmax(dve, a, i, 2)
                    dve_shift(dve, a, i, 1)
                    dve_rowmax(dve, a, i, 3)
                    dve_shift(dve, a, i, 2)
                    after_second()
                    dve_shift(dve, a, i, 3)
                else:
                    dve_kept_softmax(dve, a, i, 0)
                    after_first()
                    dve_kept_softmax(dve, a, i, 1)
                    dve_kept_softmax(dve, a, i, 2)
                    dve_kept_softmax(dve, a, i, 3)

            def step(i, before=True, tokens=True, scores=True):
                tokens = tokens and a.queries

                def residual(j):
                    if before and a.out_proj:
                        dve_residual(dve, a, j)

                def after_first():
                    if tokens and a.affine:
                        dve_norm_plain(dve, a, i + 3)
                    elif tokens and a.wide:
                        dve_norm_apply(dve, a, i + 2)
                    if not a.queries:
                        residual(i - 1)

                def after_second():
                    if tokens and not a.wide:
                        dve_norm_apply(dve, a, i + 3)
                    if a.wide:
                        residual(i - 1)

                if tokens:
                    dve_norm_stats(dve, a, i + (2 if a.wide else 3))
                if scores:
                    softmax(i + 1, after_first, after_second, lambda: residual(i - 1))
                if before and not scores:
                    residual(i - 1)
                dve_reciprocal(dve, a, i)
                if scores:
                    dve_values(dve, a, i + 1)
                dve_heads(dve, a, i)
                if not a.out_proj:
                    dve_residual(dve, a, i)

            if a.wide:
                nc.vector.tensor_tensor(biasprod[:], w("D_bq"), w("D_bk"), ALU.mult).then_inc(d.biasprod.sem, 1)
            if a.st in kb:
                bias_copies(dve, a)
            if a.queries:
                dve_norm(dve, a, 0)
                if a is A:
                    dve.wait_ge(load.x.sem, load.x.at(16))
                dve_norm(dve, a, 1)
            if a is Dw:
                dve.wait_ge(loads["F"].sem, loads["F"].at(16))
                weight_sums_dve(dve)
            softmax(0, lambda: None, lambda: None, lambda: None)
            if a is Dw:
                weights_dve(dve)
            dve_values(dve, a, 0)
            if a.queries and not a.wide:
                dve_norm(dve, a, 2)
            over_bodies(dve, step, 2 if a.wide else 3)
            if a.out_proj:
                dve_residual(dve, a, PAIRS - 1)
            dve.wait_ge(a.s.res.sem, a.s.res.at(PAIRS))

        def attention_pool(pool, a):
            def step(j):
                pool_norm(pool, a, j)

            def wide_step(j):
                pool_cmask(pool, a, j)
                pool_norm(pool, a, j + 2)

            if not a.queries:
                return
            if a.wide:
                pool.wait_ge(loads["D"].sem, loads["D"].at(16))
                pool_norm(pool, a, 0)
                pool_norm(pool, a, 1)
                over_pairs(pool, wide_step, PAIRS - 2)
                pool_cmask(pool, a, PAIRS - 2)
                pool_cmask(pool, a, PAIRS - 1)
            else:
                over_pairs(pool, step, PAIRS)

        def within(i, lo, hi):
            return lo <= i < hi if isinstance(i, int) else True

        def over_tempered(eng, step, last=PAIRS - 2):
            for i in range(3):
                step(i)
            with eng.Fori(3, last) as i:
                step(i)
            for i in range(last, PAIRS + 3):
                step(i)

        def tempered_pe(pe):
            def step(i):
                first, mlp, second, output = within(i, 0, PAIRS), within(i, 1, PAIRS + 1), within(i, 2, PAIRS + 2), within(i, 3, PAIRS + 3)
                tokens = within(i, 0, PAIRS - 1)
                if first:
                    pe_scores(pe, E1, i, (0,))
                if tokens:
                    pe_tokens_transposed(pe, E1, i + 1)
                if first:
                    pe_scores(pe, E1, i, (1,))
                if second:
                    pe_network(pe, i - 2, 1)
                if output:
                    pe_headsT(pe, E2, i - 3, more=within(i, 3, PAIRS + 2))
                if first:
                    pe_scores(pe, E1, i, (2,))
                if tokens:
                    pe_queries(pe, E1, i + 1)
                if second:
                    pe_network(pe, i - 2, 2)
                if first:
                    pe_scores(pe, E1, i, (3,))
                if output:
                    pe_out(pe, E2, i - 3)
                if first:
                    pe_means(pe, E1, i)
                if mlp:
                    pe_features(pe, i - 1)
                    if first:
                        pe.wait_ge(e.mean.sem, e.mean.at(i + 1))
                    pe_value_projection(pe, E2, i - 1)
                if second:
                    pe_transpose(pe, E2, i - 2, 0)
                if second:
                    pe_transpose(pe, E2, i - 2, 1)
                    pe_values(pe, E2, i - 2, 0)
                if mlp:
                    pe_network(pe, i - 1, 0)
                if second:
                    pe_transpose(pe, E2, i - 2, 2)
                    pe_values(pe, E2, i - 2, 1)
                    pe_transpose(pe, E2, i - 2, 3)
                    pe_values(pe, E2, i - 2, 2)
                    pe_values(pe, E2, i - 2, 3)

            pe_front(pe, E1, 0)
            over_tempered(pe, step)

        def tempered_act(act):
            def step(i):
                first, mlp, second, output = within(i, 0, PAIRS), within(i, 1, PAIRS + 1), within(i, 2, PAIRS + 2), within(i, 3, PAIRS + 3)
                tokens = within(i, 0, PAIRS - 1)

                def unit(g):
                    if first:
                        act_exp(act, E1, i, g)
                        act_squares(act, E1, i, g)

                if tokens:
                    act_tokens(act, E1, i + 1)
                if second:
                    act_network(act, i - 2, 1)
                if output:
                    act_headsT(act, E2, i - 3)
                if tokens:
                    act_queries(act, E1, i + 1, (0, 1))
                unit(0)
                if second:
                    act_inverse_t(act, i - 2)
                if tokens:
                    act_queries(act, E1, i + 1, (2,))
                if second:
                    act_exp(act, E2, i - 2, 0)
                    act_exp(act, E2, i - 2, 1)
                    act_probsT(act, E2, i - 2, 0)
                unit(1)
                if tokens:
                    act_keys(act, E1, i + 1)
                if second:
                    act_probsT(act, E2, i - 2, 1)
                    act_exp(act, E2, i - 2, 2)
                unit(2)
                if tokens:
                    act_queries(act, E1, i + 1, (3,))
                    act_plain_queries(act, E1, i + 1)
                if second:
                    act_exp(act, E2, i - 2, 3)
                    act_probsT(act, E2, i - 2, 2)
                unit(3)
                if second:
                    act_probsT(act, E2, i - 2, 3)
                if mlp:
                    act_network(act, i - 1, 0)

            act_tokens(act, E1, 0)
            act_queries(act, E1, 0)
            act_plain_queries(act, E1, 0)
            act_keys(act, E1, 0)
            over_tempered(act, step)

        def tempered_dve(dve):
            def step(i):
                first, mlp, second, output = within(i, 0, PAIRS), within(i, 1, PAIRS + 1), within(i, 2, PAIRS + 2), within(i, 3, PAIRS + 3)
                norm = within(i, 0, PAIRS - 2)

                def temper(g):
                    if second:
                        dve_kept_softmax(dve, E2, i - 2, g)

                def variance(k):
                    if mlp:
                        dve_variance(dve, i - 1, k)

                variance(0)
                if first:
                    dve_rowmax(dve, E1, i, 0)
                variance(1)
                if first:
                    dve_rowmax(dve, E1, i, 1)
                variance(2)
                if first:
                    dve_shift(dve, E1, i, 0)
                variance(3)
                if first:
                    dve_rowmax(dve, E1, i, 2)
                    dve_shift(dve, E1, i, 1)
                if second:
                    dve_log_t(dve, i - 2)
                if first:
                    dve_rowmax(dve, E1, i, 3)
                    dve_means(dve, E1, i)
                if output:
                    dve_residual(dve, E2, i - 3)
                if first:
                    dve_shift(dve, E1, i, 2)
                if second:
                    dve_over_t(dve, i - 2)
                temper(0)
                temper(1)
                if first:
                    dve_shift(dve, E1, i, 3)
                    dve_sums(dve, E1, i, 0)
                temper(2)
                if mlp:
                    dve_features(dve, i - 1)
                temper(3)
                if norm:
                    dve_norm_stats(dve, E1, i + 2)
                if first:
                    dve_sums(dve, E1, i, 1)
                if norm:
                    dve_norm_apply(dve, E1, i + 2)
                if first:
                    dve_sums(dve, E1, i, 2)
                if within(i, 0, PAIRS - 1):
                    dve_keysum(dve, E1, i + 1)
                if first:
                    dve_sums(dve, E1, i, 3)
                    dve_keep(dve, E1, i)
                if second:
                    dve_reciprocal(dve, E2, i - 2)
                if mlp:
                    dve_values(dve, E2, i - 1)
                if second:
                    dve_heads(dve, E2, i - 2)

            bias_copies(dve, E1)
            dve_norm(dve, E1, 0)
            dve_norm(dve, E1, 1)
            dve_keysum(dve, E1, 0)
            over_tempered(dve, step)
            dve.wait_ge(E2.s.res.sem, E2.s.res.at(PAIRS))

        def over_twos(eng, step):
            step(0, 0)
            step(1, 1)
            with eng.Fori(1, PAIRS // 2 - 1) as i:
                step(2 * i, 0)
                step(2 * i + 1, 1)
            step(PAIRS - 2, 0)
            step(PAIRS - 1, 1, more=False)

        def experts_pe(pe):
            def hidden_step(j, odd, more=True):
                pe_router(pe, j, odd)
                pe_hidden(pe, j, odd, (0, 1))
                if more:
                    pe_hidden_tokens(pe, j + 1)
                pe_hidden(pe, j, odd, (2, 3, 4))

            def down_step(j, odd, more=True):
                if more:
                    pe_choices(pe, j + 1)
                pe_down(pe, j, odd, 0)
                if more:
                    pe_masks(pe, j + 1)
                pe_down(pe, j, odd, 1)

            pe_hidden_tokens(pe, 0)
            over_twos(pe, hidden_step)
            maps_pe(pe)
            bias_maps_pe(pe, 0)
            route_pe(pe)
            bias_maps_pe(pe, 1)
            pe.wait_ge(c.wd.sem, c.wd.at(1))
            pe.wait_ge(d.inplace.sem, d.inplace.at(5))
            pe_choices(pe, 0)
            pe_masks(pe, 0)
            over_twos(pe, down_step)

        def experts_act(act):
            def hidden_step(j, odd, more=True):
                act_hidden(act, j, (0, 1))
                if more:
                    act_hidden_tokens(act, j + 1, 1 - odd)
                act_hidden(act, j, (2, 3, 4))

            def choices_copy(j):
                act.wait_ge(c.sel_ps.sem, c.sel_ps.at(j + 1))
                act.wait_ge(c.mask_ps.sem, c.mask_ps.at(4 * j))
                nc.scalar.activation(selT[:], psK[0:E8, 0:TOK], ACT.Copy).then_inc(c.selT.sem, 1)

            act_hidden_tokens(act, 0, 0)
            over_twos(act, hidden_step)
            act.wait_ge(c.logits.sem, c.logits.at(PAIRS))
            nc.scalar.activation(score[:], logits[:], ACT.Sigmoid).then_inc(c.sig.sem, 1)
            maps_act(act)
            over_pairs(act, choices_copy, PAIRS)

        def experts_dve(dve):
            def hidden_step(j, norm=True):
                dve_logits(dve, j)
                dve_hidden(dve, j, (0, 1, 2))
                if norm:
                    dve_stage_norm(dve, cn, j + 2)
                dve_hidden(dve, j, (3, 4))

            def down_step(j, odd, more=True):
                if more:
                    dve_masked(dve, j + 1, 1 - odd)
                    if not isinstance(j, int) or j + 2 < PAIRS:
                        dve_pick(dve, j + 2)
                dve_down_residual(dve, j, odd)

            dve_stage_norm(dve, cn, 0)
            dve_stage_norm(dve, cn, 1)
            over_pairs(dve, hidden_step, PAIRS - 2)
            hidden_step(PAIRS - 2, norm=False)
            hidden_step(PAIRS - 1, norm=False)
            nc.vector.tensor_copy(selmat[:], w("C_sel", E8)).then_inc(c.selmat.sem, 1)
            dve.wait_ge(c.selmat.sem, c.selmat.at(1))
            route_dve(dve)
            dve.wait_ge(c.sel.sem, c.sel.at(1))
            dve_pick(dve, 0)
            dve_masked(dve, 0, 0)
            dve_pick(dve, 1)
            over_twos(dve, down_step)
            dve.wait_ge(c.res.sem, c.res.at(PAIRS))

        def dve_stage_norm(dve, n, j):
            norm_stats(dve, n, j, tile_of(x, j), n.rstd, j)
            norm_apply(dve, n, j, tile_of(x, j), xn, n.xT_ps, j)

        def stage_norm_pool(pool, n):
            over_pairs(pool, lambda j: norm_rstd(pool, n, j, n.normed, 2 * j), PAIRS)

        def convolved_pe(pe):
            pe.wait_ge(f.weights.sem, f.weights.at(1))

            def step(i, more=True):
                pe_conv(pe, i + 1, 0)
                pe_second(pe, i, 0)
                if more:
                    pe_tokens(pe, i + 2)
                pe_conv(pe, i + 1, 1)
                pe_second(pe, i, 1)

            pe_tokens(pe, 0)
            pe_conv(pe, 0, 0)
            pe_conv(pe, 0, 1)
            pe_tokens(pe, 1)
            over_pairs(pe, step, PAIRS - 2)
            step(PAIRS - 2, more=False)
            for t in range(2):
                pe_second(pe, PAIRS - 1, t)

        def convolved_act(act):
            def step(i, more=True):
                act_hiddenT(act, i, 0)
                act_silu(act, i + 1, 0)
                if more:
                    act_shifts(act, i + 2)
                act_hiddenT(act, i, 1)
                act_silu(act, i + 1, 1)
                act_integers(act, i + 1, 0)
                act_integers(act, i + 1, 1)

            act.wait_ge(f.edges.sem, f.edges.at(1))
            act_shifts(act, 0)
            act_shifts(act, 1)
            for t in range(2):
                act_silu(act, 0, t)
            for t in range(2):
                act_integers(act, 0, t)
            over_pairs(act, step, PAIRS - 2)
            step(PAIRS - 2, more=False)
            for t in range(2):
                act_hiddenT(act, PAIRS - 1, t)

        def convolved_dve(dve):
            taps_dve(dve)

            def front(i):
                dve_stage_norm(dve, fn, i)
                dve_quantise(dve, i)

            def step(i, norm=True):
                dve_second_residual(dve, i, 0)
                if norm:
                    front(i + 3)
                dve_quantise_hidden(dve, i + 1, 0)
                dve_second_residual(dve, i, 1)
                dve_quantise_hidden(dve, i + 1, 1)

            front(0)
            front(1)
            for t in range(2):
                dve_quantise_hidden(dve, 0, t)
            front(2)
            over_pairs(dve, step, PAIRS - 3)
            step(PAIRS - 3, norm=False)
            step(PAIRS - 2, norm=False)
            for t in range(2):
                dve_second_residual(dve, PAIRS - 1, t)

        A = attention("A", affine=True, out_proj=False)
        Bx = attention("B", cross=True)
        c, cn = sems("C", "xT logits_ps logits gate_up silu hidden sig route sel tally total_ps wd selmat sel_ps selp shared "
                          "selT mask_ps masked down_ps res"), norm_signals()
        Dw = attention("D", wide=True, scale=D ** -0.5)
        E1 = attention("E1", wst="E", cross=True, values=False, out_proj=False)
        E2 = attention("E2", wst="E", cross=True, queries=False, scale=1.0, guard=True)
        e = sems("E", "q bk64 ksum ksb mean_ps mean sq z z2 kept var feat_ps feats h_ps h logt_ps logt clipped inv_t over_t v "
                      "stored0 stored1 stored2 stored3")
        kb_sems = sems("keybias", "A B E1")
        kb = {"A": kb_sems.A, "B": kb_sems.B, "E1": kb_sems.E1}
        d = sems("D", "maps_ps inplace biasprod")
        mapbank = [psS[0], psS[1], psT[0], psT[1]]
        e_stored = [e.stored0, e.stored1, e.stored2, e.stored3]
        f, fn = sems("F", "wstep wsum wsum_ps weights edges amax astep ainv xi clip xq xs h_ps biased silu hmax hstep hinv outstep "
                          "hr hclip hi hT_ps hT out_ps res"), norm_signals()
        block = ctx.enter_context(nc.Block())

        @block.sync
        def _(sp):
            sp.dma_start(x[:, 0:2, :].rearrange("p t d -> p (t d)"), x_in[:, 0:2 * D]).then_inc(load.first.sem, 16)
            for p in STAGES:
                sp.dma_start(wt[p][:], packs_in[p]).then_inc(loads[p].sem, 16)
                if p == "A":
                    sp.dma_start(x[:, 2:TILES, :].rearrange("p t d -> p (t d)"), x_in[:, 2 * D:TILES * D]).then_inc(load.x.sem, 16)
            sync_context(sp, Bx)
            tempered_sync(sp)
            sp.wait_ge(f.res.sem, f.res.at(TILES - 2))
            sp.dma_start(out[:, 0:(TILES - 2) * D], x[:, 0:TILES - 2, :].rearrange("p t d -> p (t d)")).then_inc(load.out.sem, 16)
            sp.wait_ge(f.res.sem, f.res.at(TILES))
            sp.dma_start(out[:, (TILES - 2) * D:TILES * D],
                         x[:, TILES - 2:TILES, :].rearrange("p t d -> p (t d)")).then_inc(load.out.sem, 16)
            sp.wait_ge(load.out.sem, load.out.at(32))

        @block.gpsimd
        def _(pool):
            nc.gpsimd.memset(minus_round[:], -ROUND).then_inc(init.round.sem, 1)
            nc.gpsimd.memset(minus_half[:], -0.5).then_inc(init.pool.sem, 1)
            nc.gpsimd.memset(ones[:], 1.0).then_inc(init.pool.sem, 1)
            nc.gpsimd.memset(zeros[:], 0.0).then_inc(init.pool.sem, 1)
            nc.gpsimd.memset(vbd[:], 0.0).then_inc(init.pool.sem, 1)
            pool.wait_ge(init.pool.sem, init.pool.at(4))
            nc.gpsimd.memset(vbd[0:64, :, :, 0, DH], 1.0).then_inc(init.pool.sem, 1)
            nc.gpsimd.memset(vbd[64:128, :, :, 1, DH], 1.0).then_inc(init.pool.sem, 1)
            for a, p in ((A, "A"), (Bx, "B"), (None, "C"), (Dw, "D"), (E1, "E"), (None, "F")):
                if p not in STAGES:
                    continue
                if a:
                    attention_pool(pool, a)
                elif p == "C":
                    stage_norm_pool(pool, cn)
                else:
                    pool.wait_ge(E1.s.scores.sem, E1.s.scores.at(G * PAIRS))
                    nc.gpsimd.memset(xs, 0.0).then_inc(f.edges.sem, 1)
                    stage_norm_pool(pool, fn)

        @block.scalar
        def _(act):
            for p in STAGES:
                act.wait_ge(loads[p].sem, loads[p].at(16))
                if p == "A":
                    attention_act(act, A)
                elif p == "B":
                    attention_act(act, Bx)
                elif p == "C":
                    experts_act(act)
                elif p == "D":
                    attention_act(act, Dw)
                elif p == "E":
                    tempered_act(act)
                else:
                    convolved_act(act)

        @block.vector
        def _(dve):
            dve.wait_ge(load.first.sem, load.first.at(16))
            dve.wait_ge(init.pool.sem, init.pool.at(6))
            for p in STAGES:
                dve.wait_ge(loads[p].sem, loads[p].at(16))
                if p == "A":
                    attention_dve(dve, A)
                elif p == "B":
                    attention_dve(dve, Bx)
                elif p == "C":
                    experts_dve(dve)
                elif p == "D":
                    attention_dve(dve, Dw)
                elif p == "E":
                    nc.vector.tensor_scalar(bk64[:], w("E_bk"), float(S), None, ALU.mult).then_inc(e.bk64.sem, 1)
                    dve.wait_ge(e.bk64.sem, e.bk64.at(1))
                    tempered_dve(dve)
                else:
                    convolved_dve(dve)

        @block.tensor
        def _(pe):
            pe.wait_ge(init.pool.sem, init.pool.at(6))
            for p in STAGES:
                pe.wait_ge(loads[p].sem, loads[p].at(16))
                if p == "A":
                    attention_pe(pe, A)
                elif p == "B":
                    attention_pe(pe, Bx)
                elif p == "C":
                    experts_pe(pe)
                elif p == "D":
                    attention_pe(pe, Dw)
                elif p == "E":
                    tempered_pe(pe)
                else:
                    convolved_pe(pe)


_INS = ["x", "ctx_1024"]


def layouts(i):
    f = np.float32

    def rows(a, n=P):
        a = np.asarray(a)
        return np.concatenate([a, np.zeros((n - a.shape[0], a.shape[1]), a.dtype)]) if a.shape[0] < n else a

    def col(v):
        return rows(np.asarray(v).reshape(-1, 1))

    def square(a):
        return rows(rows(np.asarray(a)).T).T

    def over(v):
        v = np.asarray(v).reshape(1, -1)
        return np.repeat(v, P, axis=0)

    def even_odd(a):
        a = np.asarray(a)
        return a.reshape(-1, H // 2, 2, DH).transpose(0, 2, 1, 3).reshape(-1, D)

    r = np.arange(P)
    qkv, bqkv = np.asarray(i["L0_attn_w_qkv"]), np.asarray(i["L0_attn_b_qkv"])
    c = {
        "ident": np.eye(P, dtype=f),
        "headmask": (r[:, None] % 32 // DH == np.arange(HG)[None, :]).astype(f),
        "groupmask": (r[:, None] // 32 == np.arange(G)[None, :]).astype(f),
        "A_wq": qkv[0:D].T, "A_wk": qkv[D:2 * D].T, "A_wv": even_odd(qkv[2 * D:].T),
        "A_bq": col(bqkv[0:D]), "A_bk": col(bqkv[D:2 * D]), "A_bv": over(even_odd(bqkv[2 * D:])),
        "gamma": col(i["L0_attn_ln_gamma"]), "beta": col(i["L0_attn_ln_beta"]),
    }

    def grouped(a):
        a = np.asarray(a)
        a = a.reshape(4, 1, DH, *a.shape[1:])
        return np.repeat(a, 4, axis=1).reshape(P, *a.shape[3:])

    c.update({
        "B_wq": np.asarray(i["L0_xattn_w_q"]).T, "B_wk": grouped(i["L0_xattn_w_k"]).T, "B_wv": even_odd(grouped(i["L0_xattn_w_v"]).T),
        "B_bq": col(i["L0_xattn_b_q"]), "B_bk": col(grouped(i["L0_xattn_b_k"])), "B_bv": over(even_odd(grouped(i["L0_xattn_b_v"]))),
        "B_wo": np.asarray(i["L0_xattn_w_o"]).T, "B_bo": over(i["L0_xattn_b_o"]),
    })
    def experts(a):
        return np.asarray(a).reshape(E8 * FI, D).T

    lw = np.arange(4)
    c.update({
        "C_gate": i["L0_ffn_gate_w"].T, "C_lb": over(i["L0_ffn_lb_bias"]),
        "C_wg": np.concatenate([experts(i["L0_ffn_expert_gate_w"]), i["L0_ffn_shared_gate_w"].T], axis=1),
        "C_wu": np.concatenate([experts(i["L0_ffn_expert_up_w"]), i["L0_ffn_shared_up_w"].T], axis=1),
        "C_wd": np.concatenate([i["L0_ffn_expert_down_w"].transpose(0, 2, 1).reshape(4, P, D).transpose(1, 0, 2).reshape(P, 4 * D),
                                i["L0_ffn_shared_down_w"].T], axis=1),
        "C_first": over(np.arange(E8, 0, -1).astype(f)),
        "C_sel": rows((np.arange(E8)[:, None, None] == 2 * lw[None, :, None] + (r // 64)[None, None, :]).astype(f).reshape(E8, 4 * P)),
    })
    kqv, bkqv = i["L1_attn_Wkqv"], i["L1_attn_bkqv"]
    c.update({
        "D_wkT": kqv[:, :, 0:D].transpose(2, 0, 1).reshape(D, H * D), "D_wqT": kqv[:, :, D:2 * D].transpose(2, 0, 1).reshape(D, H * D),
        "D_wv": even_odd(kqv[:, :, 2 * D:].transpose(1, 0, 2).reshape(D, D)),
        "D_bk": bkqv[:, 0:D].T, "D_bq": bkqv[:, D:2 * D].T, "D_bv": over(even_odd(bkqv[:, 2 * D:].reshape(1, D))),
        "D_wo": i["L1_attn_Wp"], "D_bo": over(i["L1_attn_bp"]),
        "D_causal": np.where(np.arange(S)[None, :] <= (r % S)[:, None], 0.0, -1e30).astype(f),
    })
    featsel = np.zeros((P, 2, 3, 3), f)
    for b in range(2):
        for n, v in enumerate((1 / S / DH ** 0.5, 1 / S / DH ** 0.5, 1 / S)):
            featsel[64 * b:64 * b + 64, b, n, n] = v
    c.update({
        "E_wq": i["L1_xattn_Wq"].T, "E_wk": i["L1_xattn_Wk"].T, "E_wv": even_odd(i["L1_xattn_Wv"].T),
        "E_bq": col(i["L1_xattn_bq"]), "E_bk": col(i["L1_xattn_bk"]), "E_bv": over(even_odd(i["L1_xattn_bv"])),
        "E_wo": i["L1_xattn_Wo"].T, "E_bo": over(i["L1_xattn_bo"]),
        "E_w1": square(i["L1_xattn_w1"].T), "E_b1": col(i["L1_xattn_b1"]), "E_w2": square(i["L1_xattn_w2"].T),
        "E_b2": col(i["L1_xattn_b2"]), "E_w3": rows(np.repeat(i["L1_xattn_w3"].T, 64, axis=1)), "E_b3": over(i["L1_xattn_b3"]),
        "E_headblk": (r[:, None] // DH == np.arange(H)[None, :]).astype(f), "E_featsel": featsel.reshape(P, 18),
        "F_w1": i["L1_ffn_w1"].T, "F_cw": over(i["L1_ffn_conv_w"][:, 0, :].T), "F_cb": over(i["L1_ffn_conv_b"]),
        "F_w2": i["L1_ffn_w2"].T.reshape(HC, P, D).transpose(1, 0, 2).reshape(P, HC * D),
    })
    return c


def kernel(**inputs):
    import concourse.bacc as bacc
    from concourse.bass_utils import run_bass_kernel_spmd

    nc = bacc.Bacc("TRN2", target_bir_lowering=False, num_devices=1)
    i = {k: np.asarray(v) for k, v in inputs.items()}
    c = layouts(i)
    arrays = {
        "x_tiles": np.ascontiguousarray(i["x"].reshape(TILES, P, D).transpose(1, 0, 2).reshape(P, TILES * D)),
        "ctx_T": np.ascontiguousarray(i["ctx_1024"].reshape(B * S, D).T),
    }
    for pack, parts in PACKS.items():
        if pack in STAGES:
            arrays["weights_" + pack] = np.ascontiguousarray(np.concatenate([c[n] for n, _ in parts], axis=1))
    dram = {n: nc.dram_tensor(n, a.shape, mybir.dt.from_np(a.dtype), kind="ExternalInput").ap() for n, a in arrays.items()}
    out = nc.dram_tensor("out_tiles", (P, TILES * D), F32, kind="ExternalOutput").ap()
    build(nc, dram["x_tiles"], dram["ctx_T"], {p: dram["weights_" + p] for p in PACKS if p in STAGES}, out)
    r = run_bass_kernel_spmd(nc, [arrays], core_ids=[0])
    got = r.results[0]["out_tiles"]
    return got.reshape(P, TILES, D).transpose(1, 0, 2).reshape(B, S, D)
```
